# Optimizing a Trainium2 kernel written in Bass

```python
import numpy as np
import jax
import jax.numpy as jnp

def _softmax(x, axis=-1):
    return jax.nn.softmax(x, axis=axis)

def _gelu(x):
    return jax.nn.gelu(x, approximate=True)

def _silu(x):
    return jax.nn.silu(x)

def _sigmoid(x):
    return jax.nn.sigmoid(x)

def _layernorm(x, axis=-1, eps=1e-05):
    m = jnp.mean(x, axis=axis, keepdims=True)
    v = jnp.var(x, axis=axis, keepdims=True)
    return (x - m) / jnp.sqrt(v + eps)

def _scatter_add(tgt, idx, src, axis=0):
    return tgt.at[idx].add(src)

def _segment_sum(src, seg, n):
    return jax.ops.segment_sum(src, seg, n)
kernel_name = 'mk_conv_attn_hybrid_d2_conv_nchw256_r4_69fc8e'

def setup_inputs(seed: int=0):
    np.random.seed(seed)
    _w = jnp.asarray

    def _rec_inputs():
        import jax
        import jax.numpy as jnp
        _gk = jax.random.key(seed)
        x = 7.22e-05 + 1 * jax.random.normal(jax.random.fold_in(_gk, 1), (32, 64, 16, 16), jnp.float32)
        return x
    x = _rec_inputs()

    def _L0_conv_setup():
        import jax, jax.numpy as jnp
        import numpy as np
        IN_F = 64
        OUT_F = 64
        K = 3
        STRIDE = 1
        PAD = K // 2
        SEARCH_SPACE = [2, 4, 8, 16]
        BATCH = 32
        FEAT = 16

        def trans_to_cir(weight, alphas):
            a = jax.nn.softmax(alphas)
            w_total = a[0] * weight
            for idx, bs in enumerate(SEARCH_SPACE):
                q = OUT_F // bs
                p = IN_F // bs
                tmp = weight.reshape(q, bs, p, bs, K, K).transpose(0, 2, 1, 3, 4, 5)
                r = jnp.arange(bs)
                cols = (r[:, None] + r[None, :]) % bs
                gathered = tmp[:, :, r[:, None], cols]
                compress = jnp.mean(gathered, axis=2)
                circ = compress[:, :, (r[:, None] - r[None, :]) % bs]
                w = circ.transpose(0, 2, 1, 3, 4, 5).reshape(OUT_F, IN_F, K, K)
                w_total = w_total + a[idx + 1] * w
            return w_total
        key = jax.random.key(seed)
        k1, k2 = jax.random.split(key)
        x = jax.random.normal(k1, (BATCH, IN_F, FEAT, FEAT), dtype=jnp.float32)
        fan_in = IN_F * K * K
        bound = float(np.sqrt(6.0 / fan_in))
        weight = jax.random.uniform(k2, (OUT_F, IN_F, K, K), dtype=jnp.float32, minval=-bound, maxval=bound)
        alphas = jnp.ones((len(SEARCH_SPACE) + 1,), dtype=jnp.float32)
        return {'x': x, 'weight': weight, 'alphas': alphas}
    _L0_conv_all = _L0_conv_setup()
    _L0_conv_in = {k: v for k, v in _L0_conv_all.items() if k in ('weight', 'alphas')}
    del _L0_conv_all

    def _L1_attn_setup():
        import jax, jax.numpy as jnp
        import numpy as np
        import math
        HIDDEN = 64
        NUM_HEADS = 8
        HEAD_DIM = HIDDEN // NUM_HEADS
        SCALE = math.sqrt(HEAD_DIM)
        B, N, E = (1, 5000, 80000)
        key = jax.random.key(seed)
        kq, kk, kv, ke = jax.random.split(key, 4)
        q = jax.random.normal(kq, (B, N, HIDDEN), dtype=jnp.float32)
        k = jax.random.normal(kk, (B, N, HIDDEN), dtype=jnp.float32)
        v = jax.random.normal(kv, (B, N, HIDDEN), dtype=jnp.float32)
        edge_index = jax.random.randint(ke, (2, E), 0, N, dtype=jnp.int64)
        return {'q': q, 'k': k, 'v': v, 'edge_index': edge_index}
    _L1_attn_all = _L1_attn_setup()
    _L1_attn_in = {k: v for k, v in _L1_attn_all.items() if k in ('k', 'v', 'edge_index')}
    del _L1_attn_all

    def _L1_ffn_setup():
        import jax, jax.numpy as jnp
        import numpy as np
        B, N, D = (16, 1024, 64)
        NUM_EXPERTS, TOP_K, HEADS = (4, 2, 4)
        N_EDGES = 262144
        LN_EPS = 1e-05

        def _layernorm(x, g, b):
            mu = x.mean(-1, keepdims=True)
            var = ((x - mu) ** 2).mean(-1, keepdims=True)
            return (x - mu) * jax.lax.rsqrt(var + LN_EPS) * g + b

        def _forward(x, edge_index, W_gat, att_src, att_dst, b_gat, ln_gamma, ln_beta, W1, b1, W2, b2):
            Bc, Nc, Dc = x.shape
            M = Bc * Nc
            x_flat = x.reshape(M, Dc)
            h = (x_flat @ W_gat).reshape(M, HEADS, NUM_EXPERTS)
            loops = jnp.arange(M, dtype=edge_index.dtype)
            src = jnp.concatenate([edge_index[0], loops])
            dst = jnp.concatenate([edge_index[1], loops])
            a_src = (h * att_src).sum(-1)
            a_dst = (h * att_dst).sum(-1)
            e = jax.nn.leaky_relu(a_src[src] + a_dst[dst], negative_slope=0.2)
            e_max = jax.ops.segment_max(e, dst, num_segments=M)
            ee = jnp.exp(e - e_max[dst])
            denom = jax.ops.segment_sum(ee, dst, num_segments=M)
            alpha = ee / (denom[dst] + 1e-16)
            msg = h[src] * alpha[:, :, None]
            agg = jax.ops.segment_sum(msg, dst, num_segments=M).reshape(M, HEADS * NUM_EXPERTS) + b_gat
            scores = _layernorm(agg, ln_gamma, ln_beta).reshape(M, HEADS, NUM_EXPERTS).mean(1)
            scores = scores.reshape(Bc, Nc, NUM_EXPERTS)
            topk_s, topk_i = jax.lax.top_k(scores, TOP_K)
            w = jax.nn.softmax(topk_s, axis=-1)
            out = jnp.zeros_like(x)
            for ei in range(NUM_EXPERTS):
                g = jnp.where(topk_i == ei, w, 0.0).sum(-1)
                hh = jax.nn.gelu(x @ W1[ei] + b1[ei], approximate=False)
                out = out + g[..., None] * (hh @ W2[ei] + b2[ei])
            return out
        key = jax.random.key(seed)
        ks = jax.random.split(key, 8)
        s = 0.05
        return {'x': jax.random.normal(ks[0], (B, N, D), jnp.float32), 'W_gat': jax.random.normal(ks[1], (D, HEADS * NUM_EXPERTS), jnp.float32) * s, 'att_src': jax.random.normal(ks[2], (HEADS, NUM_EXPERTS), jnp.float32) * s, 'att_dst': jax.random.normal(ks[3], (HEADS, NUM_EXPERTS), jnp.float32) * s, 'b_gat': jnp.zeros((HEADS * NUM_EXPERTS,), jnp.float32), 'ln_gamma': jnp.ones((HEADS * NUM_EXPERTS,), jnp.float32), 'ln_beta': jnp.zeros((HEADS * NUM_EXPERTS,), jnp.float32), 'W1': jax.random.normal(ks[4], (NUM_EXPERTS, D, 2 * D), jnp.float32) * s, 'b1': jnp.zeros((NUM_EXPERTS, 2 * D), jnp.float32), 'W2': jax.random.normal(ks[5], (NUM_EXPERTS, 2 * D, D), jnp.float32) * s, 'b2': jnp.zeros((NUM_EXPERTS, D), jnp.float32), 'edge_index': jax.random.randint(ks[6], (2, N_EDGES), 0, B * N, jnp.int32)}
    _L1_ffn_all = _L1_ffn_setup()
    _L1_ffn_in = {k: v for k, v in _L1_ffn_all.items() if k in ('W_gat', 'att_src', 'att_dst', 'b_gat', 'ln_gamma', 'ln_beta', 'W1', 'b1', 'W2', 'b2', 'edge_index')}
    del _L1_ffn_all
    return {'x': x, 'L0_conv_weight': _L0_conv_in['weight'], 'L0_conv_alphas': _L0_conv_in['alphas'], 'L1_attn_k': _L1_attn_in['k'], 'L1_attn_v': _L1_attn_in['v'], 'L1_attn_edge_index': _L1_attn_in['edge_index'], 'L1_ffn_W_gat': _L1_ffn_in['W_gat'], 'L1_ffn_att_src': _L1_ffn_in['att_src'], 'L1_ffn_att_dst': _L1_ffn_in['att_dst'], 'L1_ffn_b_gat': _L1_ffn_in['b_gat'], 'L1_ffn_ln_gamma': _L1_ffn_in['ln_gamma'], 'L1_ffn_ln_beta': _L1_ffn_in['ln_beta'], 'L1_ffn_W1': _L1_ffn_in['W1'], 'L1_ffn_b1': _L1_ffn_in['b1'], 'L1_ffn_W2': _L1_ffn_in['W2'], 'L1_ffn_b2': _L1_ffn_in['b2'], 'L1_ffn_edge_index': _L1_ffn_in['edge_index']}

def reference(x, L0_conv_weight, L0_conv_alphas, L1_attn_k, L1_attn_v, L1_attn_edge_index, L1_ffn_W_gat, L1_ffn_att_src, L1_ffn_att_dst, L1_ffn_b_gat, L1_ffn_ln_gamma, L1_ffn_ln_beta, L1_ffn_W1, L1_ffn_b1, L1_ffn_W2, L1_ffn_b2, L1_ffn_edge_index):
    import jax
    import jax.numpy as jnp

    def _L0_conv_ref(x, weight, alphas):
        import jax, jax.numpy as jnp
        import numpy as np
        IN_F = 64
        OUT_F = 64
        K = 3
        STRIDE = 1
        PAD = K // 2
        SEARCH_SPACE = [2, 4, 8, 16]
        BATCH = 32
        FEAT = 16

        def trans_to_cir(weight, alphas):
            a = jax.nn.softmax(alphas)
            w_total = a[0] * weight
            for idx, bs in enumerate(SEARCH_SPACE):
                q = OUT_F // bs
                p = IN_F // bs
                tmp = weight.reshape(q, bs, p, bs, K, K).transpose(0, 2, 1, 3, 4, 5)
                r = jnp.arange(bs)
                cols = (r[:, None] + r[None, :]) % bs
                gathered = tmp[:, :, r[:, None], cols]
                compress = jnp.mean(gathered, axis=2)
                circ = compress[:, :, (r[:, None] - r[None, :]) % bs]
                w = circ.transpose(0, 2, 1, 3, 4, 5).reshape(OUT_F, IN_F, K, K)
                w_total = w_total + a[idx + 1] * w
            return w_total
        w = trans_to_cir(weight, alphas)
        out = jax.lax.conv_general_dilated(x, w, window_strides=(STRIDE, STRIDE), padding=((PAD, PAD), (PAD, PAD)), dimension_numbers=('NCHW', 'OIHW', 'NCHW'))
        return out

    def _L1_attn_ref(q, k, v, edge_index):
        import jax, jax.numpy as jnp
        import numpy as np
        import math
        HIDDEN = 64
        NUM_HEADS = 8
        HEAD_DIM = HIDDEN // NUM_HEADS
        SCALE = math.sqrt(HEAD_DIM)
        B, N, E = (1, 5000, 80000)
        batch_size, node_num = (q.shape[0], q.shape[1])
        qf = q.reshape(-1, NUM_HEADS, HEAD_DIM)
        kf = k.reshape(-1, NUM_HEADS, HEAD_DIM)
        vf = v.reshape(-1, NUM_HEADS, HEAD_DIM)
        src_idx = edge_index[0]
        dst_idx = edge_index[1]
        src = kf[src_idx]
        dest = qf[dst_idx]
        score = jnp.clip(jnp.sum(src * dest, axis=-1, keepdims=True) / SCALE, -5.0, 5.0)
        score = jnp.exp(score)
        msg = vf[src_idx] * score
        num_seg = qf.shape[0]
        wV = jax.ops.segment_sum(msg, dst_idx, num_segments=num_seg)
        Z = jax.ops.segment_sum(score, dst_idx, num_segments=num_seg)
        x = wV / (Z + 1e-06)
        return x.reshape(batch_size, node_num, -1)

    def _L1_ffn_ref(x, W_gat, att_src, att_dst, b_gat, ln_gamma, ln_beta, W1, b1, W2, b2, edge_index):
        import jax, jax.numpy as jnp
        import numpy as np
        B, N, D = (16, 1024, 64)
        NUM_EXPERTS, TOP_K, HEADS = (4, 2, 4)
        N_EDGES = 262144
        LN_EPS = 1e-05

        def _layernorm(x, g, b):
            mu = x.mean(-1, keepdims=True)
            var = ((x - mu) ** 2).mean(-1, keepdims=True)
            return (x - mu) * jax.lax.rsqrt(var + LN_EPS) * g + b

        def _forward(x, edge_index, W_gat, att_src, att_dst, b_gat, ln_gamma, ln_beta, W1, b1, W2, b2):
            Bc, Nc, Dc = x.shape
            M = Bc * Nc
            x_flat = x.reshape(M, Dc)
            h = (x_flat @ W_gat).reshape(M, HEADS, NUM_EXPERTS)
            loops = jnp.arange(M, dtype=edge_index.dtype)
            src = jnp.concatenate([edge_index[0], loops])
            dst = jnp.concatenate([edge_index[1], loops])
            a_src = (h * att_src).sum(-1)
            a_dst = (h * att_dst).sum(-1)
            e = jax.nn.leaky_relu(a_src[src] + a_dst[dst], negative_slope=0.2)
            e_max = jax.ops.segment_max(e, dst, num_segments=M)
            ee = jnp.exp(e - e_max[dst])
            denom = jax.ops.segment_sum(ee, dst, num_segments=M)
            alpha = ee / (denom[dst] + 1e-16)
            msg = h[src] * alpha[:, :, None]
            agg = jax.ops.segment_sum(msg, dst, num_segments=M).reshape(M, HEADS * NUM_EXPERTS) + b_gat
            scores = _layernorm(agg, ln_gamma, ln_beta).reshape(M, HEADS, NUM_EXPERTS).mean(1)
            scores = scores.reshape(Bc, Nc, NUM_EXPERTS)
            topk_s, topk_i = jax.lax.top_k(scores, TOP_K)
            w = jax.nn.softmax(topk_s, axis=-1)
            out = jnp.zeros_like(x)
            for ei in range(NUM_EXPERTS):
                g = jnp.where(topk_i == ei, w, 0.0).sum(-1)
                hh = jax.nn.gelu(x @ W1[ei] + b1[ei], approximate=False)
                out = out + g[..., None] * (hh @ W2[ei] + b2[ei])
            return out
        return _forward(x, edge_index, W_gat, att_src, att_dst, b_gat, ln_gamma, ln_beta, W1, b1, W2, b2)

    def _gn(v, G=32, eps=1e-05):
        B_, C_, H_, W_ = v.shape
        g = v.reshape(B_, G, C_ // G, H_, W_)
        m = jnp.mean(g, axis=(2, 3, 4), keepdims=True)
        s = jnp.var(g, axis=(2, 3, 4), keepdims=True)
        return ((g - m) / jnp.sqrt(s + eps)).reshape(v.shape)

    def _ln_c(v, eps=1e-06):
        m = jnp.mean(v, axis=1, keepdims=True)
        s = jnp.var(v, axis=1, keepdims=True)
        return (v - m) / jnp.sqrt(s + eps)

    def _ln_t(v, eps=1e-05):
        m = jnp.mean(v, axis=-1, keepdims=True)
        s = jnp.var(v, axis=-1, keepdims=True)
        return (v - m) / jnp.sqrt(s + eps)

    def _to_tokens(v):
        B_, C_, H_, W_ = v.shape
        return v.reshape(B_, C_, H_ * W_).transpose(0, 2, 1)

    def _from_tokens(t, like):
        B_, C_, H_, W_ = like.shape
        return t.transpose(0, 2, 1).reshape(B_, C_, H_, W_)
    x = x + _L0_conv_ref(_gn(x), L0_conv_weight, L0_conv_alphas)
    t = _to_tokens(x)
    t = t + _L1_attn_ref(_ln_t(t), L1_attn_k, L1_attn_v, L1_attn_edge_index)
    t = t + _L1_ffn_ref(_ln_t(t), L1_ffn_W_gat, L1_ffn_att_src, L1_ffn_att_dst, L1_ffn_b_gat, L1_ffn_ln_gamma, L1_ffn_ln_beta, L1_ffn_W1, L1_ffn_b1, L1_ffn_W2, L1_ffn_b2, L1_ffn_edge_index)
    x = _from_tokens(t, x)
    return x

_drawn_inputs = setup_inputs


def setup_inputs(seed=0):
    import zlib

    import numpy as np

    out = dict(_drawn_inputs(seed))
    spreads = {'L0_conv_alphas': (1.0, 0.2),
     'L1_ffn_b_gat': (0.0, 0.1),
     'L1_ffn_ln_gamma': (1.0, 0.6),
     'L1_ffn_ln_beta': (0.0, 0.727),
     'L1_ffn_b1': (0.0, 0.359),
     'L1_ffn_b2': (0.0, 0.1)}
    factors = {'L1_ffn_att_src': 26.409, 'L1_ffn_att_dst': 53.986}
    for name, (base, spread) in spreads.items():
        noise = np.random.default_rng([zlib.crc32(name.encode()), seed]).standard_normal(out[name].shape)
        drawn = base * np.exp(spread * noise) if base else spread * noise
        out[name] = jnp.asarray(drawn.astype(out[name].dtype))
    for name, factor in factors.items():
        out[name] = (out[name] * factor).astype(out[name].dtype)
    return out
```

```python
from contextlib import ExitStack

import numpy as np

import concourse.bass as bass
from concourse import mybir

F32 = mybir.dt.float32
BF16 = mybir.dt.bfloat16
I32 = mybir.dt.int32
ALU = mybir.AluOpType
ACT = mybir.ActivationFunctionType
AX_X = mybir.AxisListType.X

P = 128
IMAGES, CH, SIDE = 32, 64, 16
PIX = SIDE * SIDE
HALF = IMAGES // 2
TOKENS = IMAGES * PIX
NT = TOKENS // P
PAD_SIDE = SIDE + 2
TAPS = 9
BLOCKS = (2, 4, 8, 16)
N_SHIFT = sum(BLOCKS)

A_NODES = 5000
A_EDGES = 80000
A_W = 1024
A_HEADS, A_DIM = 8, 8
A_F = CH + A_HEADS
A_RUN = 32
A_CHUNKS = 20
A_USED = A_CHUNKS * P * A_RUN
A_RUNS = A_CHUNKS * P

G_EDGES = 262144
G_W = G_EDGES // P
G_HEADS, G_EXP = 4, 4
G_HF = G_HEADS * G_EXP
G_ROW = G_HF + G_HEADS
G_F = G_HF + G_HEADS
G_OUT = G_F + G_HEADS
G_RUN = 64
G_CHUNKS = G_W // G_RUN
G_RUNS = G_CHUNKS * P
HID = 2 * CH

SRC_BITS = 13
NONE = TOKENS
KEY_BASE = 0x40000000
PAD_KEY = KEY_BASE | (NONE << SRC_BITS)
BIG = 1.0e30
FAR = float(1 << 20)

C_IDENT, C_TRIU, C_SHIFT, C_WRAP, C_PAIR, C_IOTA, C_NODE, C_TOGGLE = (0, 128, 256, 384, 512, 640, 768, 832)
C_COLS = 840


def shape_constants():
    c = np.zeros((P, C_COLS), np.float32)
    p = np.arange(P)
    c[p, C_IDENT + p] = 1.0
    c[:, C_TRIU:C_TRIU + P] = p[:, None] <= p[None, :]
    c[p[:-1], C_SHIFT + p[1:]] = 1.0
    c[P - 1, C_WRAP] = 1.0
    c[:, C_PAIR:C_PAIR + P] = 0.5 * (p[:, None] // 2 == p[None, :] // 2)
    c[:, C_IOTA:C_IOTA + P] = p[None, :]
    c[:, C_NODE:C_NODE + NT] = p[:, None] + P * np.arange(NT)[None, :]
    sign = [np.where((p >> m) & 1, -1.0, 1.0) for m in range(7)]
    for m in range(8):
        c[:, C_TOGGLE + m] = (sign[m] if m < 7 else 1.0) * (sign[m - 1] if m else 1.0)
    perm = np.zeros((CH, 1 + N_SHIFT, 2, CH), np.float32)
    m = np.arange(CH)
    perm[m, 0, :, m] = 1.0
    n = 1
    for bs in BLOCKS:
        for k in range(bs):
            perm[m // bs * bs + (m % bs - k) % bs, n, :, m] = 1.0
            n += 1
    return c, perm.reshape(CH, (1 + N_SHIFT) * P)


def sort_steps(width):
    log_w = width.bit_length() - 1
    steps, cur = [], 0

    def add(*what):
        nonlocal cur
        steps.append((what, cur, 1 - cur))
        cur = 1 - cur

    for k in range(1, log_w + 8):
        if k >= log_w:
            add("toggle", k - log_w)
        cross = k - log_w
        if cross > 0:
            add("flip")
            for s in reversed(range(cross)):
                add("stage", None, 1 << s)
            add("flip")
        for s in reversed(range(min(k, log_w))):
            add("stage", k if k < log_w else None, 1 << s)
    return steps, cur


A_STEPS, A_LAST = sort_steps(A_W)
G_STEPS, G_LAST = sort_steps(G_W)
A_FLIPS = sum(s[0][0] == "flip" for s in A_STEPS)
G_FLIPS = sum(s[0][0] == "flip" for s in G_STEPS)


def build(nc, io, debug=None):
    with ExitStack() as ctx:
        def sem(name):
            return ctx.enter_context(nc.semaphore(name))

        def dram(name, shape, dt):
            kind = "ExternalOutput" if debug and name in debug else "Internal"
            return nc.dram_tensor(name, shape, dt, kind=kind).ap()

        d_asrc = dram("d_asrc", (P * A_W,), I32)
        d_adst = dram("d_adst", (P * A_W,), I32)
        d_adstq = dram("d_adstq", (P * A_W,), I32)
        d_gsrc = dram("d_gsrc", (G_EDGES,), I32)
        d_gdst = dram("d_gdst", (G_EDGES,), I32)
        d_gdstq = dram("d_gdstq", (G_EDGES,), I32)
        d_q = dram("d_q", (TOKENS, CH), F32)
        d_qseed = dram("d_qseed", (A_USED, CH), F32)
        d_as = dram("d_as", (A_USED, A_F), F32)
        d_acont = dram("d_acont", (P * A_W // A_RUN,), F32)
        d_ac = dram("d_ac", (A_RUNS, A_F), F32)
        d_h = dram("d_h", (TOKENS, G_ROW), F32)
        d_ad = dram("d_ad", (TOKENS, G_HEADS), F32)
        d_adseed = dram("d_adseed", (G_EDGES, G_HEADS), F32)
        d_gs = dram("d_gs", (G_EDGES, G_OUT), F32)
        d_gcont = dram("d_gcont", (G_RUNS,), F32)
        d_gc = dram("d_gc", (G_RUNS, G_OUT), F32)

        LIMIT = 53200
        arena = ctx.enter_context(nc.sbuf_tensor("arena", [P, LIMIT], F32))

        class Region:
            def __init__(self, at):
                self.at = at

            def take(self, n, dt=F32):
                a = self.at
                self.at += n
                assert self.at <= LIMIT, self.at
                v = arena[:, a:a + n]
                return v if dt == F32 else v.bitcast(dt)

        r = Region(0)
        const = r.take(C_COLS)
        ident = const[:, C_IDENT:C_IDENT + P]
        triu = const[:, C_TRIU:C_TRIU + P]
        shift = const[:, C_SHIFT:C_SHIFT + P]
        wrap = const[:, C_WRAP:C_WRAP + P]
        pair = const[:, C_PAIR:C_PAIR + P]
        iota = const[:, C_IOTA:C_IOTA + P]
        node = const[:, C_NODE:C_NODE + NT]
        ones = r.take(P)
        zeros = r.take(512)
        t_tok = r.take(NT * CH).rearrange("p (i c) -> p i c", c=CH)
        y_tok = r.take(NT * CH).rearrange("p (i c) -> p i c", c=CH)
        t_tile, y_tile = (x.rearrange("p (i h) c -> p h i c", h=2) for x in (t_tok, y_tok))

        def slot(tile):
            return tile % (NT // 2) * 2 + tile // (NT // 2)

        g_key_at = r.at
        g_key = [r.take(G_W) for _ in range(2)]
        a_key_at = r.at
        a_key = [r.take(A_W) for _ in range(2)]

        def node_table(dt=F32):
            return r.take(NT, dt)

        class Nodes:
            def __init__(self):
                self.run = node_table()
                self.run_i = node_table(I32)
                self.count = node_table()
                self.end = r.take(NT + 1)
                self.start = node_table()
                self.has = node_table()
                self.pos_f = node_table()
                self.pos = node_table(I32)
                self.prun = node_table(I32)
                self.cidx_f = node_table()
                self.cidx = node_table(I32)
                self.carried = node_table()
                self.seed_f = node_table()
                self.seed = node_table(I32)
                self.tot = node_table()

        a_nodes, g_nodes = Nodes(), Nodes()
        small = r.take(640)
        piv = [small[:, 0:16].bitcast(I32), small[:, 16:32].bitcast(I32)]
        gn_stat = small[:, 32:32 + HALF * 6].rearrange("p (j s) -> p j s", s=6)
        gn_mv = small[:, 128:160].rearrange("p (j s) -> p j s", s=2)
        gn_mean = small[:, 160:176]
        gn_dev = small[:, 176:192]
        gn_rstd = small[:, 192:208]
        gn_bias = small[:, 208:224]
        alph = small[:, 224:240]
        ln_sum = small[:, 256:320]
        ln_var = small[:, 320:384]
        run_prev = small[:, 384:416]
        run_cont = small[:, 416:448]
        first = r.at

        kv = [r.take(A_RUN * 2 * CH).rearrange("p (j f) -> p j f", f=2 * CH) for _ in range(2)]
        a_found = Region(first).take(NT * P, I32).rearrange("p (n j) -> p n j", j=P)
        y_at = C_COLS + P + 512 + NT * CH
        rr = Region(y_at)
        list_nodes = rr.take(G_W, I32)
        a_below = list_nodes.bitcast(F32).rearrange("p (n j) -> p n j", j=P)
        hot_lo = rr.take(16 * P // 2, BF16).rearrange("p (n j) -> p n j", j=P)
        hot_hi = rr.take(16 * NT // 2, BF16).rearrange("p (n j) -> p n j", j=NT)
        assert rr.at <= y_at + NT * CH
        mid = r.at
        c = Region(mid)
        x_ch = c.take(HALF * PIX).rearrange("p (j s) -> p j s", s=PIX)
        y_pad = c.take(HALF * PAD_SIDE ** 2).rearrange("p (j y x) -> p j y x", y=PAD_SIDE, x=PAD_SIDE)
        w_taps = c.take(TAPS * P).rearrange("p (t o) -> p t o", o=P)
        w_dup = c.take(len(BLOCKS) * 2 * CH * TAPS).rearrange("p (b n) -> p b n", b=len(BLOCKS))
        w_own = c.take(CH * TAPS)
        square_a = y_pad.rearrange("p j y x -> p (j y x)")[:, 0:NT * CH // 2].rearrange("p (i c) -> p i c", c=CH)
        perm = c.take((1 + N_SHIFT) * P).rearrange("p (n m) -> p n m", m=P)
        a = Region(mid)
        q_seed = [a.take(A_RUN * CH).rearrange("p (j f) -> p j f", f=CH) for _ in range(2)]
        a_sidx = [a.take(A_RUN, I32) for _ in range(2)]
        a_didx = [a.take(A_RUN, I32) for _ in range(2)]
        a_fidx = [a.take(4, I32) for _ in range(2)]
        q_first = [a.take(CH) for _ in range(2)]
        q_fm = a.take(CH * A_RUN)
        q_edge = a.take(CH * A_RUN)
        a_nst = a.take(A_RUN)
        a_go = a.take(A_F * A_RUN)
        a_prod = a.take(CH * A_RUN)
        a_score = a.take(A_HEADS * A_RUN)
        a_msg = a.take(A_F * A_RUN)
        a_sum = a.take(A_F * A_RUN)
        a_rows = [a.take(A_RUN * A_F).rearrange("p (j f) -> p j f", f=A_F) for _ in range(2)]
        a2 = Region(first)
        a_tail = a2.take(A_CHUNKS * A_F).rearrange("p (c f) -> p c f", f=A_F)
        a_tailT = a2.take(A_RUNS)
        a_cont = a2.take(A_RUNS)
        a_carT = a2.take(A_RUNS)
        a_car = a2.take(A_CHUNKS * A_F).rearrange("p (c f) -> p c f", f=A_F)
        a_end = a2.take(NT * A_F).rearrange("p (i f) -> p i f", f=A_F)
        a_before = a2.take(NT * A_F).rearrange("p (i f) -> p i f", f=A_F)
        g = Region(first)
        yT = g.take(NT // 2 * P).rearrange("p (i n) -> p i n", n=P)
        w1 = g.take(4 * HID).rearrange("p (e n) -> p e n", e=4)
        w2 = g.take(4 * CH).rearrange("p (e n) -> p e n", e=4)
        b1 = g.take(4)
        b2 = g.take(4 * CH)
        wgat = g.take(G_HF)
        att = g.take(5 * G_HF).rearrange("p (v n) -> p v n", v=5)
        h_tok = g.take(NT * G_ROW).rearrange("p (i f) -> p i f", f=G_ROW)
        ad_tok = g.take(NT * G_HEADS).rearrange("p (i f) -> p i f", f=G_HEADS)
        h_prod = Region(y_at).take(NT * G_HF).rearrange("p (i h k) -> p i h k", h=G_HEADS, k=G_EXP)
        hid = [g.take(512) for _ in range(2)]
        exp_out = g.take(NT * 4 * CH).rearrange("p (i n) -> p i n", n=4 * CH)
        g_mid = g.at
        hs = [g.take(G_RUN * G_ROW).rearrange("p (j f) -> p j f", f=G_ROW) for _ in range(2)]
        ad_seed = [g.take(G_RUN * G_HEADS).rearrange("p (j f) -> p j f", f=G_HEADS) for _ in range(2)]
        g_sidx = [g.take(G_RUN, I32) for _ in range(2)]
        g_didx = [g.take(G_RUN, I32) for _ in range(2)]
        g_fidx = [g.take(4, I32) for _ in range(2)]
        ad_first = [g.take(G_HEADS) for _ in range(2)]
        g_rows = [g.take(G_RUN * G_OUT).rearrange("p (j f) -> p j f", f=G_OUT) for _ in range(2)]
        HJ = G_HEADS * G_RUN
        g = Region(y_at)
        g_nst = g.take(HJ)
        g_cut = g.take(HJ)
        ad_fm = g.take(HJ)
        ad_edge = g.take(HJ)
        g_x = g.take(HJ)
        g_e = g.take(HJ)
        g_max = g.take(HJ + 1)
        g_dm = g.take(HJ)
        g_corr = g.take(HJ)
        g_em = g.take(HJ)
        g_msg = g.take(G_F * G_RUN)
        g_corr_f = g.take(G_F * G_RUN)
        g_sum = g.take(G_F * G_RUN)
        assert g.at <= g_key_at + 2 * G_W
        r_a = Region(y_at)
        g_tailT = r_a.take(G_RUNS)
        g_cutT = r_a.take(G_RUNS)
        assert r_a.at <= g_key_at + 2 * G_W
        gs_ = Region(g_mid)
        g_found = gs_.take(NT * P, I32).rearrange("p (n j) -> p n j", j=P)
        g_below = gs_.take(16 * P).rearrange("p (n j) -> p n j", j=P)
        square = g_below.rearrange("p n j -> p (n j)").rearrange("p (i c) -> p i c", c=CH)
        g2 = Region(g_mid)
        g_tmaxT = g2.take(G_RUNS)
        g_cmaxT = g2.take(G_RUNS + 1)
        g3 = Region(first)
        g_dT = g3.take(G_RUNS)
        g_end = g2.take(NT * G_OUT).rearrange("p (i f) -> p i f", f=G_OUT)
        g_tail = Region(a_key_at).take(G_CHUNKS * (G_OUT + G_F)).rearrange("p (c f) -> p c f", f=G_OUT + G_F)
        g4 = Region(y_at)
        n4 = [g4.take(NT * 4).rearrange("p (i h) -> p i h", h=4) for _ in range(12)]
        n16 = [g4.take(NT * G_HF) for _ in range(3)]
        g_before = g4.take(NT * G_OUT).rearrange("p (i f) -> p i f", f=G_OUT)
        assert g4.at <= g_key_at + 2 * G_W
        out_ch = arena[:, g_mid:g_mid + HALF * PIX].rearrange("p (j s) -> p j s", s=PIX)

        ps = [ctx.enter_context(nc.psum_tensor(f"ps{b}", [P, 512], F32)) for b in range(8)]

        const_in, perm_in, x_in, w_in, a_edges_in, g_edges_in = (
            sem(n) for n in ("const_in", "perm_in", "x_in", "w_in", "a_edges_in", "g_edges_in"))
        zeros_set, qseed_zero, adseed_zero = sem("zeros_set"), sem("qseed_zero"), sem("adseed_zero")
        dve_step, dve_loop_a, dve_loop_g = sem("dve_step"), sem("dve_loop_a"), sem("dve_loop_g")
        gathers_begun = sem("gathers_begun")
        gn_pair_in, gn_pair = sem("gn_pair_in"), sem("gn_pair")
        gn_ready, gn_root, y_ready = sem("gn_ready"), sem("gn_root"), sem("y_ready")
        border_set, perm_scaled, w_mixed, w_ready = sem("border_set"), sem("perm_scaled"), sem("w_mixed"), sem("w_ready")
        alpha_exp_in, alpha_exp = sem("alpha_exp_in"), sem("alpha_exp")
        conv_done, conv_added, t_turned, t_taken = sem("conv_done"), sem("conv_added"), sem("t_turned"), sem("t_taken")
        flip_in, flip_done, flip_taken = sem("flip_in"), sem("flip_done"), sem("flip_taken")
        a_list_set, a_list_out, g_list_set, g_list_out = (sem(n) for n in ("a_list_set", "a_list_out", "g_list_set", "g_list_out"))
        hot_set, hist_done, hist_set, cum_done, run_set, ends_set, starts_done, pos_set = (
            sem(n) for n in ("hot_set", "hist_done", "hist_set", "cum_done", "run_set",
                             "ends_set", "starts_done", "pos_set"))
        found = [[sem(f"found{k}_{n}") for n in range(4)] for k in range(2)]
        last_set, last_shifted, cont_set, cont_out = sem("last_set"), sem("last_shifted"), sem("cont_set"), sem("cont_out")
        root_in, root_out, y_set, q_out, q_scattered = sem("root_in"), sem("root_out"), sem("y_set"), sem("q_out"), sem("q_scattered")
        a_idx_in = [sem(f"a_idx_in{b}") for b in range(2)]
        a_seed_in = [sem(f"a_seed_in{b}") for b in range(2)]
        kv_in = [sem(f"kv_in{b}") for b in range(2)]
        a_used, a_flags, a_laid, a_scored, a_weighed, a_summed, a_rows_set = (
            sem(n) for n in ("a_used", "a_flags", "a_laid", "a_scored", "a_weighed", "a_summed", "a_rows_set"))
        a_rows_out = [sem(f"a_rows_out{b}") for b in range(2)]
        a_tail_in, a_tail_turned, a_tail_taken, a_carried, a_car_turned, a_car_taken, a_car_out, a_ends_in = (
            sem(n) for n in ("a_tail_in", "a_tail_turned", "a_tail_taken", "a_carried", "a_car_turned", "a_car_taken",
                             "a_car_out", "a_ends_in"))
        gw_in, yT_turned, yT_taken, h_done, h_set, h_out, ad_scattered = (
            sem(n) for n in ("gw_in", "yT_turned", "yT_taken", "h_done", "h_set", "h_out", "ad_scattered"))
        hid_done, hid_set, hid_used, exp_taken = (sem(n) for n in ("hid_done", "hid_set", "hid_used", "exp_taken"))
        g_idx_in = [sem(f"g_idx_in{b}") for b in range(2)]
        hs_in = [sem(f"hs_in{b}") for b in range(2)]
        g_used, g_laid, g_max_set, g_exp_done, g_weighed, g_summed, g_rows_set, g_flags = (
            sem(n) for n in ("g_used", "g_laid", "g_max_set", "g_exp_done", "g_weighed", "g_summed", "g_rows_set", "g_flags"))
        g_rows_out = [sem(f"g_rows_out{b}") for b in range(2)]
        g_tail_in, g_rep_set, g_tail_turned, g_tail_taken, g_dT_set, g_dT_exp, g_carried, g_car_turned, g_car_taken, g_car_out, g_ends_in = (
            sem(n) for n in ("g_tail_in", "g_rep_set", "g_tail_turned", "g_tail_taken", "g_dT_set", "g_dT_exp", "g_carried",
                             "g_car_turned", "g_car_taken", "g_car_out", "g_ends_in"))
        node_exp_in, node_exp, gate_root_in, gate_root, gate_exp_in, gate_exp = (
            sem(n) for n in ("node_exp_in", "node_exp", "gate_root_in", "gate_root", "gate_exp_in", "gate_exp"))
        out_set, out_turned, out_laid, out_stored = sem("out_set"), sem("out_turned"), sem("out_laid"), sem("out_stored")

        block = ctx.enter_context(nc.Block())

        def bc(ap, shape):
            return ap.to_broadcast(shape)

        @block.sync
        def _(sp):
            sp.dma_start(a_key[1][:, 0:A_EDGES // P].bitcast(I32),
                         io["a_edges"][1].rearrange("(p j) -> p j", p=P)).then_inc(a_edges_in, 16)
            sp.dma_start(a_key[0][:, 0:A_EDGES // P].bitcast(I32),
                         io["a_edges"][0].rearrange("(p j) -> p j", p=P)).then_inc(a_edges_in, 16)
            sp.dma_start(const, io["const"]).then_inc(const_in, 16)
            for half in range(2):
                sp.dma_start(x_ch[half * CH:(half + 1) * CH, :, :],
                             io["x"][half * HALF:(half + 1) * HALF].rearrange("j c s -> c j s")).then_inc(x_in, 16)
            sp.dma_start(perm[0:CH, :, :].rearrange("p n m -> p (n m)"), io["perm"]).then_inc(perm_in, 16)
            sp.dma_start(alph[0:CH, 0:5], io["alphas"].partition_broadcast(CH)).then_inc(w_in, 16)
            sp.dma_start(w_own[0:CH, :], io["w_own"]).then_inc(w_in, 16)
            for n, bs in enumerate(BLOCKS):
                view = w_dup[0:CH, n, :].rearrange("p (q s b) -> p q s b", s=2, b=bs * TAPS)
                for copy in range(2):
                    sp.dma_start(view[:, :, copy, :],
                                 io["w_blocks"][n].rearrange("p (q b) -> p q b", b=bs * TAPS)).then_inc(w_in, 16)
            for n in range(2):
                sp.dma_start(g_key[n].bitcast(I32), io["g_edges"][n].rearrange("(p j) -> p j", p=P)).then_inc(g_edges_in, 16)
            sp.wait_ge(zeros_set, 1)
            zq = d_qseed.rearrange("(p n) f -> p (n f)", p=P)
            per = A_USED // P * CH
            for n in range(0, per, 8192):
                sp.dma_start(zq[:, n:n + 8192].rearrange("p (r z) -> p r z", z=512),
                             bc(zeros[:, None, :], [P, 16, 512])).then_inc(qseed_zero, 16)
            sp.dma_start(d_adseed.rearrange("(p n) f -> p (n f)", p=P).rearrange("p (r z) -> p r z", z=512),
                         bc(zeros[:, None, :], [P, 16, 512])).then_inc(adseed_zero, 16)

            sp.wait_ge(a_list_set, 1)
            for out, src in ((d_asrc, a_key[1 - A_LAST]), (d_adst, a_key[A_LAST]), (d_adstq, list_nodes[:, 0:A_W])):
                sp.dma_start(out.rearrange("(p j) -> p j", p=P), src.bitcast(I32)).then_inc(a_list_out, 16)
            sp.wait_ge(cont_set, 1)
            sp.dma_start(d_acont.rearrange("(p j) -> p j", p=P), run_cont[:, 0:A_W // A_RUN]).then_inc(cont_out, 16)
            sp.wait_ge(y_set, 1)
            for half in range(2):
                sp.dma_start(d_q.rearrange("(h i p) c -> h p i c", p=P, h=2)[half], y_tile[:, half]).then_inc(q_out, 16)
            sp.wait_ge(a_list_out, 48)
            sp.wait_ge(q_scattered, 16 * NT)

            src_v = d_asrc.rearrange("(c p j) -> c p j", p=P, j=A_RUN)
            dst_v = d_adst.rearrange("(c p j) -> c p j", p=P, j=A_RUN)
            dstq_v = d_adstq.rearrange("(c p j) -> c p j", p=P, j=A_RUN)
            seed_v = d_qseed.rearrange("(c p j) f -> c p j f", p=P, j=A_RUN)
            out_v = d_as.rearrange("(c p j) f -> c p j f", p=P, j=A_RUN)

            def a_load(c, b):
                sp.dma_start(a_sidx[b], src_v[c]).then_inc(a_idx_in[b], 16)
                sp.dma_start(a_didx[b], dst_v[c]).then_inc(a_idx_in[b], 16)
                sp.dma_start(a_fidx[b], dstq_v[c][:, 0:4]).then_inc(a_idx_in[b], 16)
                sp.dma_start(q_seed[b], seed_v[c]).then_inc(a_seed_in[b], 16)

            for b in range(2):
                a_load(b, b)
            sp.wait_ge(g_list_set, 1)
            for out, src in ((d_gsrc, g_key[1 - G_LAST]), (d_gdst, g_key[G_LAST]), (d_gdstq, list_nodes)):
                sp.dma_start(out.rearrange("(p j) -> p j", p=P), src.bitcast(I32)).then_inc(g_list_out, 16)
            sp.wait_ge(cont_set, 2)
            sp.dma_start(d_gcont.rearrange("(p j) -> p j", p=P), run_cont[:, 0:G_W // G_RUN]).then_inc(cont_out, 16)

            with sp.Fori(0, A_CHUNKS // 2 - 1) as it:
                for b in range(2):
                    sp.wait_ge(a_used, it * 2 + (b + 1))
                    sp.wait_ge(a_rows_set, it * 2 + (b + 1))
                    sp.dma_start(out_v[bass.ds(it * 2 + b, 1)].rearrange("c p j f -> (c p) j f"), a_rows[b]).then_inc(a_rows_out[b], 16)
                    nxt = it * 2 + (b + 2)
                    sp.dma_start(a_sidx[b], src_v[bass.ds(nxt, 1)].rearrange("c p j -> (c p) j")).then_inc(a_idx_in[b], 16)
                    sp.dma_start(a_didx[b], dst_v[bass.ds(nxt, 1)].rearrange("c p j -> (c p) j")).then_inc(a_idx_in[b], 16)
                    sp.dma_start(a_fidx[b], dstq_v[bass.ds(nxt, 1), :, 0:4].rearrange("c p j -> (c p) j")).then_inc(a_idx_in[b], 16)
                    sp.dma_start(q_seed[b], seed_v[bass.ds(nxt, 1)].rearrange("c p j f -> (c p) j f")).then_inc(a_seed_in[b], 16)
            for b in range(2):
                sp.wait_ge(a_rows_set, A_CHUNKS - 1 + b)
                sp.dma_start(out_v[A_CHUNKS - 2 + b], a_rows[b]).then_inc(a_rows_out[b], 16)
            for b in range(2):
                sp.wait_ge(a_rows_out[b], 16 * (A_CHUNKS // 2))
            sp.wait_ge(cont_out, 16)
            sp.dma_start(a_tail, d_as.rearrange("(c p j) f -> j p c f", p=P, j=A_RUN)[A_RUN - 1]).then_inc(a_tail_in, 16)
            sp.dma_start(a_cont[0:A_F, :], d_acont[0:A_RUNS].partition_broadcast(A_F)).then_inc(a_tail_in, 16)
            sp.wait_ge(a_car_taken, 5)
            sp.dma_start(d_ac.rearrange("(c p) f -> p c f", p=P), a_car).then_inc(a_car_out, 16)

            sp.wait_ge(y_set, 2)
            for half in range(2):
                at = slice(half * CH, (half + 1) * CH)
                sp.dma_start(w1[at], io["w1"].rearrange("e c n -> c e n")).then_inc(gw_in, 16)
                sp.dma_start(wgat[at], io["wgat"]).then_inc(gw_in, 16)
            sp.dma_start(w2, io["w2"].rearrange("e n c -> n e c")).then_inc(gw_in, 16)
            sp.dma_start(b1, io["b1"]).then_inc(gw_in, 16)
            sp.dma_start(b2, io["b2"].rearrange("e c -> (e c)").partition_broadcast(P)).then_inc(gw_in, 16)
            for n, name in enumerate(("att_src", "att_dst", "b_gat", "gamma", "beta")):
                sp.dma_start(att[:, n, :], io[name].partition_broadcast(P)).then_inc(gw_in, 16)

            sp.wait_ge(h_set, 1)
            sp.dma_start(d_h.rearrange("(i p) f -> p i f", p=P), h_tok).then_inc(h_out, 16)
            sp.dma_start(d_ad.rearrange("(i p) f -> p i f", p=P), ad_tok).then_inc(h_out, 16)
            sp.wait_ge(g_list_out, 48)
            sp.wait_ge(ad_scattered, 16 * NT)

            gsrc_v = d_gsrc.rearrange("(c p j) -> c p j", p=P, j=G_RUN)
            gdst_v = d_gdst.rearrange("(c p j) -> c p j", p=P, j=G_RUN)
            gdstq_v = d_gdstq.rearrange("(c p j) -> c p j", p=P, j=G_RUN)
            gseed_v = d_adseed.rearrange("(c p j) f -> c p j f", p=P, j=G_RUN)
            gout_v = d_gs.rearrange("(c p j) f -> c p j f", p=P, j=G_RUN)
            for b in range(2):
                sp.dma_start(g_sidx[b], gsrc_v[b]).then_inc(g_idx_in[b], 16)
                sp.dma_start(g_didx[b], gdst_v[b]).then_inc(g_idx_in[b], 16)
                sp.dma_start(g_fidx[b], gdstq_v[b][:, 0:4]).then_inc(g_idx_in[b], 16)
                sp.dma_start(ad_seed[b], gseed_v[b]).then_inc(g_idx_in[b], 16)
            with sp.Fori(0, G_CHUNKS // 2 - 1) as it:
                for b in range(2):
                    sp.wait_ge(g_used, it * 2 + (b + 1))
                    sp.wait_ge(g_rows_set, it * 2 + (b + 1))
                    sp.dma_start(gout_v[bass.ds(it * 2 + b, 1)].rearrange("c p j f -> (c p) j f"), g_rows[b]).then_inc(g_rows_out[b], 16)
                    nxt = it * 2 + (b + 2)
                    sp.dma_start(g_sidx[b], gsrc_v[bass.ds(nxt, 1)].rearrange("c p j -> (c p) j")).then_inc(g_idx_in[b], 16)
                    sp.dma_start(g_didx[b], gdst_v[bass.ds(nxt, 1)].rearrange("c p j -> (c p) j")).then_inc(g_idx_in[b], 16)
                    sp.dma_start(g_fidx[b], gdstq_v[bass.ds(nxt, 1), :, 0:4].rearrange("c p j -> (c p) j")).then_inc(g_idx_in[b], 16)
                    sp.dma_start(ad_seed[b], gseed_v[bass.ds(nxt, 1)].rearrange("c p j f -> (c p) j f")).then_inc(g_idx_in[b], 16)
            for b in range(2):
                sp.wait_ge(g_rows_set, G_CHUNKS - 1 + b)
                sp.dma_start(gout_v[G_CHUNKS - 2 + b], g_rows[b]).then_inc(g_rows_out[b], 16)
            for b in range(2):
                sp.wait_ge(g_rows_out[b], 16 * (G_CHUNKS // 2))
            sp.wait_ge(cont_out, 32)
            sp.dma_start(g_tail[:, :, 0:G_OUT], d_gs.rearrange("(c p j) f -> j p c f", p=P, j=G_RUN)[G_RUN - 1]).then_inc(g_tail_in, 16)
            sp.dma_start(g_cutT[0:G_F, :], d_gcont.partition_broadcast(G_F)).then_inc(g_tail_in, 16)
            sp.wait_ge(g_car_taken, 2 * G_CHUNKS // 4)
            sp.dma_start(d_gc.rearrange("(c p) f -> p c f", p=P), g_tail[:, :, 0:G_OUT]).then_inc(g_car_out, 16)

            out_dram = io["out"]
            for n in range(4):
                sp.wait_ge(out_laid, 2 * (n + 1))
                for half in range(2):
                    sp.dma_start(out_dram[half * HALF + 4 * n:half * HALF + 4 * n + 4].rearrange("j c s -> c j s"),
                                 out_ch[half * CH:(half + 1) * CH, 4 * n:4 * n + 4, :]).then_inc(out_stored, 16)
            sp.wait_ge(out_stored, 16 * 8)

        @block.gpsimd
        def _(pool):
            pool.memset(zeros, 0.0).then_inc(zeros_set, 1)
            pool.memset(y_pad, 0.0).then_inc(border_set, 1)

            def search_gathers(nodes, table, n_rows, out, sems):
                for i in range(NT):
                    pool.indirect_dma_start(out[:, i, :], None, table.rearrange("(n j) -> n j", j=P)[0:n_rows],
                                            bass.IndirectOffsetOnAxis(nodes.run_i[:, i:i + 1], 0)).then_inc(sems[i // 16], 16)

            pool.wait_ge(run_set, 1)
            pool.wait_ge(a_list_out, 48)
            search_gathers(a_nodes, d_adst, A_W, a_found, found[0])
            pool.wait_ge(pos_set, 1)
            pool.wait_ge(y_set, 1)
            pool.wait_ge(qseed_zero, 16 * (A_USED // P * CH // 8192))
            for i in range(NT):
                pool.indirect_dma_start(d_qseed, bass.IndirectOffsetOnAxis(a_nodes.seed[:, i:i + 1], 0), y_tok[:, slot(i), :], None,
                                        bounds_check=A_USED - 1, oob_is_err=False).then_inc(q_scattered, 16)
            pool.wait_ge(q_out, 32)

            def a_gather(b):
                for j in range(A_RUN):
                    pool.indirect_dma_start(kv[b][:, j, :], None, io["kv"], bass.IndirectOffsetOnAxis(a_sidx[b][:, j:j + 1], 0))\
                        .then_inc(kv_in[b], 16)
                pool.indirect_dma_start(q_first[b], None, d_q, bass.IndirectOffsetOnAxis(a_fidx[b][:, 0:1], 0)).then_inc(kv_in[b], 16)

            for b in range(2):
                pool.wait_ge(a_idx_in[b], 48)
                a_gather(b)
            with pool.Fori(1, A_CHUNKS // 2) as it:
                for b in range(2):
                    pool.wait_ge(a_idx_in[b], it * 48 + 48)
                    pool.wait_ge(a_used, it * 2 + (b - 1))
                    pool.sem_inc(gathers_begun, 1)
                    a_gather(b)

            for b in range(2):
                pool.wait_ge(a_rows_out[b], 16 * (A_CHUNKS // 2))
            pool.wait_ge(a_used, A_CHUNKS)
            pool.wait_ge(a_rows_set, A_CHUNKS)
            for i in range(NT):
                pool.indirect_dma_start(a_end[:, i, :], None, d_as, bass.IndirectOffsetOnAxis(a_nodes.pos[:, i:i + 1], 0))\
                    .then_inc(a_ends_in, 16)
            pool.wait_ge(run_set, 2)
            pool.wait_ge(g_list_out, 48)
            search_gathers(g_nodes, d_gdst, G_W, g_found, found[1])
            pool.wait_ge(a_car_out, 16)
            for i in range(NT):
                pool.indirect_dma_start(a_before[:, i, :], None, d_ac, bass.IndirectOffsetOnAxis(a_nodes.cidx[:, i:i + 1], 0))\
                    .then_inc(a_ends_in, 16)

            pool.wait_ge(pos_set, 2)
            pool.wait_ge(h_set, 1)
            pool.wait_ge(adseed_zero, 16)
            for i in range(NT):
                pool.indirect_dma_start(d_adseed, bass.IndirectOffsetOnAxis(g_nodes.seed[:, i:i + 1], 0), ad_tok[:, i, :], None,
                                        bounds_check=G_EDGES - 1, oob_is_err=False).then_inc(ad_scattered, 16)
            pool.wait_ge(h_out, 32)

            def g_gather(b):
                pool.indirect_dma_start(ad_first[b], None, d_ad, bass.IndirectOffsetOnAxis(g_fidx[b][:, 0:1], 0)).then_inc(hs_in[b], 16)
                for j in range(G_RUN):
                    pool.indirect_dma_start(hs[b][:, j, :], None, d_h, bass.IndirectOffsetOnAxis(g_sidx[b][:, j:j + 1], 0))\
                        .then_inc(hs_in[b], 16)

            for b in range(2):
                pool.wait_ge(g_idx_in[b], 64)
                g_gather(b)
            with pool.Fori(1, G_CHUNKS // 2) as it:
                for b in range(2):
                    pool.wait_ge(g_idx_in[b], it * 64 + 64)
                    pool.wait_ge(g_used, it * 2 + (b - 1))
                    pool.sem_inc(gathers_begun, 1)
                    g_gather(b)
            for b in range(2):
                pool.wait_ge(g_rows_out[b], 16 * (G_CHUNKS // 2))
            pool.wait_ge(g_rows_set, G_CHUNKS)
            for i in range(NT):
                pool.indirect_dma_start(g_end[:, i, :], None, d_gs, bass.IndirectOffsetOnAxis(g_nodes.pos[:, i:i + 1], 0))\
                    .then_inc(g_ends_in, 16)
            pool.wait_ge(g_car_out, 16)
            for i in range(NT):
                pool.indirect_dma_start(g_before[:, i, :], None, d_gc, bass.IndirectOffsetOnAxis(g_nodes.cidx[:, i:i + 1], 0))\
                    .then_inc(g_ends_in, 16)

        @block.tensor
        def _(pe):
            def turn(out, in_, n=P):
                return nc.tensor.transpose(out, in_, ident[0:n, 0:n])

            def sort_flips(steps, key, done):
                n = done
                for what, src, dst in steps:
                    if what[0] != "flip":
                        continue
                    n += 1
                    pe.wait_ge(flip_in, n)
                    width = key[0].shape[1]
                    for blk in range(width // P):
                        last = turn(ps[blk // 4][:, blk % 4 * P:(blk % 4 + 1) * P], key[src][:, blk * P:(blk + 1) * P])
                        if blk % 4 == 3:
                            last.then_inc(flip_done, 1)

            def histogram(nb):
                for n in range(nb):
                    last = nc.tensor.matmul(ps[4][:, 0:NT], hot_lo[:, n, :], hot_hi[:, n, :], start=n == 0, stop=n == nb - 1)
                last.then_inc(hist_done, 1)

            def running(k, nodes):
                pe.wait_ge(hist_set, k)
                nc.tensor.matmul(ps[5][:, 0:NT], triu, nodes.tot, start=True, stop=True)
                nc.tensor.matmul(ps[6][:, 0:NT], ones, nodes.tot, start=True, stop=True).then_inc(cum_done, 1)

            def starts(k, nodes):
                pe.wait_ge(ends_set, k)
                nc.tensor.matmul(ps[5][:, 0:NT], shift, nodes.end[:, 1:NT + 1], start=True, stop=False)
                nc.tensor.matmul(ps[5][:, 0:NT], wrap, nodes.end[:, 0:NT], start=False, stop=True).then_inc(starts_done, 1)

            def last_of_before(k):
                pe.wait_ge(last_set, k)
                nc.tensor.matmul(ps[7][:, 0:1], shift, ln_sum[:, 0:1],
                                 start=True, stop=True).then_inc(last_shifted, 1)

            pe.wait_ge(const_in, 16)
            pe.wait_ge(gn_pair_in, 1)
            nc.tensor.matmul(ps[7][:, 0:HALF], pair, gn_mean, start=True, stop=True).then_inc(gn_pair, 1)
            pe.wait_ge(gn_pair_in, 2)
            nc.tensor.matmul(ps[7][:, 32:32 + HALF], pair, gn_dev, start=True, stop=True).then_inc(gn_pair, 1)
            pe.wait_ge(perm_scaled, 1)
            for part in range(2):
                cols = CH * TAPS // 2
                acc = ps[4 + part][:, 0:cols]
                nc.tensor.matmul(acc, perm[0:CH, 0, :], w_own[0:CH, part * cols:(part + 1) * cols], start=True, stop=False)
                n = 1
                for m, bs in enumerate(BLOCKS):
                    view = w_dup[0:CH, m, :].rearrange("p (q b) -> p q b", b=2 * bs * TAPS)
                    q = CH // bs // 2
                    for k in range(bs):
                        lo = (bs - k) % bs * TAPS
                        last = nc.tensor.matmul(acc, perm[0:CH, n, :], view[:, part * q:(part + 1) * q, lo:lo + bs * TAPS],
                                                start=False, stop=n == N_SHIFT)
                        n += 1
                last.then_inc(w_mixed, 1)
            sort_flips(A_STEPS, a_key, 0)
            last_of_before(1)
            pe.wait_ge(hot_set, 1)
            histogram(A_W // P)
            running(1, a_nodes)
            pe.wait_ge(run_set, 1)
            pe.wait_ge(w_ready, 1)
            pe.wait_ge(y_ready, HALF)
            for j in range(HALF // 2):
                if j >= 2:
                    pe.wait_ge(conv_added, j - 1)
                acc = ps[4 + j % 2][:, :]
                for tap in range(TAPS):
                    dy, dx = tap // 3, tap % 3
                    last = nc.tensor.matmul(acc, w_taps[:, tap, :], y_pad[:, 2 * j:2 * j + 2, dy:dy + SIDE, dx:dx + SIDE],
                                            start=tap == 0, stop=tap == TAPS - 1)
                last.then_inc(conv_done, 1)
                if j:
                    pe.wait_ge(conv_added, j)
                    if j >= 3:
                        pe.wait_ge(t_taken, j - 2)
                    for n in range(4):
                        last = turn(ps[6 + (j - 1) % 2][:, n * P:(n + 1) * P], x_ch[:, 2 * (j - 1) + n // 2, n % 2 * P:(n % 2 + 1) * P])
                    last.then_inc(t_turned, 1)
            j = HALF // 2
            pe.wait_ge(conv_added, j)
            pe.wait_ge(t_taken, j - 2)
            for n in range(4):
                last = turn(ps[6 + (j - 1) % 2][:, n * P:(n + 1) * P], x_ch[:, 2 * (j - 1) + n // 2, n % 2 * P:(n % 2 + 1) * P])
            last.then_inc(t_turned, 1)

            starts(1, a_nodes)
            sort_flips(G_STEPS, g_key, A_FLIPS)
            last_of_before(2)
            pe.wait_ge(hot_set, 2)
            histogram(G_W // P)
            running(2, g_nodes)
            pe.wait_ge(run_set, 2)

            pe.wait_ge(a_tail_in, 32)
            for n in range(A_CHUNKS // 4):
                if n >= 2:
                    pe.wait_ge(a_tail_taken, n - 1)
                for c_ in range(4):
                    last = turn(ps[4 + n % 2][0:A_F, c_ * P:(c_ + 1) * P], a_tail[:, 4 * n + c_, :])
                last.then_inc(a_tail_turned, 1)
            pe.wait_ge(a_carried, 1)
            for n in range(A_CHUNKS // 4):
                if n >= 2:
                    pe.wait_ge(a_car_taken, n - 1)
                for c_ in range(4):
                    last = turn(ps[6 + n % 2][:, c_ * A_F:(c_ + 1) * A_F], a_carT[0:A_F, (4 * n + c_) * P:(4 * n + c_ + 1) * P], A_F)
                last.then_inc(a_car_turned, 1)

            pe.wait_ge(y_set, 2)
            for n in range(8):
                if n >= 2:
                    pe.wait_ge(yT_taken, n - 1)
                for k in range(4):
                    i = 4 * n + k
                    last = turn(ps[n % 2][:, k * P:(k + 1) * P],
                                y_tok[:, 2 * i:2 * i + 2, :].rearrange("p a c -> p (a c)"))
                last.then_inc(yT_turned, 1)
            pe.wait_ge(gw_in, 16 * 12)
            pe.wait_ge(yT_taken, 8)
            for i in range(NT):
                half = i // (NT // 2)
                at = slice(half * CH, (half + 1) * CH)
                last = nc.tensor.matmul(ps[2 + half][:, i % 32 * G_HF:(i % 32 + 1) * G_HF], yT[at, i % 32, :], wgat[at], start=True, stop=True)
            last.then_inc(h_done, 1)
            starts(2, g_nodes)
            pe.wait_ge(pos_set, 2)
            def expert_out(n):
                grp, e = n // 4, n % 4
                if n % 4 == 0 and grp >= 1:
                    pe.wait_ge(exp_taken, grp)
                pe.wait_ge(hid_set, n + 1)
                for k in range(4):
                    last = nc.tensor.matmul(ps[6 + k // 2][:, k % 2 * 256 + e * CH:k % 2 * 256 + (e + 1) * CH],
                                            hid[n % 2][:, k * P:(k + 1) * P], w2[:, e, :], start=True, stop=True)
                last.then_inc(hid_used, 1)

            for n in range(64):
                grp, e = n // 4, n % 4
                half, i0 = grp // 8, grp % 8 * 4
                at = slice(half * CH, (half + 1) * CH)
                if n >= 2:
                    pe.wait_ge(hid_set, n - 1)
                nc.tensor.matmul(ps[4 + n % 2][:, :], w1[at, e, :], yT[at, i0:i0 + 4, :].rearrange("p i n -> p (i n)"),
                                 start=True, stop=True).then_inc(hid_done, 1)
                if n >= 1:
                    expert_out(n - 1)
            expert_out(63)

            pe.wait_ge(g_rep_set, 1)
            for n in range(G_CHUNKS // 4):
                if n >= 1:
                    pe.wait_ge(g_tail_taken, 2 * n)
                for c_ in range(4):
                    nc_ = 4 * n + c_
                    turn(ps[4][0:G_F, c_ * P:(c_ + 1) * P], g_tail[:, nc_, 0:G_F])
                    last = turn(ps[5][0:G_F, c_ * P:(c_ + 1) * P], g_tail[:, nc_, G_OUT:G_OUT + G_F])
                last.then_inc(g_tail_turned, 1)
            pe.wait_ge(g_carried, 1)
            for n in range(G_CHUNKS // 4):
                if n >= 1:
                    pe.wait_ge(g_car_taken, 2 * n)
                for c_ in range(4):
                    nc_ = 4 * n + c_
                    turn(ps[6][:, c_ * G_F:(c_ + 1) * G_F], g_cutT[0:G_F, nc_ * P:(nc_ + 1) * P], G_F)
                    last = turn(ps[7][:, c_ * G_F:(c_ + 1) * G_F], g_cmaxT[0:G_F, 1 + nc_ * P:1 + (nc_ + 1) * P], G_F)
                last.then_inc(g_car_turned, 1)

            pe.wait_ge(out_set, 1)
            for n in range(8):
                if n >= 2:
                    pe.wait_ge(out_laid, n - 1)
                for k in range(4):
                    i = 4 * n + k
                    last = turn(ps[n % 2][:, k * P:(k + 1) * P], t_tok[:, 2 * i:2 * i + 2, :].rearrange("p a c -> p (a c)"))
                last.then_inc(out_turned, 1)

        @block.scalar
        def _(act):
            act.wait_ge(alpha_exp_in, 1)
            nc.scalar.activation(alph[0:CH, 8:13], alph[0:CH, 0:5], ACT.Exp).then_inc(alpha_exp, 1)
            act.wait_ge(gn_ready, 1)
            nc.scalar.activation(gn_rstd, gn_rstd, ACT.Sqrt).then_inc(gn_root, 1)
            act.wait_ge(gn_ready, 2)
            act.wait_ge(border_set, 1)
            act.wait_ge(x_in, 32)
            for j in range(HALF):
                nc.scalar.activation(y_pad[:, j, 1:1 + SIDE, 1:1 + SIDE], x_ch[:, j, :].rearrange("p (y x) -> p y x", x=SIDE),
                                     ACT.Identity, bias=gn_bias[:, j:j + 1], scale=gn_rstd[:, j:j + 1]).then_inc(y_ready, 1)

            def sort_flips(steps, key, banks_done):
                n = banks_done
                for what, src, dst in steps:
                    if what[0] != "flip":
                        continue
                    for bank in range(key[0].shape[1] // 512):
                        n += 1
                        act.wait_ge(flip_done, n)
                        nc.scalar.copy(key[dst][:, bank * 512:(bank + 1) * 512], ps[bank][:, :]).then_inc(flip_taken, 1)

            sort_flips(A_STEPS, a_key, 0)
            for j in range(HALF // 2):
                act.wait_ge(t_turned, j + 1)
                nc.scalar.copy(t_tok[:, 8 * j:8 * j + 8, :].rearrange("p i c -> p (i c)"), ps[6 + j % 2][:, :]).then_inc(t_taken, 1)
            act.wait_ge(root_in, 1)
            nc.scalar.activation(ln_var, ln_var, ACT.Sqrt).then_inc(root_out, 1)
            sort_flips(G_STEPS, g_key, A_FLIPS * (A_W // 512))

            def a_chunk(it, b, first):
                c1 = it * 2 + (b + 1)
                act.wait_ge(a_seed_in[b], it * 16 + 16)
                act.wait_ge(a_flags, c1)
                by_f = q_fm.rearrange("p (f j) -> p f j", j=A_RUN)
                nc.scalar.copy(by_f[:, :, 1:], q_seed[b].rearrange("p j f -> p f j")[:, :, 1:])
                nc.scalar.copy(a_go.rearrange("p (f j) -> p f j", j=A_RUN), bc(a_nst[:, None, :], [P, A_F, A_RUN]))
                act.wait_ge(kv_in[b], it * (16 * (A_RUN + 1)) + 16 * (A_RUN + 1))
                nc.scalar.copy(by_f[:, :, 0], q_first[b]).then_inc(a_laid, 1)
                act.wait_ge(a_scored, c1)
                nc.scalar.activation(a_msg[:, CH * A_RUN:], a_score, ACT.Exp).then_inc(a_weighed, 1)
                act.wait_ge(a_summed, c1)
                if not first:
                    act.wait_ge(a_rows_out[b], it * 16)
                nc.scalar.copy(a_rows[b].rearrange("p j f -> p f j"), a_sum.rearrange("p (f j) -> p f j", j=A_RUN)).then_inc(a_rows_set, 1)

            for b in range(2):
                a_chunk(0, b, True)
            with act.Fori(1, A_CHUNKS // 2) as it:
                for b in range(2):
                    a_chunk(it, b, False)

            for n in range(A_CHUNKS // 4):
                act.wait_ge(a_tail_turned, n + 1)
                nc.scalar.copy(a_tailT[0:A_F, n * 512:(n + 1) * 512], ps[4 + n % 2][0:A_F, :]).then_inc(a_tail_taken, 1)
            for n in range(A_CHUNKS // 4):
                act.wait_ge(a_car_turned, n + 1)
                nc.scalar.copy(a_car[:, 4 * n:4 * n + 4, :].rearrange("p c f -> p (c f)"), ps[6 + n % 2][:, 0:4 * A_F]).then_inc(a_car_taken, 1)

            act.wait_ge(root_in, 2)
            nc.scalar.activation(ln_var, ln_var, ACT.Sqrt).then_inc(root_out, 1)
            for n in range(8):
                act.wait_ge(yT_turned, n + 1)
                nc.scalar.copy(yT[:, 4 * n:4 * n + 4, :].rearrange("p i n -> p (i n)"), ps[n % 2][:, :]).then_inc(yT_taken, 1)
            act.wait_ge(gw_in, 16 * 12)
            for n in range(64):
                act.wait_ge(hid_done, n + 1)
                if n >= 2:
                    act.wait_ge(hid_used, n - 1)
                nc.scalar.activation(hid[n % 2], ps[4 + n % 2][:, :], ACT.Gelu, bias=b1[:, n % 4:n % 4 + 1]).then_inc(hid_set, 1)

            def g_chunk(it, b, first):
                c1 = it * 2 + (b + 1)
                act.wait_ge(g_idx_in[b], it * 64 + 64)
                act.wait_ge(g_flags, c1)
                by_f = ad_fm.rearrange("p (f j) -> p f j", j=G_RUN)
                nc.scalar.copy(by_f[:, :, 1:], ad_seed[b].rearrange("p j f -> p f j")[:, :, 1:])
                act.wait_ge(hs_in[b], it * (16 * (G_RUN + 1)) + 16 * (G_RUN + 1))
                nc.scalar.copy(by_f[:, :, 0], ad_first[b]).then_inc(g_laid, 1)
                act.wait_ge(g_max_set, c1)
                nc.scalar.activation(g_msg[:, G_HF * G_RUN:], g_em, ACT.Exp).then_inc(g_exp_done, 1)
                nc.scalar.activation(g_corr_f[:, G_HF * G_RUN:], g_dm, ACT.Exp).then_inc(g_exp_done, 1)
                act.wait_ge(g_exp_done, it * 4 + (2 * b + 2))
                nc.scalar.copy(g_corr_f[:, 0:G_HF * G_RUN].rearrange("p (h k j) -> p h k j", h=G_HEADS, j=G_RUN),
                               bc(g_corr_f[:, G_HF * G_RUN:].rearrange("p (h j) -> p h j", j=G_RUN)[:, :, None, :],
                                  [P, G_HEADS, G_EXP, G_RUN])).then_inc(g_weighed, 1)
                act.wait_ge(g_summed, c1)
                if not first:
                    act.wait_ge(g_rows_out[b], it * 16)
                rows_f = g_rows[b].rearrange("p j f -> p f j")
                nc.scalar.copy(rows_f[:, 0:G_F], g_sum.rearrange("p (f j) -> p f j", j=G_RUN))
                nc.scalar.copy(rows_f[:, G_F:], g_max[:, 1:].rearrange("p (f j) -> p f j", j=G_RUN)).then_inc(g_rows_set, 1)

            for b in range(2):
                g_chunk(0, b, True)
            with act.Fori(1, G_CHUNKS // 2) as it:
                for b in range(2):
                    g_chunk(it, b, False)

            for n in range(G_CHUNKS // 4):
                act.wait_ge(g_tail_turned, n + 1)
                nc.scalar.copy(g_tailT[0:G_F, n * 512:(n + 1) * 512], ps[4][0:G_F, :]).then_inc(g_tail_taken, 1)
                nc.scalar.copy(g_tmaxT[0:G_F, n * 512:(n + 1) * 512], ps[5][0:G_F, :]).then_inc(g_tail_taken, 1)
            for k in range(2):
                act.wait_ge(g_dT_set, k + 1)
                tgt = (g_dT, g_tmaxT)[k]
                nc.scalar.activation(tgt[0:G_F, :], tgt[0:G_F, :], ACT.Exp).then_inc(g_dT_exp, 1)
            for n in range(G_CHUNKS // 4):
                act.wait_ge(g_car_turned, n + 1)
                nc.scalar.copy(g_tail[:, 4 * n:4 * n + 4, 0:G_F],
                               ps[6][:, 0:4 * G_F].rearrange("p (c f) -> p c f", f=G_F)).then_inc(g_car_taken, 1)
                nc.scalar.copy(g_tail[:, 4 * n:4 * n + 4, G_F:G_OUT],
                               ps[7][:, 0:4 * G_F].rearrange("p (c f) -> p c f", f=G_F)[:, :, G_HF:]).then_inc(g_car_taken, 1)
            act.wait_ge(node_exp_in, 1)
            for k in range(3):
                nc.scalar.activation(n4[4 + k], n4[4 + k], ACT.Exp).then_inc(node_exp, 1)
            act.wait_ge(gate_root_in, 1)
            nc.scalar.activation(ln_var, ln_var, ACT.Sqrt).then_inc(gate_root, 1)
            act.wait_ge(gate_exp_in, 1)
            nc.scalar.activation(n4[8], n4[8], ACT.Exp).then_inc(gate_exp, 1)
            for n in range(8):
                act.wait_ge(out_turned, n + 1)
                nc.scalar.copy(out_ch[:, 2 * n:2 * n + 2, :].rearrange("p j s -> p (j s)"), ps[n % 2][:, :]).then_inc(out_laid, 1)

        @block.vector
        def _(dve):
            V = nc.vector
            done = [0]

            def step(ins):
                done[0] += 1
                ins.then_inc(dve_step, 1)
                dve.wait_ge(dve_step, done[0])

            def tt(o, a_, b_, op):
                return V.tensor_tensor(o, a_, b_, op)

            def ts(o, a_, s1, op0, s2=None, op1=None):
                return V.tensor_scalar(o, a_, s1, s2, op0, op1) if op1 is not None else V.tensor_scalar(o, a_, s1, None, op0)

            step(V.memset(ones, 1.0))
            dve.wait_ge(x_in, 32)
            for j in range(HALF):
                ins = V.bn_stats(gn_stat[:, j, :], x_ch[:, j, :])
            step(ins)
            for j in range(HALF):
                ins = V.bn_aggr(gn_mv[:, j, :], gn_stat[:, j, :])
            step(ins)
            V.tensor_copy(gn_mean, gn_mv[:, :, 0]).then_inc(gn_pair_in, 1)
            dve.wait_ge(gn_pair, 1)
            step(tt(gn_dev, gn_mv[:, :, 0], ps[7][:, 0:HALF], ALU.subtract))
            step(tt(gn_dev, gn_dev, gn_dev, ALU.mult))
            tt(gn_dev, gn_dev, gn_mv[:, :, 1], ALU.add).then_inc(gn_pair_in, 1)
            dve.wait_ge(gn_pair, 2)
            ts(gn_rstd, ps[7][:, 32:32 + HALF], 1e-5, ALU.add).then_inc(gn_ready, 1)
            dve.wait_ge(w_in, 16 * 10)
            dve.wait_ge(perm_in, 16)
            al = alph[0:CH]
            step(V.tensor_reduce(al[:, 13:14], al[:, 0:5], AX_X, ALU.max))
            ts(al[:, 0:5], al[:, 0:5], al[:, 13:14], ALU.subtract).then_inc(alpha_exp_in, 1)
            dve.wait_ge(alpha_exp, 1)
            step(V.tensor_reduce(al[:, 14:15], al[:, 8:13], AX_X, ALU.add))
            step(V.reciprocal(al[:, 15:16], al[:, 14:15]))
            step(ts(al[:, 0:5], al[:, 8:13], al[:, 15:16], ALU.mult))
            ts(perm[0:CH, 0, :], perm[0:CH, 0, :], al[:, 0:1], ALU.mult)
            n = 1
            for m, bs in enumerate(BLOCKS):
                ins = ts(perm[0:CH, n:n + bs, :], perm[0:CH, n:n + bs, :], al[:, m + 1:m + 2], ALU.mult, 1.0 / bs, ALU.mult)
                n += bs
            step(ins)
            V.memset(w_taps, 0.0).then_inc(perm_scaled, 1)
            dve.wait_ge(gn_root, 1)
            step(V.reciprocal(gn_rstd, gn_rstd))
            V.scalar_tensor_tensor(gn_bias, ps[7][:, 0:HALF], -1.0, gn_rstd, ALU.mult, ALU.mult).then_inc(gn_ready, 1)
            dve.wait_ge(w_mixed, 2)
            for part in range(2):
                for half in range(2):
                    at = slice(half * CH, (half + 1) * CH)
                    o = half * CH + part * 32
                    ins = V.tensor_copy(w_taps[at, :, o:o + 32], ps[4 + part][at, 0:288].rearrange("p (o t) -> p t o", t=TAPS))
            ins.then_inc(w_ready, 1)

            def sort(steps, key, flips):
                taken = flips[0]
                for what, src, dst in steps:
                    s, d = key[src], key[dst]
                    if what[0] == "toggle":
                        step(ts(d, s, const[:, C_TOGGLE + what[1]:C_TOGGLE + what[1] + 1], ALU.mult))
                    elif what[0] == "flip":
                        dve.sem_inc(flip_in, 1)
                        taken += key[0].shape[1] // 512
                        dve.wait_ge(flip_taken, taken)
                    else:
                        k, dist = what[1:]
                        if k is None:
                            sv = s.rearrange("p (a h d) -> p a h d", h=2, d=dist)
                            dv = d.rearrange("p (a h d) -> p a h d", h=2, d=dist)
                            tt(dv[:, :, 0], sv[:, :, 0], sv[:, :, 1], ALU.min)
                            step(tt(dv[:, :, 1], sv[:, :, 0], sv[:, :, 1], ALU.max))
                        else:
                            pat = "p (a s b h d) -> p a s b h d"
                            b_ = (1 << k) // (2 * dist)
                            sv = s.rearrange(pat, s=2, b=b_, h=2, d=dist)
                            dv = d.rearrange(pat, s=2, b=b_, h=2, d=dist)
                            for way in range(2):
                                lo, hi = sv[:, :, way, :, 0], sv[:, :, way, :, 1]
                                tt(dv[:, :, way, :, 0], lo, hi, (ALU.min, ALU.max)[way])
                                ins_ = tt(dv[:, :, way, :, 1], lo, hi, (ALU.max, ALU.min)[way])
                            step(ins_)
                flips[0] = taken

            def pack(key, cols, n_src):
                s, d = key[0][:, 0:cols].bitcast(I32), key[1][:, 0:cols].bitcast(I32)
                step(ts(s, s, float(n_src - 1), ALU.min, 0.0, ALU.max))
                step(ts(d, d, float(NONE), ALU.min, 0.0, ALU.max))
                step(ts(d, d, SRC_BITS, ALU.logical_shift_left, KEY_BASE, ALU.bitwise_or))
                step(tt(s, s, d, ALU.bitwise_or))

            def unpack(key, last, extra):
                k_, o_ = key[last].bitcast(I32), key[1 - last].bitcast(I32)
                step(ts(o_, k_, (1 << SRC_BITS) - 1, ALU.bitwise_and))
                step(ts(k_, k_, SRC_BITS, ALU.logical_shift_right, (1 << 14) - 1, ALU.bitwise_and))
                return ts(extra, k_, float(TOKENS - 1), ALU.min)

            def runs(key, run, k):
                d_ = key.bitcast(I32)
                n_ = key.shape[1] // run
                head = d_.rearrange("p (n j) -> p n j", j=run)[:, :, 0]
                tail = d_.rearrange("p (n j) -> p n j", j=run)[:, :, run - 1]
                V.tensor_copy(run_prev[:, 1:n_], tail[:, 0:n_ - 1])
                V.tensor_copy(ln_sum[:, 0:1], tail[:, n_ - 1:n_]).then_inc(last_set, 1)
                dve.wait_ge(last_shifted, k)
                step(V.tensor_copy(run_prev[:, 0:1], ps[7][:, 0:1]))
                step(tt(run_cont[:, 0:n_], head, run_prev[:, 0:n_], ALU.is_equal))
                step(tt(run_prev[:, 0:n_], head, tail, ALU.is_equal))
                step(tt(run_cont[:, 0:n_], run_cont[:, 0:n_], run_prev[:, 0:n_], ALU.mult))
                dve.sem_inc(cont_set, 1)

            def search_rows(key, nodes, k):
                nb = key.shape[1] // P
                p_ = key.bitcast(I32).rearrange("p (n j) -> p n j", j=P)[:, :, 0]
                step(ts(piv[0][:, 0:nb], p_, P - 1, ALU.bitwise_and))
                step(ts(piv[1][:, 0:nb], p_, 7, ALU.logical_shift_right))
                tt(hot_lo[:, 0:nb, :], bc(piv[0][:, 0:nb, None], [P, nb, P]), bc(iota[:, None, :], [P, nb, P]), ALU.is_equal)
                step(tt(hot_hi[:, 0:nb, :], bc(piv[1][:, 0:nb, None], [P, nb, NT]), bc(iota[:, None, 0:NT], [P, nb, NT]), ALU.is_equal))
                dve.sem_inc(hot_set, 1)
                dve.wait_ge(hist_done, k)
                step(V.tensor_copy(nodes.tot, ps[4][:, 0:NT]))
                dve.sem_inc(hist_set, 1)
                dve.wait_ge(cum_done, k)
                step(V.tensor_copy(nodes.count, ps[6][:, 0:NT]))
                step(V.tensor_tensor_scan(nodes.start, ones[:, 0:NT], nodes.count, 0.0, ALU.mult, ALU.add))
                step(tt(nodes.run, nodes.start, nodes.count, ALU.subtract))
                step(tt(nodes.run, nodes.run, ps[5][:, 0:NT], ALU.add))
                step(ts(nodes.run, nodes.run, -1.0, ALU.add, 0.0, ALU.max))
                step(V.tensor_copy(nodes.run_i, nodes.run))
                dve.sem_inc(run_set, 1)

            def search_ends(nodes, k, run, rows, below):
                for n_ in range(4):
                    at = slice(16 * n_, 16 * n_ + 16)
                    dve.wait_ge(found[k - 1][n_], 256)
                    step(tt(below, rows[:, at, :], bc(node[:, at, None], [P, 16, P]), ALU.is_le))
                    step(V.tensor_reduce(nodes.count[:, at], below, AX_X, ALU.add))
                V.memset(nodes.end[:, 0:1], 0.0)
                step(V.scalar_tensor_tensor(nodes.end[:, 1:], nodes.run, float(P), nodes.count, ALU.mult, ALU.add))
                dve.sem_inc(ends_set, 1)
                dve.wait_ge(starts_done, k)
                end = nodes.end[:, 1:]
                step(V.tensor_copy(nodes.start, ps[5][:, 0:NT]))
                step(tt(nodes.has, end, nodes.start, ALU.is_gt))
                step(ts(nodes.pos, end, -1.0, ALU.add, 0.0, ALU.max))
                step(ts(nodes.prun, nodes.pos, run.bit_length() - 1, ALU.logical_shift_right))
                step(ts(nodes.cidx_f, nodes.prun, float(run), ALU.mult))
                step(tt(nodes.carried, nodes.start, nodes.cidx_f, ALU.is_lt))
                step(tt(nodes.carried, nodes.carried, nodes.has, ALU.mult))
                step(ts(nodes.cidx, nodes.prun, -1.0, ALU.add, 0.0, ALU.max))
                step(ts(nodes.seed_f, nodes.has, -FAR, ALU.mult, FAR, ALU.add))
                step(tt(nodes.seed, nodes.seed_f, nodes.start, ALU.add))
                dve.sem_inc(pos_set, 1)

            def layer_norm(k, eps, square_):
                step(V.tensor_reduce(ln_sum, t_tok, AX_X, ALU.add))
                step(ts(ln_sum, ln_sum, 1.0 / CH, ALU.mult))
                step(tt(y_tok, t_tok, bc(ln_sum[:, :, None], [P, NT, CH]), ALU.subtract))
                for n_ in range(2):
                    part = slice(n_ * NT // 2, (n_ + 1) * NT // 2)
                    step(tt(square_, y_tok[:, part], y_tok[:, part], ALU.mult))
                    step(V.tensor_reduce(ln_var[:, part], square_, AX_X, ALU.add))
                step(ts(ln_var, ln_var, 1.0 / CH, ALU.mult, eps, ALU.add))
                dve.sem_inc(root_in, 1)
                dve.wait_ge(root_out, k)
                step(V.reciprocal(ln_var, ln_var))
                step(tt(y_tok, y_tok, bc(ln_var[:, :, None], [P, NT, CH]), ALU.mult))
                dve.sem_inc(y_set, 1)

            flips = [0]
            dve.wait_ge(a_edges_in, 32)
            pack(a_key, A_EDGES // P, A_NODES)
            step(V.memset(a_key[0][:, A_EDGES // P:].bitcast(I32), PAD_KEY))
            dve.wait_ge(const_in, 16)
            sort(A_STEPS, a_key, flips)
            step(unpack(a_key, A_LAST, list_nodes[:, 0:A_W]))
            dve.sem_inc(a_list_set, 1)
            runs(a_key[A_LAST], A_RUN, 1)
            search_rows(a_key[A_LAST], a_nodes, 1)

            for j in range(HALF // 2):
                dve.wait_ge(conv_done, j + 1)
                xs = x_ch[:, 2 * j:2 * j + 2, :].rearrange("p j s -> p (j s)")
                tt(xs, xs, ps[4 + j % 2][:, :], ALU.add).then_inc(conv_added, 1)
            search_ends(a_nodes, 1, A_RUN, a_found, a_below)
            dve.wait_ge(t_taken, HALF // 2)
            layer_norm(1, 1e-5, square_a)

            dve.wait_ge(g_edges_in, 32)
            pack(g_key, G_W, TOKENS)
            sort(G_STEPS, g_key, flips)
            dve.wait_ge(q_out, 32)
            dve.wait_ge(q_scattered, 16 * NT)
            step(unpack(g_key, G_LAST, list_nodes))
            dve.sem_inc(g_list_set, 1)
            dve.wait_ge(cont_out, 16)
            runs(g_key[G_LAST], G_RUN, 2)
            search_rows(g_key[G_LAST], g_nodes, 2)

            A_STEPS_DVE = 6
            step(V.memset(a_nst[:, 0:1], 0.0))

            def a_chunk(it, b, first):
                n_done = [0]

                def link(ins):
                    n_done[0] += 1
                    ins.then_inc(dve_loop_a, 1)
                    dve.wait_ge(dve_loop_a, it * (2 * A_STEPS_DVE) + (b * A_STEPS_DVE + n_done[0]))

                c1 = it * 2 + (b + 1)
                dve.wait_ge(a_idx_in[b], it * 48 + 48)
                tt(a_nst[:, 1:], a_didx[b][:, 1:], a_didx[b][:, :-1], ALU.is_equal).then_inc(a_flags, 1)
                dve.wait_ge(a_laid, c1)
                link(V.tensor_tensor_scan(q_edge, a_go[:, 0:CH * A_RUN], q_fm, 0.0, ALU.mult, ALU.add))
                k_f = kv[b][:, :, 0:CH].rearrange("p j f -> p f j")
                link(tt(a_prod.rearrange("p (f j) -> p f j", j=A_RUN), q_edge.rearrange("p (f j) -> p f j", j=A_RUN), k_f, ALU.mult))
                link(V.tensor_reduce(a_score.rearrange("p (h j) -> p h j", j=A_RUN),
                                     a_prod.rearrange("p (h d j) -> p h j d", d=A_DIM, j=A_RUN), AX_X, ALU.add))
                link(ts(a_score, a_score, A_DIM ** -0.5, ALU.mult, -5.0, ALU.max))
                ts(a_score, a_score, 5.0, ALU.min).then_inc(a_scored, 1)
                dve.wait_ge(a_weighed, c1)
                w = a_msg[:, CH * A_RUN:].rearrange("p (h j) -> p h j", j=A_RUN)
                link(tt(a_msg[:, 0:CH * A_RUN].rearrange("p (h d j) -> p h d j", d=A_DIM, j=A_RUN),
                        kv[b][:, :, CH:].rearrange("p j (h d) -> p h d j", d=A_DIM),
                        bc(w[:, :, None, :], [P, A_HEADS, A_DIM, A_RUN]), ALU.mult))
                dve.sem_inc(a_used, 1)
                if not first:
                    dve.wait_ge(a_rows_set, c1 - 1)
                link(V.tensor_tensor_scan(a_sum, a_go, a_msg, 0.0, ALU.mult, ALU.add))
                dve.sem_inc(a_summed, 1)
                assert n_done[0] == A_STEPS_DVE

            for b in range(2):
                a_chunk(0, b, b == 0)
            with dve.Fori(1, A_CHUNKS // 2) as it:
                for b in range(2):
                    a_chunk(it, b, False)

            dve.wait_ge(a_tail_taken, A_CHUNKS // 4)
            dve.wait_ge(a_tail_in, 32)
            step(V.tensor_tensor_scan(a_carT[0:A_F], a_cont[0:A_F], a_tailT[0:A_F], 0.0, ALU.mult, ALU.add))
            dve.sem_inc(a_carried, 1)
            dve.wait_ge(a_ends_in, 16 * 2 * NT)
            tt(a_before, a_before, bc(a_nodes.carried[:, :, None], [P, NT, A_F]), ALU.mult)
            step(tt(a_end, a_end, bc(a_nodes.has[:, :, None], [P, NT, A_F]), ALU.mult))
            step(tt(a_end, a_end, a_before, ALU.add))
            z = a_end[:, :, CH:]
            step(ts(z, z, 1e-6, ALU.add))
            step(V.reciprocal(z, z))
            wv = a_end[:, :, 0:CH].rearrange("p i (h d) -> p i h d", d=A_DIM)
            step(tt(wv, wv, bc(z[:, :, :, None], [P, NT, A_HEADS, A_DIM]), ALU.mult))
            step(tt(t_tile, t_tile, a_end[:, :, 0:CH].rearrange("p (h i) c -> p h i c", h=2), ALU.add))
            dve.wait_ge(g_list_out, 48)
            layer_norm(2, 1e-5, square)

            dve.wait_ge(gw_in, 16 * 12)
            dve.wait_ge(h_done, 1)
            for half in range(2):
                V_last = V.tensor_copy(h_tok[:, half * 32:half * 32 + 32, 0:G_HF], ps[2 + half][:, :].rearrange("p (i f) -> p i f", f=G_HF))
            step(V_last)
            hh = h_tok[:, :, 0:G_HF]
            prod = h_prod.rearrange("p i h k -> p i (h k)")
            step(tt(prod, hh, bc(att[:, 0:1, :], [P, NT, G_HF]), ALU.mult))
            step(V.tensor_reduce(h_tok[:, :, G_HF:], h_prod, AX_X, ALU.add))
            step(tt(prod, hh, bc(att[:, 1:2, :], [P, NT, G_HF]), ALU.mult))
            step(V.tensor_reduce(ad_tok, h_prod, AX_X, ALU.add))
            dve.sem_inc(h_set, 1)
            search_ends(g_nodes, 2, G_RUN, g_found, g_below)
            for grp in range(16):
                dve.wait_ge(hid_used, 4 * grp + 4)
                i0 = grp // 8 * 32 + grp % 8 * 4
                for k in range(2):
                    ins = tt(exp_out[:, i0 + 2 * k:i0 + 2 * k + 2, :], ps[6 + k][:, :].rearrange("p (i n) -> p i n", n=4 * CH),
                             bc(b2[:, None, :], [P, 2, 4 * CH]), ALU.add)
                ins.then_inc(exp_taken, 1)

            G_STEPS_DVE = 9
            V.memset(g_max[:, 0:1], 0.0)
            step(V.memset(g_nst.rearrange("p (h j) -> p h j", j=G_RUN)[:, :, 0:1], 0.0))

            def g_chunk(it, b, first):
                n_done = [0]

                def link(ins):
                    n_done[0] += 1
                    ins.then_inc(dve_loop_g, 1)
                    dve.wait_ge(dve_loop_g, it * (2 * G_STEPS_DVE) + (b * G_STEPS_DVE + n_done[0]))

                c1 = it * 2 + (b + 1)
                dve.wait_ge(g_idx_in[b], it * 64 + 64)
                n_ = G_RUN - 1
                link(tt(g_nst.rearrange("p (h j) -> p h j", j=G_RUN)[:, :, 1:], bc(g_didx[b][:, None, 1:], [P, G_HEADS, n_]),
                        bc(g_didx[b][:, None, :-1], [P, G_HEADS, n_]), ALU.is_equal))
                ts(g_cut, g_nst, BIG, ALU.mult, -BIG, ALU.add).then_inc(g_flags, 1)
                dve.wait_ge(g_laid, c1)
                link(V.tensor_tensor_scan(ad_edge, g_nst, ad_fm, 0.0, ALU.mult, ALU.add))
                hs_f = hs[b].rearrange("p j f -> p f j")
                link(tt(g_x.rearrange("p (h j) -> p h j", j=G_RUN), ad_edge.rearrange("p (h j) -> p h j", j=G_RUN), hs_f[:, G_HF:], ALU.add))
                link(V.scalar_tensor_tensor(g_e, g_x, 0.2, g_x, ALU.mult, ALU.max))
                if not first:
                    dve.wait_ge(g_rows_set, c1 - 1)
                link(V.tensor_tensor_scan(g_max[:, 1:], g_cut, g_e, 0.0, ALU.add, ALU.max))
                tt(g_em, g_e, g_max[:, 1:], ALU.subtract)
                link(tt(g_dm, g_max[:, :-1], g_max[:, 1:], ALU.subtract))
                link(tt(g_dm, g_dm, g_cut, ALU.add))
                dve.sem_inc(g_max_set, 1)
                dve.wait_ge(g_weighed, c1)
                w = g_msg[:, G_HF * G_RUN:].rearrange("p (h j) -> p h j", j=G_RUN)
                link(tt(g_msg[:, 0:G_HF * G_RUN].rearrange("p (h k j) -> p h k j", k=G_EXP, j=G_RUN),
                        hs[b][:, :, 0:G_HF].rearrange("p j (h k) -> p h k j", k=G_EXP),
                        bc(w[:, :, None, :], [P, G_HEADS, G_EXP, G_RUN]), ALU.mult))
                dve.sem_inc(g_used, 1)
                link(V.tensor_tensor_scan(g_sum, g_corr_f, g_msg, 0.0, ALU.mult, ALU.add))
                dve.sem_inc(g_summed, 1)
                assert n_done[0] == G_STEPS_DVE

            for b in range(2):
                g_chunk(0, b, b == 0)
            with dve.Fori(1, G_CHUNKS // 2) as it:
                for b in range(2):
                    g_chunk(it, b, False)

            dve.wait_ge(g_tail_in, 32)
            m_tail = g_tail[:, :, G_F:G_OUT]
            V.tensor_copy(g_tail[:, :, G_OUT:G_OUT + G_HF].rearrange("p c (h k) -> p c h k", k=G_EXP),
                          bc(m_tail[:, :, :, None], [P, G_CHUNKS, G_HEADS, G_EXP]))
            step(V.tensor_copy(g_tail[:, :, G_OUT + G_HF:], m_tail))
            dve.sem_inc(g_rep_set, 1)
            cut, tmax, cmax, d_t, tail = (x[0:G_F] for x in (g_cutT, g_tmaxT, g_cmaxT, g_dT, g_tailT))
            step(ts(cut, cut, BIG, ALU.mult, -BIG, ALU.add))
            dve.wait_ge(g_tail_taken, G_CHUNKS // 2)
            V.memset(cmax[:, 0:1], -BIG)
            step(V.tensor_tensor_scan(cmax[:, 1:], cut, tmax, -BIG, ALU.add, ALU.max))
            step(tt(d_t, cmax[:, :-1], cmax[:, 1:], ALU.subtract))
            step(tt(d_t, d_t, cut, ALU.add))
            dve.sem_inc(g_dT_set, 1)
            step(tt(tmax, tmax, cmax[:, 1:], ALU.subtract))
            dve.sem_inc(g_dT_set, 1)
            dve.wait_ge(g_dT_exp, 2)
            step(tt(tail, tail, tmax, ALU.mult))
            step(V.tensor_tensor_scan(cut, d_t, tail, 0.0, ALU.mult, ALU.add))
            dve.sem_inc(g_carried, 1)

            dve.wait_ge(g_ends_in, 16 * 2 * NT)
            m_end, m_before, e_own, m_all, w_end, w_before, w_own_, sc, ex, rank, cmp_, den = n4
            step(tt(den, h_tok[:, :, G_HF:], ad_tok, ALU.add))
            step(V.scalar_tensor_tensor(e_own, den, 0.2, den, ALU.mult, ALU.max))
            for m_, rows_, on in ((m_end, g_end, g_nodes.has), (m_before, g_before, g_nodes.carried)):
                step(ts(g_nodes.tot, on, BIG, ALU.mult, -BIG, ALU.add))
                step(tt(m_, rows_[:, :, G_F:], bc(on[:, :, None], [P, NT, 4]), ALU.mult))
                step(tt(m_, m_, bc(g_nodes.tot[:, :, None], [P, NT, 4]), ALU.add))
            step(tt(m_all, m_end, m_before, ALU.max))
            step(tt(m_all, m_all, e_own, ALU.max))
            for w_, m_ in ((w_end, m_end), (w_before, m_before), (w_own_, e_own)):
                ins = tt(w_, m_, m_all, ALU.subtract)
            step(ins)
            dve.sem_inc(node_exp_in, 1)
            dve.wait_ge(node_exp, 3)
            agg = n16[0].rearrange("p (i h k) -> p i h k", h=4, k=4)
            part = n16[1].rearrange("p (i h k) -> p i h k", h=4, k=4)

            def heads(x):
                return x.rearrange("p i (h k) -> p i h k", k=4)

            def per_head(x):
                return bc(x[:, :, :, None], [P, NT, 4, 4])

            step(tt(agg, heads(g_end[:, :, 0:G_HF]), per_head(w_end), ALU.mult))
            step(tt(part, heads(g_before[:, :, 0:G_HF]), per_head(w_before), ALU.mult))
            step(tt(n16[0], n16[0], n16[1], ALU.add))
            step(tt(part, heads(h_tok[:, :, 0:G_HF]), per_head(w_own_), ALU.mult))
            step(tt(n16[0], n16[0], n16[1], ALU.add))
            step(tt(den, g_end[:, :, G_HF:G_F], w_end, ALU.mult))
            step(tt(cmp_, g_before[:, :, G_HF:G_F], w_before, ALU.mult))
            step(tt(den, den, cmp_, ALU.add))
            step(tt(den, den, w_own_, ALU.add))
            step(ts(den, den, 1e-16, ALU.add))
            step(V.reciprocal(den, den))
            step(tt(agg, agg, per_head(den), ALU.mult))
            flat = n16[0].rearrange("p (i f) -> p i f", f=G_HF)

            def all_nodes(v):
                return bc(att[:, v:v + 1, :], [P, NT, G_HF])

            step(tt(flat, flat, all_nodes(2), ALU.add))
            step(V.tensor_reduce(ln_sum, flat, AX_X, ALU.add))
            step(ts(ln_sum, ln_sum, 1.0 / G_HF, ALU.mult))
            step(tt(flat, flat, bc(ln_sum[:, :, None], [P, NT, G_HF]), ALU.subtract))
            sq = n16[1].rearrange("p (i f) -> p i f", f=G_HF)
            step(tt(sq, flat, flat, ALU.mult))
            step(V.tensor_reduce(ln_var, sq, AX_X, ALU.add))
            step(ts(ln_var, ln_var, 1.0 / G_HF, ALU.mult, 1e-5, ALU.add))
            dve.sem_inc(gate_root_in, 1)
            dve.wait_ge(gate_root, 1)
            step(V.reciprocal(ln_var, ln_var))
            step(tt(flat, flat, bc(ln_var[:, :, None], [P, NT, G_HF]), ALU.mult))
            step(tt(flat, flat, all_nodes(3), ALU.mult))
            step(tt(flat, flat, all_nodes(4), ALU.add))
            step(V.tensor_reduce(sc, n16[0].rearrange("p (i h k) -> p i k h", h=4, k=4), AX_X, ALU.add))
            step(ts(sc, sc, 1.0 / G_HEADS, ALU.mult))
            step(V.memset(rank, 0.0))
            for j in range(4):
                if j < 3:
                    tt(cmp_[:, :, j + 1:], bc(sc[:, :, j:j + 1], [P, NT, 3 - j]), sc[:, :, j + 1:], ALU.is_ge)
                step(tt(cmp_[:, :, 0:j + 1], bc(sc[:, :, j:j + 1], [P, NT, j + 1]), sc[:, :, 0:j + 1], ALU.is_gt))
                step(tt(rank, rank, cmp_, ALU.add))
            step(ts(rank, rank, 2.0, ALU.is_lt))
            step(V.tensor_reduce(ln_sum, sc, AX_X, ALU.max))
            step(tt(ex, sc, bc(ln_sum[:, :, None], [P, NT, 4]), ALU.subtract))
            dve.sem_inc(gate_exp_in, 1)
            dve.wait_ge(gate_exp, 1)
            step(tt(ex, ex, rank, ALU.mult))
            step(V.tensor_reduce(ln_sum, ex, AX_X, ALU.add))
            step(V.reciprocal(ln_sum, ln_sum))
            step(tt(ex, ex, bc(ln_sum[:, :, None], [P, NT, 4]), ALU.mult))
            eo = exp_out.rearrange("p i (e c) -> p (i e) c", c=CH)
            step(tt(eo, eo, bc(ex.rearrange("p i e -> p (i e)")[:, :, None], [P, NT * 4, CH]), ALU.mult))
            for e in range(4):
                step(tt(t_tile, t_tile, exp_out[:, :, e * CH:(e + 1) * CH].rearrange("p (h i) c -> p h i c", h=2), ALU.add))
            dve.sem_inc(out_set, 1)


OUT_SHAPE = (IMAGES, CH, SIDE, SIDE)


def kernel(debug=None, **inputs):
    import concourse.bacc as bacc
    from concourse.bass_utils import run_bass_kernel_spmd

    def given(name, shape=None):
        a = np.ascontiguousarray(inputs[name])
        return a.reshape(shape) if shape else a

    w = given("L0_conv_weight", (CH, CH, TAPS))
    const, perm = shape_constants()
    arrays = {
        "x": given("x", (IMAGES, CH, PIX)),
        "alphas": given("L0_conv_alphas"),
        "w_own": np.ascontiguousarray(w.transpose(1, 0, 2)).reshape(CH, CH * TAPS),
        "w_blocks": np.stack([np.ascontiguousarray(
            w.reshape(CH // bs, bs, CH // bs, bs, TAPS).transpose(2, 1, 0, 3, 4)).reshape(CH, CH * TAPS) for bs in BLOCKS]),
        "kv": np.concatenate([given("L1_attn_k", (A_NODES, CH)), given("L1_attn_v", (A_NODES, CH))], axis=1),
        "a_edges": given("L1_attn_edge_index"),
        "g_edges": given("L1_ffn_edge_index"),
        "wgat": given("L1_ffn_W_gat"), "att_src": given("L1_ffn_att_src", (G_HF,)), "att_dst": given("L1_ffn_att_dst", (G_HF,)),
        "b_gat": given("L1_ffn_b_gat"), "gamma": given("L1_ffn_ln_gamma"), "beta": given("L1_ffn_ln_beta"),
        "w1": given("L1_ffn_W1"), "b1": np.ascontiguousarray(given("L1_ffn_b1").T), "w2": given("L1_ffn_W2"), "b2": given("L1_ffn_b2"),
        "const": const, "perm": perm,
    }
    nc = bacc.Bacc("TRN2", target_bir_lowering=False, num_devices=1)
    io = {n: nc.dram_tensor(f"in_{n}", a.shape, mybir.dt.from_np(a.dtype), kind="ExternalInput").ap() for n, a in arrays.items()}
    io["out"] = nc.dram_tensor("out", (IMAGES, CH, PIX), F32, kind="ExternalOutput").ap()
    build(nc, io, debug)
    r = run_bass_kernel_spmd(nc, [{f"in_{n}": a for n, a in arrays.items()}], core_ids=[0])
    return r.results[0]["out"].reshape(OUT_SHAPE)
```

```python
from contextlib import ExitStack

import numpy as np

import concourse.bass as bass
from concourse import mybir

F32 = mybir.dt.float32
BF16 = mybir.dt.bfloat16
I32 = mybir.dt.int32
ALU = mybir.AluOpType
ACT = mybir.ActivationFunctionType
AX_X = mybir.AxisListType.X

P = 128
IMAGES, CH, SIDE = 32, 64, 16
PIX = SIDE * SIDE
HALF = IMAGES // 2
TOKENS = IMAGES * PIX
NT = TOKENS // P
PAD_SIDE = SIDE + 2
TAPS = 9
BLOCKS = (2, 4, 8, 16)
N_SHIFT = sum(BLOCKS)

A_NODES = 5000
A_EDGES = 80000
A_W = 1024
A_HEADS, A_DIM = 8, 8
A_F = CH + A_HEADS
A_RUN = 32
A_CHUNKS = 20
A_USED = A_CHUNKS * P * A_RUN
A_RUNS = A_CHUNKS * P

G_EDGES = 262144
G_W = G_EDGES // P
G_HEADS, G_EXP = 4, 4
G_HF = G_HEADS * G_EXP
G_ROW = G_HF + G_HEADS
G_F = G_HF + G_HEADS
G_OUT = G_F + G_HEADS
G_RUN = 64
G_CHUNKS = G_W // G_RUN
G_RUNS = G_CHUNKS * P
HID = 2 * CH

SRC_BITS = 13
NONE = TOKENS
KEY_BASE = 0x40000000
PAD_KEY = KEY_BASE | (NONE << SRC_BITS)
BIG = 1.0e30
FAR = float(1 << 20)

C_IDENT, C_TRIU, C_SHIFT, C_WRAP, C_PAIR, C_IOTA, C_NODE, C_TOGGLE = (0, 128, 256, 384, 512, 640, 768, 832)
C_COLS = 840


def shape_constants():
    c = np.zeros((P, C_COLS), np.float32)
    p = np.arange(P)
    c[p, C_IDENT + p] = 1.0
    c[:, C_TRIU:C_TRIU + P] = p[:, None] <= p[None, :]
    c[p[:-1], C_SHIFT + p[1:]] = 1.0
    c[P - 1, C_WRAP] = 1.0
    c[:, C_PAIR:C_PAIR + P] = 0.5 * (p[:, None] // 2 == p[None, :] // 2)
    c[:, C_IOTA:C_IOTA + P] = p[None, :]
    c[:, C_NODE:C_NODE + NT] = p[:, None] + P * np.arange(NT)[None, :]
    sign = [np.where((p >> m) & 1, -1.0, 1.0) for m in range(7)]
    for m in range(8):
        c[:, C_TOGGLE + m] = (sign[m] if m < 7 else 1.0) * (sign[m - 1] if m else 1.0)
    perm = np.zeros((CH, 1 + N_SHIFT, 2, CH), np.float32)
    m = np.arange(CH)
    perm[m, 0, :, m] = 1.0
    n = 1
    for bs in BLOCKS:
        for k in range(bs):
            perm[m // bs * bs + (m % bs - k) % bs, n, :, m] = 1.0
            n += 1
    return c, perm.reshape(CH, (1 + N_SHIFT) * P)


def sort_steps(width):
    log_w = width.bit_length() - 1
    merges, cur = [], 0

    def add(*what):
        nonlocal cur
        merges[-1].append((what, cur, 1 - cur))
        cur = 1 - cur

    for k in range(1, log_w + 8):
        merges.append([])
        if k >= log_w:
            add("toggle", k - log_w)
        cross = k - log_w
        if cross > 0:
            add("flip")
            for s in reversed(range(cross)):
                add("stage", None, 1 << s)
            add("flip")
        for s in reversed(range(min(k, log_w))):
            add("stage", k if k < log_w else None, 1 << s)
    return merges, cur


A_MERGES, A_LAST = sort_steps(A_W)
G_MERGES, G_LAST = sort_steps(G_W)
A_FLIPS = sum(s[0][0] == "flip" for m in A_MERGES for s in m)
FLIP_FROM = A_W.bit_length()
PAIR_FROM = len(G_MERGES) - A_CHUNKS // 2 + 1


def build(nc, io, debug=None):
    with ExitStack() as ctx:
        def sem(name):
            return ctx.enter_context(nc.semaphore(name))

        def dram(name, shape, dt):
            kind = "ExternalOutput" if debug and name in debug else "Internal"
            return nc.dram_tensor(name, shape, dt, kind=kind).ap()

        d_asrc = dram("d_asrc", (P * A_W,), I32)
        d_adst = dram("d_adst", (P * A_W,), I32)
        d_adstq = dram("d_adstq", (P * A_W,), I32)
        d_gsrc = dram("d_gsrc", (G_EDGES,), I32)
        d_gdst = dram("d_gdst", (G_EDGES,), I32)
        d_gdstq = dram("d_gdstq", (G_EDGES,), I32)
        d_q = dram("d_q", (TOKENS, CH), F32)
        d_qseed = dram("d_qseed", (A_USED, CH), F32)
        d_as = dram("d_as", (A_USED, A_F), F32)
        d_acont = dram("d_acont", (P * A_W // A_RUN,), F32)
        d_ac = dram("d_ac", (A_RUNS, A_F), F32)
        d_h = dram("d_h", (TOKENS, G_ROW), F32)
        d_ad = dram("d_ad", (TOKENS, G_HEADS), F32)
        d_adseed = dram("d_adseed", (G_EDGES, G_HEADS), F32)
        d_gs = dram("d_gs", (G_EDGES, G_OUT), F32)
        d_gcont = dram("d_gcont", (G_RUNS,), F32)
        d_gc = dram("d_gc", (G_RUNS, G_OUT), F32)

        LIMIT = 53200
        arena = ctx.enter_context(nc.sbuf_tensor("arena", [P, LIMIT], F32))

        class Region:
            def __init__(self, at):
                self.at = at

            def take(self, n, dt=F32):
                a = self.at
                self.at += n
                assert self.at <= LIMIT, self.at
                v = arena[:, a:a + n]
                return v if dt == F32 else v.bitcast(dt)

        r = Region(0)
        const = r.take(C_COLS)
        ident = const[:, C_IDENT:C_IDENT + P]
        triu = const[:, C_TRIU:C_TRIU + P]
        shift = const[:, C_SHIFT:C_SHIFT + P]
        wrap = const[:, C_WRAP:C_WRAP + P]
        pair = const[:, C_PAIR:C_PAIR + P]
        iota = const[:, C_IOTA:C_IOTA + P]
        node = const[:, C_NODE:C_NODE + NT]
        ones = r.take(P)
        zeros = r.take(512)
        t_tok = r.take(NT * CH).rearrange("p (i c) -> p i c", c=CH)
        y_tok = r.take(NT * CH).rearrange("p (i c) -> p i c", c=CH)
        t_tile, y_tile = (x.rearrange("p (i h) c -> p h i c", h=2) for x in (t_tok, y_tok))

        def slot(tile):
            return tile % (NT // 2) * 2 + tile // (NT // 2)

        g_key_at = r.at
        g_key = [r.take(G_W) for _ in range(2)]
        a_key_at = r.at
        a_key = [r.take(A_W) for _ in range(2)]

        def node_table(dt=F32):
            return r.take(NT, dt)

        class Nodes:
            def __init__(self):
                self.run = node_table()
                self.run_i = node_table(I32)
                self.count = node_table()
                self.end = r.take(NT + 1)
                self.start = node_table()
                self.has = node_table()
                self.pos_f = node_table()
                self.pos = node_table(I32)
                self.prun = node_table(I32)
                self.cidx_f = node_table()
                self.cidx = node_table(I32)
                self.carried = node_table()
                self.seed_f = node_table()
                self.seed = node_table(I32)
                self.tot = node_table()

        a_nodes, g_nodes = Nodes(), Nodes()
        small = r.take(640)
        g_count = small[:, 448:453].bitcast(I32)
        piv = [small[:, 0:16].bitcast(I32), small[:, 16:32].bitcast(I32)]
        gn_stat = small[:, 32:32 + HALF * 6].rearrange("p (j s) -> p j s", s=6)
        gn_mv = small[:, 128:160].rearrange("p (j s) -> p j s", s=2)
        gn_mean = small[:, 160:176]
        gn_dev = small[:, 176:192]
        gn_rstd = small[:, 192:208]
        gn_bias = small[:, 208:224]
        alph = small[:, 224:240]
        ln_sum = small[:, 256:320]
        ln_var = small[:, 320:384]
        run_prev = small[:, 384:416]
        run_cont = small[:, 416:448]
        first = r.at

        kv = [r.take(A_RUN * 2 * CH).rearrange("p (j f) -> p j f", f=2 * CH) for _ in range(2)]
        a_found = Region(first).take(NT * P, I32).rearrange("p (n j) -> p n j", j=P)
        y_at = C_COLS + P + 512 + NT * CH
        rr = Region(y_at)
        list_nodes = rr.take(G_W, I32)
        a_below = list_nodes.bitcast(F32).rearrange("p (n j) -> p n j", j=P)
        hot_lo = rr.take(16 * P // 2, BF16).rearrange("p (n j) -> p n j", j=P)
        hot_hi = rr.take(16 * NT // 2, BF16).rearrange("p (n j) -> p n j", j=NT)
        assert rr.at <= y_at + NT * CH
        a_sidx = [r.take(A_RUN, I32) for _ in range(2)]
        a_didx = [r.take(A_RUN, I32) for _ in range(2)]
        a_fidx = [r.take(4, I32) for _ in range(2)]
        mid = r.at
        c = Region(mid)
        x_ch = c.take(HALF * PIX).rearrange("p (j s) -> p j s", s=PIX)
        y_pad = c.take(HALF * PAD_SIDE ** 2).rearrange("p (j y x) -> p j y x", y=PAD_SIDE, x=PAD_SIDE)
        w_taps = c.take(TAPS * P).rearrange("p (t o) -> p t o", o=P)
        w_dup = c.take(len(BLOCKS) * 2 * CH * TAPS).rearrange("p (b n) -> p b n", b=len(BLOCKS))
        w_own = c.take(CH * TAPS)
        square_a = y_pad.rearrange("p j y x -> p (j y x)")[:, 0:NT * CH // 2].rearrange("p (i c) -> p i c", c=CH)
        perm = c.take((1 + N_SHIFT) * P).rearrange("p (n m) -> p n m", m=P)
        a = Region(mid)
        q_seed = [a.take(A_RUN * CH).rearrange("p (j f) -> p j f", f=CH) for _ in range(2)]
        q_first = [a.take(CH) for _ in range(2)]
        q_fm = a.take(CH * A_RUN)
        q_edge = a.take(CH * A_RUN)
        a_nst = a.take(A_RUN)
        a_go = a.take(A_F * A_RUN)
        a_prod = a.take(CH * A_RUN)
        a_score = a.take(A_HEADS * A_RUN)
        a_msg = a.take(A_F * A_RUN)
        a_sum = a.take(A_F * A_RUN)
        a_rows = [a.take(A_RUN * A_F).rearrange("p (j f) -> p j f", f=A_F) for _ in range(2)]
        a2 = Region(first)
        a_tail = a2.take(A_CHUNKS * A_F).rearrange("p (c f) -> p c f", f=A_F)
        a_tailT = a2.take(A_RUNS)
        a_cont = a2.take(A_RUNS)
        a_carT = a2.take(A_RUNS)
        a_car = a2.take(A_CHUNKS * A_F).rearrange("p (c f) -> p c f", f=A_F)
        a_end = a2.take(NT * A_F).rearrange("p (i f) -> p i f", f=A_F)
        a_before = a2.take(NT * A_F).rearrange("p (i f) -> p i f", f=A_F)
        g = Region(first)
        yT = g.take(NT // 2 * P).rearrange("p (i n) -> p i n", n=P)
        w1 = g.take(4 * HID).rearrange("p (e n) -> p e n", e=4)
        w2 = g.take(4 * CH).rearrange("p (e n) -> p e n", e=4)
        b1 = g.take(4)
        b2 = g.take(4 * CH)
        wgat = g.take(G_HF)
        att = g.take(5 * G_HF).rearrange("p (v n) -> p v n", v=5)
        h_tok = g.take(NT * G_ROW).rearrange("p (i f) -> p i f", f=G_ROW)
        ad_tok = g.take(NT * G_HEADS).rearrange("p (i f) -> p i f", f=G_HEADS)
        h_prod = Region(y_at).take(NT * G_HF).rearrange("p (i h k) -> p i h k", h=G_HEADS, k=G_EXP)
        hid = [g.take(512) for _ in range(2)]
        exp_out = g.take(NT * 4 * CH).rearrange("p (i n) -> p i n", n=4 * CH)
        g_mid = g.at
        hs = [g.take(G_RUN * G_ROW).rearrange("p (j f) -> p j f", f=G_ROW) for _ in range(2)]
        ad_seed = [g.take(G_RUN * G_HEADS).rearrange("p (j f) -> p j f", f=G_HEADS) for _ in range(2)]
        g_sidx = [g.take(G_RUN, I32) for _ in range(2)]
        g_didx = [g.take(G_RUN, I32) for _ in range(2)]
        g_fidx = [g.take(4, I32) for _ in range(2)]
        ad_first = [g.take(G_HEADS) for _ in range(2)]
        g_rows = [g.take(G_RUN * G_OUT).rearrange("p (j f) -> p j f", f=G_OUT) for _ in range(2)]
        HJ = G_HEADS * G_RUN
        g = Region(y_at)
        g_nst = g.take(HJ)
        g_cut = g.take(HJ)
        ad_fm = g.take(HJ)
        ad_edge = g.take(HJ)
        g_x = g.take(HJ)
        g_e = g.take(HJ)
        g_max = g.take(HJ + 1)
        g_dm = g.take(HJ)
        g_corr = g.take(HJ)
        g_em = g.take(HJ)
        g_msg = g.take(G_F * G_RUN)
        g_corr_f = g.take(G_F * G_RUN)
        g_sum = g.take(G_F * G_RUN)
        assert g.at <= g_key_at + 2 * G_W
        r_a = Region(y_at)
        g_tailT = r_a.take(G_RUNS)
        g_cutT = r_a.take(G_RUNS)
        assert r_a.at <= g_key_at + 2 * G_W
        gs_ = Region(g_mid)
        g_found = gs_.take(NT * P, I32).rearrange("p (n j) -> p n j", j=P)
        g_below = gs_.take(16 * P).rearrange("p (n j) -> p n j", j=P)
        square = g_below.rearrange("p n j -> p (n j)").rearrange("p (i c) -> p i c", c=CH)
        g2 = Region(g_mid)
        g_tmaxT = g2.take(G_RUNS)
        g_cmaxT = g2.take(G_RUNS + 1)
        g3 = Region(first)
        g_dT = g3.take(G_RUNS)
        g_end = g2.take(NT * G_OUT).rearrange("p (i f) -> p i f", f=G_OUT)
        g_tail = Region(a_key_at).take(G_CHUNKS * (G_OUT + G_F)).rearrange("p (c f) -> p c f", f=G_OUT + G_F)
        g4 = Region(y_at)
        n4 = [g4.take(NT * 4).rearrange("p (i h) -> p i h", h=4) for _ in range(12)]
        n16 = [g4.take(NT * G_HF) for _ in range(3)]
        g_before = g4.take(NT * G_OUT).rearrange("p (i f) -> p i f", f=G_OUT)
        assert g4.at <= g_key_at + 2 * G_W
        out_ch = arena[:, g_mid:g_mid + HALF * PIX].rearrange("p (j s) -> p j s", s=PIX)

        ps = [ctx.enter_context(nc.psum_tensor(f"ps{b}", [P, 512], F32)) for b in range(8)]

        const_in, perm_in, x_in, w_in, a_edges_in, g_edges_in = (
            sem(n) for n in ("const_in", "perm_in", "x_in", "w_in", "a_edges_in", "g_edges_in"))
        g_filled, g_count_set, g_stored = sem("g_filled"), sem("g_count_set"), sem("g_stored")
        zeros_set, qseed_zero, adseed_zero = sem("zeros_set"), sem("qseed_zero"), sem("adseed_zero")
        dve_step, dve_loop_a, dve_loop_g = sem("dve_step"), sem("dve_loop_a"), sem("dve_loop_g")
        gathers_begun, stores_begun = sem("gathers_begun"), sem("stores_begun")
        gn_pair_in, gn_pair = sem("gn_pair_in"), sem("gn_pair")
        gn_ready, gn_root, y_ready = sem("gn_ready"), sem("gn_root"), sem("y_ready")
        w_copied = sem("w_copied")
        border_set, perm_scaled, w_mixed, w_ready = sem("border_set"), sem("perm_scaled"), sem("w_mixed"), sem("w_ready")
        alpha_exp_in, alpha_exp = sem("alpha_exp_in"), sem("alpha_exp")
        conv_done, conv_added, t_turned, t_taken = sem("conv_done"), sem("conv_added"), sem("t_turned"), sem("t_taken")
        flip_in, flip_done, flip_taken = sem("flip_in"), sem("flip_done"), sem("flip_taken")
        a_list_set, a_list_out, g_list_set, g_list_out = (sem(n) for n in ("a_list_set", "a_list_out", "g_list_set", "g_list_out"))
        hot_set, hist_done, hist_set, cum_done, run_set, ends_set, starts_done, pos_set = (
            sem(n) for n in ("hot_set", "hist_done", "hist_set", "cum_done", "run_set",
                             "ends_set", "starts_done", "pos_set"))
        found = [[sem(f"found{k}_{n}") for n in range(4)] for k in range(2)]
        last_set, last_shifted, cont_set, cont_out = sem("last_set"), sem("last_shifted"), sem("cont_set"), sem("cont_out")
        root_in, root_out, y_set, q_out, q_scattered = sem("root_in"), sem("root_out"), sem("y_set"), sem("q_out"), sem("q_scattered")
        a_idx_in = [sem(f"a_idx_in{b}") for b in range(2)]
        a_seed_in = [sem(f"a_seed_in{b}") for b in range(2)]
        kv_in = [sem(f"kv_in{b}") for b in range(2)]
        a_used, a_flags, a_laid, a_scored, a_weighed, a_summed, a_rows_set = (
            sem(n) for n in ("a_used", "a_flags", "a_laid", "a_scored", "a_weighed", "a_summed", "a_rows_set"))
        a_rows_out = [sem(f"a_rows_out{b}") for b in range(2)]
        a_tail_in, a_tail_turned, a_tail_taken, a_carried, a_car_turned, a_car_taken, a_car_out, a_ends_in = (
            sem(n) for n in ("a_tail_in", "a_tail_turned", "a_tail_taken", "a_carried", "a_car_turned", "a_car_taken",
                             "a_car_out", "a_ends_in"))
        gw_in, yT_turned, yT_taken, h_done, h_set, h_out, ad_scattered = (
            sem(n) for n in ("gw_in", "yT_turned", "yT_taken", "h_done", "h_set", "h_out", "ad_scattered"))
        hid_done, hid_set, hid_used, exp_taken = (sem(n) for n in ("hid_done", "hid_set", "hid_used", "exp_taken"))
        g_idx_in = [sem(f"g_idx_in{b}") for b in range(2)]
        hs_in = [sem(f"hs_in{b}") for b in range(2)]
        g_used, g_laid, g_max_set, g_exp_done, g_weighed, g_summed, g_rows_set, g_flags = (
            sem(n) for n in ("g_used", "g_laid", "g_max_set", "g_exp_done", "g_weighed", "g_summed", "g_rows_set", "g_flags"))
        g_rows_out = [sem(f"g_rows_out{b}") for b in range(2)]
        g_tail_in, g_rep_set, g_tail_turned, g_tail_taken, g_dT_set, g_dT_exp, g_carried, g_car_turned, g_car_taken, g_car_out, g_ends_in = (
            sem(n) for n in ("g_tail_in", "g_rep_set", "g_tail_turned", "g_tail_taken", "g_dT_set", "g_dT_exp", "g_carried",
                             "g_car_turned", "g_car_taken", "g_car_out", "g_ends_in"))
        node_exp_in, node_exp, gate_root_in, gate_root, gate_exp_in, gate_exp = (
            sem(n) for n in ("node_exp_in", "node_exp", "gate_root_in", "gate_root", "gate_exp_in", "gate_exp"))
        out_set, out_turned, out_laid, out_stored = sem("out_set"), sem("out_turned"), sem("out_laid"), sem("out_stored")

        block = ctx.enter_context(nc.Block())

        def bc(ap, shape):
            return ap.to_broadcast(shape)

        @block.sync
        def _(sp):
            sp.dma_start(a_key[1][:, 0:A_EDGES // P].bitcast(I32),
                         io["a_edges"][1].rearrange("(p j) -> p j", p=P)).then_inc(a_edges_in, 16)
            sp.dma_start(a_key[0][:, 0:A_EDGES // P].bitcast(I32),
                         io["a_edges"][0].rearrange("(p j) -> p j", p=P)).then_inc(a_edges_in, 16)
            sp.dma_start(const, io["const"]).then_inc(const_in, 16)
            for half in range(2):
                sp.dma_start(x_ch[half * CH:(half + 1) * CH, :, :],
                             io["x"][half * HALF:(half + 1) * HALF].rearrange("j c s -> c j s")).then_inc(x_in, 16)
            sp.dma_start(perm[0:CH, :, :].rearrange("p n m -> p (n m)"), io["perm"]).then_inc(perm_in, 16)
            sp.dma_start(alph[0:CH, 0:5], io["alphas"].partition_broadcast(CH)).then_inc(w_in, 16)
            sp.dma_start(w_own[0:CH, :], io["w_own"]).then_inc(w_in, 16)
            for n, bs in enumerate(BLOCKS):
                view = w_dup[0:CH, n, :].rearrange("p (q s b) -> p q s b", s=2, b=bs * TAPS)
                for copy in range(2):
                    sp.dma_start(view[:, :, copy, :],
                                 io["w_blocks"][n].rearrange("p (q b) -> p q b", b=bs * TAPS)).then_inc(w_in, 16)
            for n in range(2):
                sp.dma_start(g_key[n].bitcast(I32), io["g_edges"][n].rearrange("(p j) -> p j", p=P)).then_inc(g_edges_in, 16)
            sp.wait_ge(zeros_set, 1)
            zq = d_qseed.rearrange("(p n) f -> p (n f)", p=P)
            per = A_USED // P * CH
            for n in range(0, per, 8192):
                sp.dma_start(zq[:, n:n + 8192].rearrange("p (r z) -> p r z", z=512),
                             bc(zeros[:, None, :], [P, 16, 512])).then_inc(qseed_zero, 16)
            sp.dma_start(d_adseed.rearrange("(p n) f -> p (n f)", p=P).rearrange("p (r z) -> p r z", z=512),
                         bc(zeros[:, None, :], [P, 16, 512])).then_inc(adseed_zero, 16)

            sp.wait_ge(a_list_set, 1)
            for out, src in ((d_asrc, a_key[1 - A_LAST]), (d_adst, a_key[A_LAST]), (d_adstq, list_nodes[:, 0:A_W])):
                sp.dma_start(out.rearrange("(p j) -> p j", p=P), src.bitcast(I32)).then_inc(a_list_out, 16)
            sp.wait_ge(cont_set, 1)
            sp.dma_start(d_acont.rearrange("(p j) -> p j", p=P), run_cont[:, 0:A_W // A_RUN]).then_inc(cont_out, 16)
            src_v = d_asrc.rearrange("(c p j) -> c p j", p=P, j=A_RUN)
            dst_v = d_adst.rearrange("(c p j) -> c p j", p=P, j=A_RUN)
            dstq_v = d_adstq.rearrange("(c p j) -> c p j", p=P, j=A_RUN)
            seed_v = d_qseed.rearrange("(c p j) f -> c p j f", p=P, j=A_RUN)
            out_v = d_as.rearrange("(c p j) f -> c p j f", p=P, j=A_RUN)

            sp.wait_ge(a_list_out, 48)
            for b in range(2):
                sp.dma_start(a_sidx[b], src_v[b]).then_inc(a_idx_in[b], 16)
                sp.dma_start(a_didx[b], dst_v[b]).then_inc(a_idx_in[b], 16)
                sp.dma_start(a_fidx[b], dstq_v[b][:, 0:4]).then_inc(a_idx_in[b], 16)
            sp.wait_ge(y_set, 1)
            for half in range(2):
                sp.dma_start(d_q.rearrange("(h i p) c -> h p i c", p=P, h=2)[half], y_tile[:, half]).then_inc(q_out, 16)
            sp.wait_ge(q_scattered, 16 * NT)
            for b in range(2):
                sp.dma_start(q_seed[b], seed_v[b]).then_inc(a_seed_in[b], 16)

            with sp.Fori(0, A_CHUNKS // 2 - 1) as it:
                for b in range(2):
                    sp.wait_ge(a_used, it * 2 + (b + 1))
                    sp.wait_ge(a_rows_set, it * 2 + (b + 1))
                    sp.dma_start(out_v[bass.ds(it * 2 + b, 1)].rearrange("c p j f -> (c p) j f"), a_rows[b]).then_inc(a_rows_out[b], 16)
                    nxt = it * 2 + (b + 2)
                    sp.dma_start(a_sidx[b], src_v[bass.ds(nxt, 1)].rearrange("c p j -> (c p) j")).then_inc(a_idx_in[b], 16)
                    sp.dma_start(a_didx[b], dst_v[bass.ds(nxt, 1)].rearrange("c p j -> (c p) j")).then_inc(a_idx_in[b], 16)
                    sp.dma_start(a_fidx[b], dstq_v[bass.ds(nxt, 1), :, 0:4].rearrange("c p j -> (c p) j")).then_inc(a_idx_in[b], 16)
                    sp.dma_start(q_seed[b], seed_v[bass.ds(nxt, 1)].rearrange("c p j f -> (c p) j f")).then_inc(a_seed_in[b], 16)
            for b in range(2):
                sp.wait_ge(a_rows_set, A_CHUNKS - 1 + b)
                sp.dma_start(out_v[A_CHUNKS - 2 + b], a_rows[b]).then_inc(a_rows_out[b], 16)
            sp.wait_ge(g_list_set, 1)
            for out, src in ((d_gsrc, g_key[1 - G_LAST]), (d_gdst, g_key[G_LAST]), (d_gdstq, list_nodes)):
                sp.dma_start(out.rearrange("(p j) -> p j", p=P), src.bitcast(I32)).then_inc(g_list_out, 16)
            sp.wait_ge(cont_set, 2)
            sp.dma_start(d_gcont.rearrange("(p j) -> p j", p=P), run_cont[:, 0:G_W // G_RUN]).then_inc(cont_out, 16)

            for b in range(2):
                sp.wait_ge(a_rows_out[b], 16 * (A_CHUNKS // 2))
            sp.wait_ge(cont_out, 16)
            sp.dma_start(a_tail, d_as.rearrange("(c p j) f -> j p c f", p=P, j=A_RUN)[A_RUN - 1]).then_inc(a_tail_in, 16)
            sp.dma_start(a_cont[0:A_F, :], d_acont[0:A_RUNS].partition_broadcast(A_F)).then_inc(a_tail_in, 16)
            sp.wait_ge(a_car_taken, 5)
            sp.dma_start(d_ac.rearrange("(c p) f -> p c f", p=P), a_car).then_inc(a_car_out, 16)

            sp.wait_ge(y_set, 2)
            for half in range(2):
                at = slice(half * CH, (half + 1) * CH)
                sp.dma_start(w1[at], io["w1"].rearrange("e c n -> c e n")).then_inc(gw_in, 16)
                sp.dma_start(wgat[at], io["wgat"]).then_inc(gw_in, 16)
            sp.dma_start(w2, io["w2"].rearrange("e n c -> n e c")).then_inc(gw_in, 16)
            sp.dma_start(b1, io["b1"]).then_inc(gw_in, 16)
            sp.dma_start(b2, io["b2"].rearrange("e c -> (e c)").partition_broadcast(P)).then_inc(gw_in, 16)
            for n, name in enumerate(("att_src", "att_dst", "b_gat", "gamma", "beta")):
                sp.dma_start(att[:, n, :], io[name].partition_broadcast(P)).then_inc(gw_in, 16)

            sp.wait_ge(h_set, 1)
            sp.dma_start(d_h.rearrange("(i p) f -> p i f", p=P), h_tok).then_inc(h_out, 16)
            sp.dma_start(d_ad.rearrange("(i p) f -> p i f", p=P), ad_tok).then_inc(h_out, 16)
            sp.wait_ge(g_list_out, 48)
            sp.wait_ge(ad_scattered, 16 * NT)

            gsrc_v = d_gsrc.rearrange("(c p j) -> c p j", p=P, j=G_RUN)
            gdst_v = d_gdst.rearrange("(c p j) -> c p j", p=P, j=G_RUN)
            gdstq_v = d_gdstq.rearrange("(c p j) -> c p j", p=P, j=G_RUN)
            gseed_v = d_adseed.rearrange("(c p j) f -> c p j f", p=P, j=G_RUN)
            gout_v = d_gs.rearrange("(c p j) f -> c p j f", p=P, j=G_RUN)
            for b in range(2):
                sp.dma_start(g_sidx[b], gsrc_v[b]).then_inc(g_idx_in[b], 16)
                sp.dma_start(g_didx[b], gdst_v[b]).then_inc(g_idx_in[b], 16)
                sp.dma_start(g_fidx[b], gdstq_v[b][:, 0:4]).then_inc(g_idx_in[b], 16)
                sp.dma_start(ad_seed[b], gseed_v[b]).then_inc(g_idx_in[b], 16)
            sp.wait_ge(g_count_set, 1)
            n_all, n_of = sp.value_load(g_count[0:1, 0:1], min_val=2, max_val=G_CHUNKS), [
                sp.value_load(g_count[0:1, 1 + b:2 + b], min_val=1, max_val=G_CHUNKS // 2) for b in range(2)]
            n_fill = sp.value_load(g_count[0:1, 4:5], min_val=0, max_val=16 * G_CHUNKS)
            flat_v = gout_v.rearrange("c p j f -> c p (j f)").rearrange("c p (r z) -> c p r z", z=512)
            with sp.Fori(2, G_CHUNKS) as it:
                with sp.If(it >= n_all):
                    sp.dma_start(flat_v[bass.ds(it, 1)].rearrange("c p r z -> (c p) r z"),
                                 bc(zeros[:, None, :], [P, G_RUN * G_OUT // 512, 512])).then_inc(g_filled, 16)
            with sp.Fori(1, G_CHUNKS // 2) as it:
                for b in range(2):
                    with sp.If(it * 2 + b < n_all):
                        sp.wait_ge(g_used, it * 2 + (b - 1))
                        sp.wait_ge(g_rows_set, it * 2 + (b - 1))
                        sp.sem_inc(stores_begun, 1)
                        sp.dma_start(gout_v[bass.ds(it * 2 + (b - 2), 1)].rearrange("c p j f -> (c p) j f"), g_rows[b]).then_inc(g_rows_out[b], 16)
                        nxt = it * 2 + b
                        sp.dma_start(g_sidx[b], gsrc_v[bass.ds(nxt, 1)].rearrange("c p j -> (c p) j")).then_inc(g_idx_in[b], 16)
                        sp.dma_start(g_didx[b], gdst_v[bass.ds(nxt, 1)].rearrange("c p j -> (c p) j")).then_inc(g_idx_in[b], 16)
                        sp.dma_start(g_fidx[b], gdstq_v[bass.ds(nxt, 1), :, 0:4].rearrange("c p j -> (c p) j")).then_inc(g_idx_in[b], 16)
                        sp.dma_start(ad_seed[b], gseed_v[bass.ds(nxt, 1)].rearrange("c p j f -> (c p) j f")).then_inc(g_idx_in[b], 16)
            sp.wait_ge(g_rows_set, n_all)
            sp.sem_inc(stores_begun, 1)
            for b in range(2):
                sp.dma_start(gout_v[bass.ds(n_of[b] * 2 + (b - 2), 1)].rearrange("c p j f -> (c p) j f"), g_rows[b]).then_inc(g_rows_out[b], 16)
            for b in range(2):
                sp.wait_ge(g_rows_out[b], n_of[b] * 16)
                sp.sem_inc(g_stored, 1)
            with sp.If(n_all < G_CHUNKS):
                sp.wait_ge(g_filled, n_fill)
                sp.sem_inc(stores_begun, 1)
            sp.sem_inc(g_stored, 1)
            sp.wait_ge(cont_out, 32)
            sp.dma_start(g_tail[:, :, 0:G_OUT], d_gs.rearrange("(c p j) f -> j p c f", p=P, j=G_RUN)[G_RUN - 1]).then_inc(g_tail_in, 16)
            sp.dma_start(g_cutT[0:G_F, :], d_gcont.partition_broadcast(G_F)).then_inc(g_tail_in, 16)
            sp.wait_ge(g_car_taken, 2 * G_CHUNKS // 4)
            sp.dma_start(d_gc.rearrange("(c p) f -> p c f", p=P), g_tail[:, :, 0:G_OUT]).then_inc(g_car_out, 16)

            out_dram = io["out"]
            for n in range(4):
                sp.wait_ge(out_laid, 2 * (n + 1))
                for half in range(2):
                    sp.dma_start(out_dram[half * HALF + 4 * n:half * HALF + 4 * n + 4].rearrange("j c s -> c j s"),
                                 out_ch[half * CH:(half + 1) * CH, 4 * n:4 * n + 4, :]).then_inc(out_stored, 16)
            sp.wait_ge(out_stored, 16 * 8)

        @block.gpsimd
        def _(pool):
            pool.memset(zeros, 0.0).then_inc(zeros_set, 1)
            pool.memset(y_pad, 0.0).then_inc(border_set, 1)
            pool.memset(w_taps, 0.0).then_inc(border_set, 1)

            def search_gathers(nodes, table, n_rows, out, sems):
                for i in range(NT):
                    pool.indirect_dma_start(out[:, i, :], None, table.rearrange("(n j) -> n j", j=P)[0:n_rows],
                                            bass.IndirectOffsetOnAxis(nodes.run_i[:, i:i + 1], 0)).then_inc(sems[i // 16], 16)

            pool.wait_ge(run_set, 1)
            pool.wait_ge(a_list_out, 48)
            search_gathers(a_nodes, d_adst, A_W, a_found, found[0])

            def a_gather(b):
                for j in range(A_RUN):
                    pool.indirect_dma_start(kv[b][:, j, :], None, io["kv"], bass.IndirectOffsetOnAxis(a_sidx[b][:, j:j + 1], 0))\
                        .then_inc(kv_in[b], 16)

            def a_gather_first(b):
                pool.indirect_dma_start(q_first[b], None, d_q, bass.IndirectOffsetOnAxis(a_fidx[b][:, 0:1], 0)).then_inc(kv_in[b], 16)

            pool.wait_ge(ends_set, 1)
            for b in range(2):
                pool.wait_ge(a_idx_in[b], 48)
                a_gather(b)
            pool.wait_ge(pos_set, 1)
            pool.wait_ge(y_set, 1)
            pool.wait_ge(qseed_zero, 16 * (A_USED // P * CH // 8192))
            for i in range(NT):
                pool.indirect_dma_start(d_qseed, bass.IndirectOffsetOnAxis(a_nodes.seed[:, i:i + 1], 0), y_tok[:, slot(i), :], None,
                                        bounds_check=A_USED - 1, oob_is_err=False).then_inc(q_scattered, 16)
            pool.wait_ge(q_out, 32)
            for b in range(2):
                a_gather_first(b)
            with pool.Fori(1, A_CHUNKS // 2) as it:
                for b in range(2):
                    pool.wait_ge(a_idx_in[b], it * 48 + 48)
                    pool.wait_ge(a_used, it * 2 + (b - 1))
                    pool.sem_inc(gathers_begun, 1)
                    a_gather(b)
                    a_gather_first(b)

            for b in range(2):
                pool.wait_ge(a_rows_out[b], 16 * (A_CHUNKS // 2))
            pool.wait_ge(a_used, A_CHUNKS)
            pool.wait_ge(a_rows_set, A_CHUNKS)
            for i in range(NT):
                pool.indirect_dma_start(a_end[:, i, :], None, d_as, bass.IndirectOffsetOnAxis(a_nodes.pos[:, i:i + 1], 0))\
                    .then_inc(a_ends_in, 16)
            pool.wait_ge(run_set, 2)
            pool.wait_ge(g_list_out, 48)
            search_gathers(g_nodes, d_gdst, G_W, g_found, found[1])
            pool.wait_ge(a_car_out, 16)
            for i in range(NT):
                pool.indirect_dma_start(a_before[:, i, :], None, d_ac, bass.IndirectOffsetOnAxis(a_nodes.cidx[:, i:i + 1], 0))\
                    .then_inc(a_ends_in, 16)

            pool.wait_ge(pos_set, 2)
            pool.wait_ge(h_set, 1)
            pool.wait_ge(adseed_zero, 16)
            for i in range(NT):
                pool.indirect_dma_start(d_adseed, bass.IndirectOffsetOnAxis(g_nodes.seed[:, i:i + 1], 0), ad_tok[:, i, :], None,
                                        bounds_check=G_EDGES - 1, oob_is_err=False).then_inc(ad_scattered, 16)
            pool.wait_ge(h_out, 32)

            def g_gather(b):
                pool.indirect_dma_start(ad_first[b], None, d_ad, bass.IndirectOffsetOnAxis(g_fidx[b][:, 0:1], 0)).then_inc(hs_in[b], 16)
                for j in range(G_RUN):
                    pool.indirect_dma_start(hs[b][:, j, :], None, d_h, bass.IndirectOffsetOnAxis(g_sidx[b][:, j:j + 1], 0))\
                        .then_inc(hs_in[b], 16)

            for b in range(2):
                pool.wait_ge(g_idx_in[b], 64)
                g_gather(b)
            pool.wait_ge(g_count_set, 1)
            n_all = pool.value_load(g_count[0:1, 0:1], min_val=2, max_val=G_CHUNKS)
            with pool.Fori(1, G_CHUNKS // 2) as it:
                for b in range(2):
                    with pool.If(it * 2 + b < n_all):
                        pool.wait_ge(g_idx_in[b], it * 64 + 64)
                        pool.wait_ge(g_used, it * 2 + (b - 1))
                        pool.sem_inc(gathers_begun, 1)
                        g_gather(b)
            pool.wait_ge(g_stored, 3)
            for i in range(NT):
                pool.indirect_dma_start(g_end[:, i, :], None, d_gs, bass.IndirectOffsetOnAxis(g_nodes.pos[:, i:i + 1], 0))\
                    .then_inc(g_ends_in, 16)
            pool.wait_ge(g_car_out, 16)
            for i in range(NT):
                pool.indirect_dma_start(g_before[:, i, :], None, d_gc, bass.IndirectOffsetOnAxis(g_nodes.cidx[:, i:i + 1], 0))\
                    .then_inc(g_ends_in, 16)

        @block.tensor
        def _(pe):
            def turn(out, in_, n=P):
                return nc.tensor.transpose(out, in_, ident[0:n, 0:n])

            flips = [0]

            def sort_flips(merge, key):
                for what, src, dst in merge:
                    if what[0] != "flip":
                        continue
                    flips[0] += 1
                    pe.wait_ge(flip_in, flips[0])
                    for blk in range(key[0].shape[1] // P):
                        last = turn(ps[blk // 4][:, blk % 4 * P:(blk % 4 + 1) * P], key[src][:, blk * P:(blk + 1) * P])
                        if blk % 4 == 3:
                            last.then_inc(flip_done, 1)

            def histogram(nb):
                for n in range(nb):
                    last = nc.tensor.matmul(ps[2][:, 0:NT], hot_lo[:, n, :], hot_hi[:, n, :], start=n == 0, stop=n == nb - 1)
                last.then_inc(hist_done, 1)

            def running(k, nodes):
                pe.wait_ge(hist_set, k)
                nc.tensor.matmul(ps[3][:, 0:NT], triu, nodes.tot, start=True, stop=True)
                nc.tensor.matmul(ps[3][:, 128:128 + NT], ones, nodes.tot, start=True, stop=True).then_inc(cum_done, 1)

            def starts(k, nodes):
                pe.wait_ge(ends_set, k)
                nc.tensor.matmul(ps[3][:, 256:256 + NT + 1], wrap, nodes.end, start=True, stop=False)
                nc.tensor.matmul(ps[3][:, 256:256 + NT], shift, nodes.end[:, 1:NT + 1], start=False, stop=True).then_inc(starts_done, 1)

            def last_of_before(k):
                pe.wait_ge(last_set, k)
                nc.tensor.matmul(ps[2][:, 128:129], shift, ln_sum[:, 0:1], start=True, stop=True).then_inc(last_shifted, 1)

            def conv(j):
                if j >= 2:
                    pe.wait_ge(conv_added, j - 1)
                for tap in range(TAPS):
                    dy, dx = tap // 3, tap % 3
                    last = nc.tensor.matmul(ps[4 + j % 2][:, :], w_taps[:, tap, :], y_pad[:, 2 * j:2 * j + 2, dy:dy + SIDE, dx:dx + SIDE],
                                            start=tap == 0, stop=tap == TAPS - 1)
                last.then_inc(conv_done, 1)

            def tokens(j):
                pe.wait_ge(conv_added, j + 1)
                if j >= 2:
                    pe.wait_ge(t_taken, j - 1)
                for n in range(4):
                    last = turn(ps[6 + j % 2][:, n * P:(n + 1) * P], x_ch[:, 2 * j + n // 2, n % 2 * P:(n % 2 + 1) * P])
                last.then_inc(t_turned, 1)

            pe.wait_ge(const_in, 16)
            pe.wait_ge(gn_pair_in, 1)
            nc.tensor.matmul(ps[7][:, 0:HALF], pair, gn_mean, start=True, stop=True).then_inc(gn_pair, 1)
            pe.wait_ge(gn_pair_in, 2)
            nc.tensor.matmul(ps[7][:, 32:32 + HALF], pair, gn_dev, start=True, stop=True).then_inc(gn_pair, 1)
            pe.wait_ge(perm_scaled, 1)
            for part in range(2):
                cols = CH * TAPS // 2
                acc = ps[4 + part][:, 0:cols]
                nc.tensor.matmul(acc, perm[0:CH, 0, :], w_own[0:CH, part * cols:(part + 1) * cols], start=True, stop=False)
                n = 1
                for m, bs in enumerate(BLOCKS):
                    view = w_dup[0:CH, m, :].rearrange("p (q b) -> p q b", b=2 * bs * TAPS)
                    q = CH // bs // 2
                    for k in range(bs):
                        lo = (bs - k) % bs * TAPS
                        last = nc.tensor.matmul(acc, perm[0:CH, n, :], view[:, part * q:(part + 1) * q, lo:lo + bs * TAPS],
                                                start=False, stop=n == N_SHIFT)
                        n += 1
                last.then_inc(w_mixed, 1)
            for k, merge in enumerate(A_MERGES, 1):
                sort_flips(merge, a_key)
                if k == FLIP_FROM:
                    pe.wait_ge(w_ready, 1)
                    pe.wait_ge(y_ready, HALF)
                if k >= FLIP_FROM:
                    conv(k - FLIP_FROM)
                if k >= FLIP_FROM + 2:
                    tokens(k - FLIP_FROM - 2)
            last_of_before(1)
            pe.wait_ge(hot_set, 1)
            histogram(A_W // P)
            running(1, a_nodes)
            conv(7)
            for j in range(5, 8):
                tokens(j)
            starts(1, a_nodes)
            for merge in G_MERGES:
                sort_flips(merge, g_key)
            last_of_before(2)
            pe.wait_ge(hot_set, 2)
            histogram(G_W // P)
            running(2, g_nodes)

            pe.wait_ge(a_tail_in, 32)
            for n in range(A_CHUNKS // 4):
                if n >= 2:
                    pe.wait_ge(a_tail_taken, n - 1)
                for c_ in range(4):
                    last = turn(ps[4 + n % 2][0:A_F, c_ * P:(c_ + 1) * P], a_tail[:, 4 * n + c_, :])
                last.then_inc(a_tail_turned, 1)
            pe.wait_ge(a_carried, 1)
            for n in range(A_CHUNKS // 4):
                if n >= 2:
                    pe.wait_ge(a_car_taken, n - 1)
                for c_ in range(4):
                    last = turn(ps[6 + n % 2][:, c_ * A_F:(c_ + 1) * A_F], a_carT[0:A_F, (4 * n + c_) * P:(4 * n + c_ + 1) * P], A_F)
                last.then_inc(a_car_turned, 1)

            pe.wait_ge(y_set, 2)
            for n in range(8):
                if n >= 2:
                    pe.wait_ge(yT_taken, n - 1)
                for k in range(4):
                    i = 4 * n + k
                    last = turn(ps[n % 2][:, k * P:(k + 1) * P],
                                y_tok[:, 2 * i:2 * i + 2, :].rearrange("p a c -> p (a c)"))
                last.then_inc(yT_turned, 1)
            pe.wait_ge(gw_in, 16 * 12)
            pe.wait_ge(yT_taken, 8)
            for i in range(NT):
                half = i // (NT // 2)
                at = slice(half * CH, (half + 1) * CH)
                last = nc.tensor.matmul(ps[2 + half][:, i % 32 * G_HF:(i % 32 + 1) * G_HF], yT[at, i % 32, :], wgat[at], start=True, stop=True)
            last.then_inc(h_done, 1)
            starts(2, g_nodes)
            def expert_out(n):
                grp, e = n // 4, n % 4
                if n % 4 == 0 and grp >= 1:
                    pe.wait_ge(exp_taken, grp)
                pe.wait_ge(hid_set, n + 1)
                for k in range(4):
                    last = nc.tensor.matmul(ps[6 + k // 2][:, k % 2 * 256 + e * CH:k % 2 * 256 + (e + 1) * CH],
                                            hid[n % 2][:, k * P:(k + 1) * P], w2[:, e, :], start=True, stop=True)
                last.then_inc(hid_used, 1)

            for n in range(64):
                grp, e = n // 4, n % 4
                half, i0 = grp // 8, grp % 8 * 4
                at = slice(half * CH, (half + 1) * CH)
                if n >= 2:
                    pe.wait_ge(hid_set, n - 1)
                nc.tensor.matmul(ps[4 + n % 2][:, :], w1[at, e, :], yT[at, i0:i0 + 4, :].rearrange("p i n -> p (i n)"),
                                 start=True, stop=True).then_inc(hid_done, 1)
                if n >= 1:
                    expert_out(n - 1)
            expert_out(63)

            pe.wait_ge(g_rep_set, 1)
            for n in range(G_CHUNKS // 4):
                if n >= 1:
                    pe.wait_ge(g_tail_taken, 2 * n)
                for c_ in range(4):
                    nc_ = 4 * n + c_
                    turn(ps[4][0:G_F, c_ * P:(c_ + 1) * P], g_tail[:, nc_, 0:G_F])
                    last = turn(ps[5][0:G_F, c_ * P:(c_ + 1) * P], g_tail[:, nc_, G_OUT:G_OUT + G_F])
                last.then_inc(g_tail_turned, 1)
            pe.wait_ge(g_carried, 1)
            for n in range(G_CHUNKS // 4):
                if n >= 1:
                    pe.wait_ge(g_car_taken, 2 * n)
                for c_ in range(4):
                    nc_ = 4 * n + c_
                    turn(ps[6][:, c_ * G_F:(c_ + 1) * G_F], g_cutT[0:G_F, nc_ * P:(nc_ + 1) * P], G_F)
                    last = turn(ps[7][:, c_ * G_F:(c_ + 1) * G_F], g_cmaxT[0:G_F, 1 + nc_ * P:1 + (nc_ + 1) * P], G_F)
                last.then_inc(g_car_turned, 1)

            pe.wait_ge(out_set, 1)
            for n in range(8):
                if n >= 2:
                    pe.wait_ge(out_laid, n - 1)
                for k in range(4):
                    i = 4 * n + k
                    last = turn(ps[n % 2][:, k * P:(k + 1) * P], t_tok[:, 2 * i:2 * i + 2, :].rearrange("p a c -> p (a c)"))
                last.then_inc(out_turned, 1)

        @block.scalar
        def _(act):
            act.wait_ge(gn_ready, 1)
            nc.scalar.activation(gn_rstd, gn_rstd, ACT.Sqrt).then_inc(gn_root, 1)
            act.wait_ge(gn_ready, 2)
            act.wait_ge(border_set, 1)
            act.wait_ge(x_in, 32)
            for j in range(HALF):
                nc.scalar.activation(y_pad[:, j, 1:1 + SIDE, 1:1 + SIDE], x_ch[:, j, :].rearrange("p (y x) -> p y x", x=SIDE),
                                     ACT.Identity, bias=gn_bias[:, j:j + 1], scale=gn_rstd[:, j:j + 1]).then_inc(y_ready, 1)

            act.wait_ge(alpha_exp_in, 1)
            nc.scalar.activation(alph[0:CH, 8:13], alph[0:CH, 0:5], ACT.Exp).then_inc(alpha_exp, 1)
            act.wait_ge(w_mixed, 2)
            act.wait_ge(border_set, 2)
            for part in range(2):
                for half in range(2):
                    at = slice(half * CH, (half + 1) * CH)
                    o = half * CH + part * CH // 2
                    last = nc.scalar.copy(w_taps[at, :, o:o + CH // 2], ps[4 + part][at, 0:CH * TAPS // 2].rearrange("p (o t) -> p t o", t=TAPS))
                    if half:
                        last.then_inc(w_copied, 1)
            act.wait_ge(w_copied, 2)
            act.sem_inc(w_ready, 1)

            banks = [0]

            def sort_flips(merge, key):
                for what, src, dst in merge:
                    if what[0] != "flip":
                        continue
                    for bank in range(key[0].shape[1] // 512):
                        banks[0] += 1
                        act.wait_ge(flip_done, banks[0])
                        nc.scalar.copy(key[dst][:, bank * 512:(bank + 1) * 512], ps[bank][:, :]).then_inc(flip_taken, 1)

            def tokens(j):
                act.wait_ge(t_turned, j + 1)
                nc.scalar.copy(t_tok[:, 8 * j:8 * j + 8, :].rearrange("p i c -> p (i c)"), ps[6 + j % 2][:, :]).then_inc(t_taken, 1)

            for k, merge in enumerate(A_MERGES, 1):
                sort_flips(merge, a_key)
                if k >= FLIP_FROM + 2:
                    tokens(k - FLIP_FROM - 2)
            for j in range(5, 8):
                tokens(j)
            act.wait_ge(root_in, 1)
            nc.scalar.activation(ln_var, ln_var, ACT.Sqrt).then_inc(root_out, 1)

            def a_chunk(it, b, first):
                c1 = it * 2 + (b + 1)
                act.wait_ge(a_seed_in[b], it * 16 + 16)
                act.wait_ge(a_flags, c1)
                by_f = q_fm.rearrange("p (f j) -> p f j", j=A_RUN)
                nc.scalar.copy(by_f[:, :, 1:], q_seed[b].rearrange("p j f -> p f j")[:, :, 1:])
                nc.scalar.copy(a_go.rearrange("p (f j) -> p f j", j=A_RUN), bc(a_nst[:, None, :], [P, A_F, A_RUN]))
                act.wait_ge(kv_in[b], it * (16 * (A_RUN + 1)) + 16 * (A_RUN + 1))
                nc.scalar.copy(by_f[:, :, 0], q_first[b]).then_inc(a_laid, 1)
                act.wait_ge(a_scored, c1)
                nc.scalar.activation(a_msg[:, CH * A_RUN:], a_score, ACT.Exp).then_inc(a_weighed, 1)
                act.wait_ge(a_summed, c1)
                if not first:
                    act.wait_ge(a_rows_out[b], it * 16)
                nc.scalar.copy(a_rows[b].rearrange("p j f -> p f j"), a_sum.rearrange("p (f j) -> p f j", j=A_RUN)).then_inc(a_rows_set, 1)

            for k, merge in enumerate(G_MERGES, 1):
                sort_flips(merge, g_key)
                for b in range(2 * (k >= PAIR_FROM)):
                    a_chunk(k - PAIR_FROM, b, k == PAIR_FROM)

            for n in range(A_CHUNKS // 4):
                act.wait_ge(a_tail_turned, n + 1)
                nc.scalar.copy(a_tailT[0:A_F, n * 512:(n + 1) * 512], ps[4 + n % 2][0:A_F, :]).then_inc(a_tail_taken, 1)
            for n in range(A_CHUNKS // 4):
                act.wait_ge(a_car_turned, n + 1)
                nc.scalar.copy(a_car[:, 4 * n:4 * n + 4, :].rearrange("p c f -> p (c f)"), ps[6 + n % 2][:, 0:4 * A_F]).then_inc(a_car_taken, 1)

            act.wait_ge(root_in, 2)
            nc.scalar.activation(ln_var, ln_var, ACT.Sqrt).then_inc(root_out, 1)
            for n in range(8):
                act.wait_ge(yT_turned, n + 1)
                nc.scalar.copy(yT[:, 4 * n:4 * n + 4, :].rearrange("p i n -> p (i n)"), ps[n % 2][:, :]).then_inc(yT_taken, 1)
            act.wait_ge(gw_in, 16 * 12)
            for n in range(64):
                act.wait_ge(hid_done, n + 1)
                if n >= 2:
                    act.wait_ge(hid_used, n - 1)
                nc.scalar.activation(hid[n % 2], ps[4 + n % 2][:, :], ACT.Gelu, bias=b1[:, n % 4:n % 4 + 1]).then_inc(hid_set, 1)

            def g_chunk(it, b, first):
                c1 = it * 2 + (b + 1)
                act.wait_ge(g_idx_in[b], it * 64 + 64)
                act.wait_ge(g_flags, c1)
                by_f = ad_fm.rearrange("p (f j) -> p f j", j=G_RUN)
                nc.scalar.copy(by_f[:, :, 1:], ad_seed[b].rearrange("p j f -> p f j")[:, :, 1:])
                act.wait_ge(hs_in[b], it * (16 * (G_RUN + 1)) + 16 * (G_RUN + 1))
                nc.scalar.copy(by_f[:, :, 0], ad_first[b]).then_inc(g_laid, 1)
                act.wait_ge(g_max_set, c1)
                nc.scalar.activation(g_msg[:, G_HF * G_RUN:], g_em, ACT.Exp).then_inc(g_exp_done, 1)
                nc.scalar.activation(g_corr_f[:, G_HF * G_RUN:], g_dm, ACT.Exp).then_inc(g_exp_done, 1)
                act.wait_ge(g_exp_done, it * 4 + (2 * b + 2))
                nc.scalar.copy(g_corr_f[:, 0:G_HF * G_RUN].rearrange("p (h k j) -> p h k j", h=G_HEADS, j=G_RUN),
                               bc(g_corr_f[:, G_HF * G_RUN:].rearrange("p (h j) -> p h j", j=G_RUN)[:, :, None, :],
                                  [P, G_HEADS, G_EXP, G_RUN])).then_inc(g_weighed, 1)
                act.wait_ge(g_summed, c1)
                if not first:
                    act.wait_ge(g_rows_out[b], it * 16)
                rows_f = g_rows[b].rearrange("p j f -> p f j")
                nc.scalar.copy(rows_f[:, 0:G_F], g_sum.rearrange("p (f j) -> p f j", j=G_RUN))
                nc.scalar.copy(rows_f[:, G_F:], g_max[:, 1:].rearrange("p (f j) -> p f j", j=G_RUN)).then_inc(g_rows_set, 1)

            for b in range(2):
                g_chunk(0, b, True)
            act.wait_ge(g_count_set, 1)
            n_all = act.value_load(g_count[0:1, 0:1], min_val=2, max_val=G_CHUNKS)
            with act.Fori(1, G_CHUNKS // 2) as it:
                for b in range(2):
                    with act.If(it * 2 + b < n_all):
                        g_chunk(it, b, False)

            for n in range(G_CHUNKS // 4):
                act.wait_ge(g_tail_turned, n + 1)
                nc.scalar.copy(g_tailT[0:G_F, n * 512:(n + 1) * 512], ps[4][0:G_F, :]).then_inc(g_tail_taken, 1)
                nc.scalar.copy(g_tmaxT[0:G_F, n * 512:(n + 1) * 512], ps[5][0:G_F, :]).then_inc(g_tail_taken, 1)
            for k in range(2):
                act.wait_ge(g_dT_set, k + 1)
                tgt = (g_dT, g_tmaxT)[k]
                nc.scalar.activation(tgt[0:G_F, :], tgt[0:G_F, :], ACT.Exp).then_inc(g_dT_exp, 1)
            for n in range(G_CHUNKS // 4):
                act.wait_ge(g_car_turned, n + 1)
                nc.scalar.copy(g_tail[:, 4 * n:4 * n + 4, 0:G_F],
                               ps[6][:, 0:4 * G_F].rearrange("p (c f) -> p c f", f=G_F)).then_inc(g_car_taken, 1)
                nc.scalar.copy(g_tail[:, 4 * n:4 * n + 4, G_F:G_OUT],
                               ps[7][:, 0:4 * G_F].rearrange("p (c f) -> p c f", f=G_F)[:, :, G_HF:]).then_inc(g_car_taken, 1)
            act.wait_ge(node_exp_in, 1)
            for k in range(3):
                nc.scalar.activation(n4[4 + k], n4[4 + k], ACT.Exp).then_inc(node_exp, 1)
            act.wait_ge(gate_root_in, 1)
            nc.scalar.activation(ln_var, ln_var, ACT.Sqrt).then_inc(gate_root, 1)
            act.wait_ge(gate_exp_in, 1)
            nc.scalar.activation(n4[8], n4[8], ACT.Exp).then_inc(gate_exp, 1)
            for n in range(8):
                act.wait_ge(out_turned, n + 1)
                nc.scalar.copy(out_ch[:, 2 * n:2 * n + 2, :].rearrange("p j s -> p (j s)"), ps[n % 2][:, :]).then_inc(out_laid, 1)

        @block.vector
        def _(dve):
            V = nc.vector
            done = [0]

            def step(ins):
                done[0] += 1
                ins.then_inc(dve_step, 1)
                dve.wait_ge(dve_step, done[0])

            def tt(o, a_, b_, op):
                return V.tensor_tensor(o, a_, b_, op)

            def ts(o, a_, s1, op0, s2=None, op1=None):
                return V.tensor_scalar(o, a_, s1, s2, op0, op1) if op1 is not None else V.tensor_scalar(o, a_, s1, None, op0)

            step(V.memset(ones, 1.0))
            def norm_means():
                dve.wait_ge(x_in, 32)
                for j in range(HALF):
                    ins = V.bn_stats(gn_stat[:, j, :], x_ch[:, j, :])
                step(ins)
                for j in range(HALF):
                    ins = V.bn_aggr(gn_mv[:, j, :], gn_stat[:, j, :])
                step(ins)
                V.tensor_copy(gn_mean, gn_mv[:, :, 0]).then_inc(gn_pair_in, 1)

            def norm_spread():
                dve.wait_ge(gn_pair, 1)
                step(tt(gn_dev, gn_mv[:, :, 0], ps[7][:, 0:HALF], ALU.subtract))
                step(tt(gn_dev, gn_dev, gn_dev, ALU.mult))
                tt(gn_dev, gn_dev, gn_mv[:, :, 1], ALU.add).then_inc(gn_pair_in, 1)

            def norm_variance():
                dve.wait_ge(gn_pair, 2)
                ts(gn_rstd, ps[7][:, 32:32 + HALF], 1e-5, ALU.add).then_inc(gn_ready, 1)

            def norm_scale():
                dve.wait_ge(gn_root, 1)
                step(V.reciprocal(gn_rstd, gn_rstd))
                V.scalar_tensor_tensor(gn_bias, ps[7][:, 0:HALF], -1.0, gn_rstd, ALU.mult, ALU.mult).then_inc(gn_ready, 1)

            def mix_maximum():
                dve.wait_ge(w_in, 16 * 10)
                al = alph[0:CH]
                step(V.tensor_reduce(al[:, 13:14], al[:, 0:5], AX_X, ALU.max))
                ts(al[:, 0:5], al[:, 0:5], al[:, 13:14], ALU.subtract).then_inc(alpha_exp_in, 1)

            def mix_permutations():
                dve.wait_ge(perm_in, 16)
                dve.wait_ge(alpha_exp, 1)
                al = alph[0:CH]
                step(V.tensor_reduce(al[:, 14:15], al[:, 8:13], AX_X, ALU.add))
                step(V.reciprocal(al[:, 15:16], al[:, 14:15]))
                step(ts(al[:, 0:5], al[:, 8:13], al[:, 15:16], ALU.mult))
                ts(perm[0:CH, 0, :], perm[0:CH, 0, :], al[:, 0:1], ALU.mult)
                n = 1
                for m, bs in enumerate(BLOCKS):
                    ins = ts(perm[0:CH, n:n + bs, :], perm[0:CH, n:n + bs, :], al[:, m + 1:m + 2], ALU.mult, 1.0 / bs, ALU.mult)
                    n += bs
                step(ins)
                dve.sem_inc(perm_scaled, 1)

            taken = [0]

            def sort(merge, key):
                for what, src, dst in merge:
                    s, d = key[src], key[dst]
                    if what[0] == "toggle":
                        step(ts(d, s, const[:, C_TOGGLE + what[1]:C_TOGGLE + what[1] + 1], ALU.mult))
                    elif what[0] == "flip":
                        dve.sem_inc(flip_in, 1)
                        taken[0] += key[0].shape[1] // 512
                        dve.wait_ge(flip_taken, taken[0])
                    else:
                        k, dist = what[1:]
                        if k is None:
                            sv = s.rearrange("p (a h d) -> p a h d", h=2, d=dist)
                            dv = d.rearrange("p (a h d) -> p a h d", h=2, d=dist)
                            tt(dv[:, :, 0], sv[:, :, 0], sv[:, :, 1], ALU.min)
                            step(tt(dv[:, :, 1], sv[:, :, 0], sv[:, :, 1], ALU.max))
                        else:
                            pat = "p (a s b h d) -> p a s b h d"
                            b_ = (1 << k) // (2 * dist)
                            sv = s.rearrange(pat, s=2, b=b_, h=2, d=dist)
                            dv = d.rearrange(pat, s=2, b=b_, h=2, d=dist)
                            for way in range(2):
                                lo, hi = sv[:, :, way, :, 0], sv[:, :, way, :, 1]
                                tt(dv[:, :, way, :, 0], lo, hi, (ALU.min, ALU.max)[way])
                                ins_ = tt(dv[:, :, way, :, 1], lo, hi, (ALU.max, ALU.min)[way])
                            step(ins_)

            def pack(key, cols, n_src):
                s, d = key[0][:, 0:cols].bitcast(I32), key[1][:, 0:cols].bitcast(I32)
                step(ts(s, s, float(n_src - 1), ALU.min, 0.0, ALU.max))
                step(ts(d, d, float(NONE), ALU.min, 0.0, ALU.max))
                step(ts(d, d, SRC_BITS, ALU.logical_shift_left, KEY_BASE, ALU.bitwise_or))
                step(tt(s, s, d, ALU.bitwise_or))

            def unpack(key, last, extra):
                k_, o_ = key[last].bitcast(I32), key[1 - last].bitcast(I32)
                step(ts(o_, k_, (1 << SRC_BITS) - 1, ALU.bitwise_and))
                step(ts(k_, k_, SRC_BITS, ALU.logical_shift_right, (1 << 14) - 1, ALU.bitwise_and))
                return ts(extra, k_, float(TOKENS - 1), ALU.min)

            def runs(key, run, k):
                d_ = key.bitcast(I32)
                n_ = key.shape[1] // run
                head = d_.rearrange("p (n j) -> p n j", j=run)[:, :, 0]
                tail = d_.rearrange("p (n j) -> p n j", j=run)[:, :, run - 1]
                V.tensor_copy(run_prev[:, 1:n_], tail[:, 0:n_ - 1])
                V.tensor_copy(ln_sum[:, 0:1], tail[:, n_ - 1:n_]).then_inc(last_set, 1)
                dve.wait_ge(last_shifted, k)
                step(V.tensor_copy(run_prev[:, 0:1], ps[2][:, 128:129]))
                step(tt(run_cont[:, 0:n_], head, run_prev[:, 0:n_], ALU.is_equal))
                step(tt(run_prev[:, 0:n_], head, tail, ALU.is_equal))
                step(tt(run_cont[:, 0:n_], run_cont[:, 0:n_], run_prev[:, 0:n_], ALU.mult))
                dve.sem_inc(cont_set, 1)

            def search_rows(key, nodes, k):
                nb = key.shape[1] // P
                p_ = key.bitcast(I32).rearrange("p (n j) -> p n j", j=P)[:, :, 0]
                step(ts(piv[0][:, 0:nb], p_, P - 1, ALU.bitwise_and))
                step(ts(piv[1][:, 0:nb], p_, 7, ALU.logical_shift_right))
                tt(hot_lo[:, 0:nb, :], bc(piv[0][:, 0:nb, None], [P, nb, P]), bc(iota[:, None, :], [P, nb, P]), ALU.is_equal)
                step(tt(hot_hi[:, 0:nb, :], bc(piv[1][:, 0:nb, None], [P, nb, NT]), bc(iota[:, None, 0:NT], [P, nb, NT]), ALU.is_equal))
                dve.sem_inc(hot_set, 1)
                dve.wait_ge(hist_done, k)
                step(V.tensor_copy(nodes.tot, ps[2][:, 0:NT]))
                dve.sem_inc(hist_set, 1)
                dve.wait_ge(cum_done, k)
                step(V.tensor_copy(nodes.count, ps[3][:, 128:128 + NT]))
                step(V.tensor_tensor_scan(nodes.start, ones[:, 0:NT], nodes.count, 0.0, ALU.mult, ALU.add))
                step(tt(nodes.run, nodes.start, nodes.count, ALU.subtract))
                step(tt(nodes.run, nodes.run, ps[3][:, 0:NT], ALU.add))
                step(ts(nodes.run, nodes.run, -1.0, ALU.add, 0.0, ALU.max))
                step(V.tensor_copy(nodes.run_i, nodes.run))
                dve.sem_inc(run_set, 1)

            def search_ends(nodes, k, run, rows, below):
                for n_ in range(4):
                    at = slice(16 * n_, 16 * n_ + 16)
                    dve.wait_ge(found[k - 1][n_], 256)
                    step(tt(below, rows[:, at, :], bc(node[:, at, None], [P, 16, P]), ALU.is_le))
                    step(V.tensor_reduce(nodes.count[:, at], below, AX_X, ALU.add))
                V.memset(nodes.end[:, 0:1], 0.0)
                step(V.scalar_tensor_tensor(nodes.end[:, 1:], nodes.run, float(P), nodes.count, ALU.mult, ALU.add))
                dve.sem_inc(ends_set, 1)
                dve.wait_ge(starts_done, k)
                end = nodes.end[:, 1:]
                step(V.tensor_copy(nodes.start, ps[3][:, 256:256 + NT]))
                step(tt(nodes.has, end, nodes.start, ALU.is_gt))
                step(ts(nodes.pos, end, -1.0, ALU.add, 0.0, ALU.max))
                step(ts(nodes.prun, nodes.pos, run.bit_length() - 1, ALU.logical_shift_right))
                step(ts(nodes.cidx_f, nodes.prun, float(run), ALU.mult))
                step(tt(nodes.carried, nodes.start, nodes.cidx_f, ALU.is_lt))
                step(tt(nodes.carried, nodes.carried, nodes.has, ALU.mult))
                step(ts(nodes.cidx, nodes.prun, -1.0, ALU.add, 0.0, ALU.max))
                step(ts(nodes.seed_f, nodes.has, -FAR, ALU.mult, FAR, ALU.add))
                step(tt(nodes.seed, nodes.seed_f, nodes.start, ALU.add))
                dve.sem_inc(pos_set, 1)

            def layer_norm(k, eps, square_):
                step(V.tensor_reduce(ln_sum, t_tok, AX_X, ALU.add))
                step(ts(ln_sum, ln_sum, 1.0 / CH, ALU.mult))
                step(tt(y_tok, t_tok, bc(ln_sum[:, :, None], [P, NT, CH]), ALU.subtract))
                for n_ in range(2):
                    part = slice(n_ * NT // 2, (n_ + 1) * NT // 2)
                    step(tt(square_, y_tok[:, part], y_tok[:, part], ALU.mult))
                    step(V.tensor_reduce(ln_var[:, part], square_, AX_X, ALU.add))
                step(ts(ln_var, ln_var, 1.0 / CH, ALU.mult, eps, ALU.add))
                dve.sem_inc(root_in, 1)
                dve.wait_ge(root_out, k)
                step(V.reciprocal(ln_var, ln_var))
                step(tt(y_tok, y_tok, bc(ln_var[:, :, None], [P, NT, CH]), ALU.mult))
                dve.sem_inc(y_set, 1)

            def conv_add(j):
                dve.wait_ge(conv_done, j + 1)
                xs = x_ch[:, 2 * j:2 * j + 2, :].rearrange("p j s -> p (j s)")
                tt(xs, xs, ps[4 + j % 2][:, :], ALU.add).then_inc(conv_added, 1)

            dve.wait_ge(a_edges_in, 32)
            pack(a_key, A_EDGES // P, A_NODES)
            step(V.memset(a_key[0][:, A_EDGES // P:].bitcast(I32), PAD_KEY))
            dve.wait_ge(const_in, 16)
            between = {3: norm_means, 4: norm_spread, 5: norm_variance, 6: norm_scale, 7: mix_maximum, 8: mix_permutations}
            for k, merge in enumerate(A_MERGES, 1):
                sort(merge, a_key)
                if k in between:
                    between[k]()
                if k > FLIP_FROM:
                    conv_add(k - FLIP_FROM - 1)
            step(unpack(a_key, A_LAST, list_nodes[:, 0:A_W]))
            dve.sem_inc(a_list_set, 1)
            runs(a_key[A_LAST], A_RUN, 1)
            search_rows(a_key[A_LAST], a_nodes, 1)
            for j in range(6, 8):
                conv_add(j)
            search_ends(a_nodes, 1, A_RUN, a_found, a_below)
            dve.wait_ge(t_taken, HALF // 2)
            layer_norm(1, 1e-5, square_a)

            A_STEPS_DVE = 6

            def a_chunk(it, b, first):
                n_done = [0]

                def link(ins):
                    n_done[0] += 1
                    ins.then_inc(dve_loop_a, 1)
                    dve.wait_ge(dve_loop_a, it * (2 * A_STEPS_DVE) + (b * A_STEPS_DVE + n_done[0]))

                c1 = it * 2 + (b + 1)
                dve.wait_ge(a_idx_in[b], it * 48 + 48)
                tt(a_nst[:, 1:], a_didx[b][:, 1:], a_didx[b][:, :-1], ALU.is_equal).then_inc(a_flags, 1)
                dve.wait_ge(a_laid, c1)
                link(V.tensor_tensor_scan(q_edge, a_go[:, 0:CH * A_RUN], q_fm, 0.0, ALU.mult, ALU.add))
                k_f = kv[b][:, :, 0:CH].rearrange("p j f -> p f j")
                link(tt(a_prod.rearrange("p (f j) -> p f j", j=A_RUN), q_edge.rearrange("p (f j) -> p f j", j=A_RUN), k_f, ALU.mult))
                link(V.tensor_reduce(a_score.rearrange("p (h j) -> p h j", j=A_RUN),
                                     a_prod.rearrange("p (h d j) -> p h j d", d=A_DIM, j=A_RUN), AX_X, ALU.add))
                link(ts(a_score, a_score, A_DIM ** -0.5, ALU.mult, -5.0, ALU.max))
                ts(a_score, a_score, 5.0, ALU.min).then_inc(a_scored, 1)
                dve.wait_ge(a_weighed, c1)
                w = a_msg[:, CH * A_RUN:].rearrange("p (h j) -> p h j", j=A_RUN)
                link(tt(a_msg[:, 0:CH * A_RUN].rearrange("p (h d j) -> p h d j", d=A_DIM, j=A_RUN),
                        kv[b][:, :, CH:].rearrange("p j (h d) -> p h d j", d=A_DIM),
                        bc(w[:, :, None, :], [P, A_HEADS, A_DIM, A_RUN]), ALU.mult))
                dve.sem_inc(a_used, 1)
                if not first:
                    dve.wait_ge(a_rows_set, c1 - 1)
                link(V.tensor_tensor_scan(a_sum, a_go, a_msg, 0.0, ALU.mult, ALU.add))
                dve.sem_inc(a_summed, 1)
                assert n_done[0] == A_STEPS_DVE

            step(V.memset(a_nst[:, 0:1], 0.0))
            dve.wait_ge(g_edges_in, 32)
            pack(g_key, G_W, TOKENS)
            for k, merge in enumerate(G_MERGES, 1):
                sort(merge, g_key)
                for b in range(2 * (k >= PAIR_FROM)):
                    a_chunk(k - PAIR_FROM, b, k == PAIR_FROM and b == 0)
            step(unpack(g_key, G_LAST, list_nodes))
            dve.sem_inc(g_list_set, 1)
            dve.wait_ge(cont_out, 16)
            runs(g_key[G_LAST], G_RUN, 2)
            search_rows(g_key[G_LAST], g_nodes, 2)

            dve.wait_ge(a_tail_taken, A_CHUNKS // 4)
            dve.wait_ge(a_tail_in, 32)
            step(V.tensor_tensor_scan(a_carT[0:A_F], a_cont[0:A_F], a_tailT[0:A_F], 0.0, ALU.mult, ALU.add))
            dve.sem_inc(a_carried, 1)
            dve.wait_ge(a_ends_in, 16 * 2 * NT)
            tt(a_before, a_before, bc(a_nodes.carried[:, :, None], [P, NT, A_F]), ALU.mult)
            step(tt(a_end, a_end, bc(a_nodes.has[:, :, None], [P, NT, A_F]), ALU.mult))
            step(tt(a_end, a_end, a_before, ALU.add))
            z = a_end[:, :, CH:]
            step(ts(z, z, 1e-6, ALU.add))
            step(V.reciprocal(z, z))
            wv = a_end[:, :, 0:CH].rearrange("p i (h d) -> p i h d", d=A_DIM)
            step(tt(wv, wv, bc(z[:, :, :, None], [P, NT, A_HEADS, A_DIM]), ALU.mult))
            step(tt(t_tile, t_tile, a_end[:, :, 0:CH].rearrange("p (h i) c -> p h i c", h=2), ALU.add))
            dve.wait_ge(g_list_out, 48)
            layer_norm(2, 1e-5, square)

            dve.wait_ge(gw_in, 16 * 12)
            dve.wait_ge(h_done, 1)
            for half in range(2):
                V_last = V.tensor_copy(h_tok[:, half * 32:half * 32 + 32, 0:G_HF], ps[2 + half][:, :].rearrange("p (i f) -> p i f", f=G_HF))
            step(V_last)
            hh = h_tok[:, :, 0:G_HF]
            prod = h_prod.rearrange("p i h k -> p i (h k)")
            step(tt(prod, hh, bc(att[:, 0:1, :], [P, NT, G_HF]), ALU.mult))
            step(V.tensor_reduce(h_tok[:, :, G_HF:], h_prod, AX_X, ALU.add))
            step(tt(prod, hh, bc(att[:, 1:2, :], [P, NT, G_HF]), ALU.mult))
            step(V.tensor_reduce(ad_tok, h_prod, AX_X, ALU.add))
            dve.sem_inc(h_set, 1)
            search_ends(g_nodes, 2, G_RUN, g_found, g_below)
            cnt = g_count[0:1]
            step(V.tensor_copy(cnt[:, 3:4], ps[3][0:1, 256 + NT:257 + NT]))
            step(ts(cnt[:, 3:4], cnt[:, 3:4], float(P * G_RUN - 1), ALU.add))
            step(ts(cnt[:, 3:4], cnt[:, 3:4], (P * G_RUN).bit_length() - 1, ALU.logical_shift_right))
            step(ts(cnt[:, 0:1], cnt[:, 3:4], 2.0, ALU.max))
            step(ts(cnt[:, 3:4], cnt[:, 0:1], 1.0, ALU.add))
            step(ts(cnt[:, 1:2], cnt[:, 3:4], 1, ALU.logical_shift_right))
            step(ts(cnt[:, 2:3], cnt[:, 0:1], 1, ALU.logical_shift_right))
            step(ts(cnt[:, 4:5], cnt[:, 0:1], -16.0, ALU.mult, 16.0 * G_CHUNKS, ALU.add))
            dve.sem_inc(g_count_set, 1)
            for grp in range(16):
                dve.wait_ge(hid_used, 4 * grp + 4)
                i0 = grp // 8 * 32 + grp % 8 * 4
                for k in range(2):
                    ins = tt(exp_out[:, i0 + 2 * k:i0 + 2 * k + 2, :], ps[6 + k][:, :].rearrange("p (i n) -> p i n", n=4 * CH),
                             bc(b2[:, None, :], [P, 2, 4 * CH]), ALU.add)
                ins.then_inc(exp_taken, 1)

            G_STEPS_DVE = 9
            V.memset(g_max[:, 0:1], 0.0)
            step(V.memset(g_nst.rearrange("p (h j) -> p h j", j=G_RUN)[:, :, 0:1], 0.0))

            def g_chunk(it, b, first):
                n_done = [0]

                def link(ins):
                    n_done[0] += 1
                    ins.then_inc(dve_loop_g, 1)
                    dve.wait_ge(dve_loop_g, it * (2 * G_STEPS_DVE) + (b * G_STEPS_DVE + n_done[0]))

                c1 = it * 2 + (b + 1)
                dve.wait_ge(g_idx_in[b], it * 64 + 64)
                n_ = G_RUN - 1
                link(tt(g_nst.rearrange("p (h j) -> p h j", j=G_RUN)[:, :, 1:], bc(g_didx[b][:, None, 1:], [P, G_HEADS, n_]),
                        bc(g_didx[b][:, None, :-1], [P, G_HEADS, n_]), ALU.is_equal))
                ts(g_cut, g_nst, BIG, ALU.mult, -BIG, ALU.add).then_inc(g_flags, 1)
                dve.wait_ge(g_laid, c1)
                link(V.tensor_tensor_scan(ad_edge, g_nst, ad_fm, 0.0, ALU.mult, ALU.add))
                hs_f = hs[b].rearrange("p j f -> p f j")
                link(tt(g_x.rearrange("p (h j) -> p h j", j=G_RUN), ad_edge.rearrange("p (h j) -> p h j", j=G_RUN), hs_f[:, G_HF:], ALU.add))
                link(V.scalar_tensor_tensor(g_e, g_x, 0.2, g_x, ALU.mult, ALU.max))
                if not first:
                    dve.wait_ge(g_rows_set, c1 - 1)
                link(V.tensor_tensor_scan(g_max[:, 1:], g_cut, g_e, 0.0, ALU.add, ALU.max))
                tt(g_em, g_e, g_max[:, 1:], ALU.subtract)
                link(tt(g_dm, g_max[:, :-1], g_max[:, 1:], ALU.subtract))
                link(tt(g_dm, g_dm, g_cut, ALU.add))
                dve.sem_inc(g_max_set, 1)
                dve.wait_ge(g_weighed, c1)
                w = g_msg[:, G_HF * G_RUN:].rearrange("p (h j) -> p h j", j=G_RUN)
                link(tt(g_msg[:, 0:G_HF * G_RUN].rearrange("p (h k j) -> p h k j", k=G_EXP, j=G_RUN),
                        hs[b][:, :, 0:G_HF].rearrange("p j (h k) -> p h k j", k=G_EXP),
                        bc(w[:, :, None, :], [P, G_HEADS, G_EXP, G_RUN]), ALU.mult))
                dve.sem_inc(g_used, 1)
                link(V.tensor_tensor_scan(g_sum, g_corr_f, g_msg, 0.0, ALU.mult, ALU.add))
                dve.sem_inc(g_summed, 1)
                assert n_done[0] == G_STEPS_DVE

            for b in range(2):
                g_chunk(0, b, b == 0)
            n_all = dve.value_load(g_count[0:1, 0:1], min_val=2, max_val=G_CHUNKS)
            with dve.Fori(1, G_CHUNKS // 2) as it:
                for b in range(2):
                    with dve.If(it * 2 + b < n_all):
                        g_chunk(it, b, False)

            dve.wait_ge(g_tail_in, 32)
            m_tail = g_tail[:, :, G_F:G_OUT]
            V.tensor_copy(g_tail[:, :, G_OUT:G_OUT + G_HF].rearrange("p c (h k) -> p c h k", k=G_EXP),
                          bc(m_tail[:, :, :, None], [P, G_CHUNKS, G_HEADS, G_EXP]))
            step(V.tensor_copy(g_tail[:, :, G_OUT + G_HF:], m_tail))
            dve.sem_inc(g_rep_set, 1)
            cut, tmax, cmax, d_t, tail = (x[0:G_F] for x in (g_cutT, g_tmaxT, g_cmaxT, g_dT, g_tailT))
            step(ts(cut, cut, BIG, ALU.mult, -BIG, ALU.add))
            dve.wait_ge(g_tail_taken, G_CHUNKS // 2)
            V.memset(cmax[:, 0:1], -BIG)
            step(V.tensor_tensor_scan(cmax[:, 1:], cut, tmax, -BIG, ALU.add, ALU.max))
            step(tt(d_t, cmax[:, :-1], cmax[:, 1:], ALU.subtract))
            step(tt(d_t, d_t, cut, ALU.add))
            dve.sem_inc(g_dT_set, 1)
            step(tt(tmax, tmax, cmax[:, 1:], ALU.subtract))
            dve.sem_inc(g_dT_set, 1)
            dve.wait_ge(g_dT_exp, 2)
            step(tt(tail, tail, tmax, ALU.mult))
            step(V.tensor_tensor_scan(cut, d_t, tail, 0.0, ALU.mult, ALU.add))
            dve.sem_inc(g_carried, 1)

            dve.wait_ge(g_ends_in, 16 * 2 * NT)
            m_end, m_before, e_own, m_all, w_end, w_before, w_own_, sc, ex, rank, cmp_, den = n4
            step(tt(den, h_tok[:, :, G_HF:], ad_tok, ALU.add))
            step(V.scalar_tensor_tensor(e_own, den, 0.2, den, ALU.mult, ALU.max))
            for m_, rows_, on in ((m_end, g_end, g_nodes.has), (m_before, g_before, g_nodes.carried)):
                step(ts(g_nodes.tot, on, BIG, ALU.mult, -BIG, ALU.add))
                step(tt(m_, rows_[:, :, G_F:], bc(on[:, :, None], [P, NT, 4]), ALU.mult))
                step(tt(m_, m_, bc(g_nodes.tot[:, :, None], [P, NT, 4]), ALU.add))
            step(tt(m_all, m_end, m_before, ALU.max))
            step(tt(m_all, m_all, e_own, ALU.max))
            for w_, m_ in ((w_end, m_end), (w_before, m_before), (w_own_, e_own)):
                ins = tt(w_, m_, m_all, ALU.subtract)
            step(ins)
            dve.sem_inc(node_exp_in, 1)
            dve.wait_ge(node_exp, 3)
            agg = n16[0].rearrange("p (i h k) -> p i h k", h=4, k=4)
            part = n16[1].rearrange("p (i h k) -> p i h k", h=4, k=4)

            def heads(x):
                return x.rearrange("p i (h k) -> p i h k", k=4)

            def per_head(x):
                return bc(x[:, :, :, None], [P, NT, 4, 4])

            step(tt(agg, heads(g_end[:, :, 0:G_HF]), per_head(w_end), ALU.mult))
            step(tt(part, heads(g_before[:, :, 0:G_HF]), per_head(w_before), ALU.mult))
            step(tt(n16[0], n16[0], n16[1], ALU.add))
            step(tt(part, heads(h_tok[:, :, 0:G_HF]), per_head(w_own_), ALU.mult))
            step(tt(n16[0], n16[0], n16[1], ALU.add))
            step(tt(den, g_end[:, :, G_HF:G_F], w_end, ALU.mult))
            step(tt(cmp_, g_before[:, :, G_HF:G_F], w_before, ALU.mult))
            step(tt(den, den, cmp_, ALU.add))
            step(tt(den, den, w_own_, ALU.add))
            step(ts(den, den, 1e-16, ALU.add))
            step(V.reciprocal(den, den))
            step(tt(agg, agg, per_head(den), ALU.mult))
            flat = n16[0].rearrange("p (i f) -> p i f", f=G_HF)

            def all_nodes(v):
                return bc(att[:, v:v + 1, :], [P, NT, G_HF])

            step(tt(flat, flat, all_nodes(2), ALU.add))
            step(V.tensor_reduce(ln_sum, flat, AX_X, ALU.add))
            step(ts(ln_sum, ln_sum, 1.0 / G_HF, ALU.mult))
            step(tt(flat, flat, bc(ln_sum[:, :, None], [P, NT, G_HF]), ALU.subtract))
            sq = n16[1].rearrange("p (i f) -> p i f", f=G_HF)
            step(tt(sq, flat, flat, ALU.mult))
            step(V.tensor_reduce(ln_var, sq, AX_X, ALU.add))
            step(ts(ln_var, ln_var, 1.0 / G_HF, ALU.mult, 1e-5, ALU.add))
            dve.sem_inc(gate_root_in, 1)
            dve.wait_ge(gate_root, 1)
            step(V.reciprocal(ln_var, ln_var))
            step(tt(flat, flat, bc(ln_var[:, :, None], [P, NT, G_HF]), ALU.mult))
            step(tt(flat, flat, all_nodes(3), ALU.mult))
            step(tt(flat, flat, all_nodes(4), ALU.add))
            step(V.tensor_reduce(sc, n16[0].rearrange("p (i h k) -> p i k h", h=4, k=4), AX_X, ALU.add))
            step(ts(sc, sc, 1.0 / G_HEADS, ALU.mult))
            step(V.memset(rank, 0.0))
            for j in range(4):
                if j < 3:
                    tt(cmp_[:, :, j + 1:], bc(sc[:, :, j:j + 1], [P, NT, 3 - j]), sc[:, :, j + 1:], ALU.is_ge)
                step(tt(cmp_[:, :, 0:j + 1], bc(sc[:, :, j:j + 1], [P, NT, j + 1]), sc[:, :, 0:j + 1], ALU.is_gt))
                step(tt(rank, rank, cmp_, ALU.add))
            step(ts(rank, rank, 2.0, ALU.is_lt))
            step(V.tensor_reduce(ln_sum, sc, AX_X, ALU.max))
            step(tt(ex, sc, bc(ln_sum[:, :, None], [P, NT, 4]), ALU.subtract))
            dve.sem_inc(gate_exp_in, 1)
            dve.wait_ge(gate_exp, 1)
            step(tt(ex, ex, rank, ALU.mult))
            step(V.tensor_reduce(ln_sum, ex, AX_X, ALU.add))
            step(V.reciprocal(ln_sum, ln_sum))
            step(tt(ex, ex, bc(ln_sum[:, :, None], [P, NT, 4]), ALU.mult))
            eo = exp_out.rearrange("p i (e c) -> p (i e) c", c=CH)
            step(tt(eo, eo, bc(ex.rearrange("p i e -> p (i e)")[:, :, None], [P, NT * 4, CH]), ALU.mult))
            for e in range(4):
                step(tt(t_tile, t_tile, exp_out[:, :, e * CH:(e + 1) * CH].rearrange("p (h i) c -> p h i c", h=2), ALU.add))
            dve.sem_inc(out_set, 1)


OUT_SHAPE = (IMAGES, CH, SIDE, SIDE)


def kernel(debug=None, **inputs):
    import concourse.bacc as bacc
    from concourse.bass_utils import run_bass_kernel_spmd

    def given(name, shape=None):
        a = np.ascontiguousarray(inputs[name])
        return a.reshape(shape) if shape else a

    w = given("L0_conv_weight", (CH, CH, TAPS))
    const, perm = shape_constants()
    arrays = {
        "x": given("x", (IMAGES, CH, PIX)),
        "alphas": given("L0_conv_alphas"),
        "w_own": np.ascontiguousarray(w.transpose(1, 0, 2)).reshape(CH, CH * TAPS),
        "w_blocks": np.stack([np.ascontiguousarray(
            w.reshape(CH // bs, bs, CH // bs, bs, TAPS).transpose(2, 1, 0, 3, 4)).reshape(CH, CH * TAPS) for bs in BLOCKS]),
        "kv": np.concatenate([given("L1_attn_k", (A_NODES, CH)), given("L1_attn_v", (A_NODES, CH))], axis=1),
        "a_edges": given("L1_attn_edge_index"),
        "g_edges": given("L1_ffn_edge_index"),
        "wgat": given("L1_ffn_W_gat"), "att_src": given("L1_ffn_att_src", (G_HF,)), "att_dst": given("L1_ffn_att_dst", (G_HF,)),
        "b_gat": given("L1_ffn_b_gat"), "gamma": given("L1_ffn_ln_gamma"), "beta": given("L1_ffn_ln_beta"),
        "w1": given("L1_ffn_W1"), "b1": np.ascontiguousarray(given("L1_ffn_b1").T), "w2": given("L1_ffn_W2"), "b2": given("L1_ffn_b2"),
        "const": const, "perm": perm,
    }
    nc = bacc.Bacc("TRN2", target_bir_lowering=False, num_devices=1)
    io = {n: nc.dram_tensor(f"in_{n}", a.shape, mybir.dt.from_np(a.dtype), kind="ExternalInput").ap() for n, a in arrays.items()}
    io["out"] = nc.dram_tensor("out", (IMAGES, CH, PIX), F32, kind="ExternalOutput").ap()
    build(nc, io, debug)
    r = run_bass_kernel_spmd(nc, [{f"in_{n}": a for n, a in arrays.items()}], core_ids=[0])
    return r.results[0]["out"].reshape(OUT_SHAPE)
```

```python
from contextlib import ExitStack

import numpy as np

import concourse.bass as bass
from concourse import mybir

F32 = mybir.dt.float32
BF16 = mybir.dt.bfloat16
F16 = mybir.dt.float16
I32 = mybir.dt.int32
ALU = mybir.AluOpType
ACT = mybir.ActivationFunctionType
AX_X = mybir.AxisListType.X

P = 128
IMAGES, CH, SIDE = 32, 64, 16
PIX = SIDE * SIDE
HALF = IMAGES // 2
TOKENS = IMAGES * PIX
NT = TOKENS // P
PAD_SIDE = SIDE + 2
TAPS = 9
BLOCKS = (2, 4, 8, 16)
N_SHIFT = sum(BLOCKS)

A_NODES = 5000
A_EDGES = 80000
A_W = 1024
A_NEAR = -(-A_NODES // P)
A_HEADS, A_DIM = 8, 8
A_F = CH + A_HEADS
A_RUN = 32
A_CHUNKS = 20
A_USED = A_CHUNKS * P * A_RUN
A_RUNS = A_CHUNKS * P

G_EDGES = 262144
G_W = G_EDGES // P
G_HEADS, G_EXP = 4, 4
G_HF = G_HEADS * G_EXP
G_ROW = G_HF + G_HEADS
G_F = G_HF + G_HEADS
G_OUT = G_F + G_HEADS
G_RUN = 64
G_CHUNKS = G_W // G_RUN
G_RUNS = G_CHUNKS * P
HID = 2 * CH
PICKS = 28
BATCH = 4
BATCHES = PICKS // BATCH
CANDS = 8
K_TILES = NT // CANDS
PICK_W = CANDS * G_HF
SPLITS = 3

SRC_BITS = 13
NONE = TOKENS
KEY_BASE = 0x40000000
PAD_KEY = KEY_BASE | (NONE << SRC_BITS)
BIG = 1.0e30
FAR = float(1 << 20)

C_IDENT, C_TRIU, C_SHIFT, C_WRAP, C_PAIR, C_IOTA, C_NODE, C_TOGGLE = (0, 128, 256, 384, 512, 640, 768, 832)
C_COLS = 840


def shape_constants():
    c = np.zeros((P, C_COLS), np.float32)
    p = np.arange(P)
    c[p, C_IDENT + p] = 1.0
    c[:, C_TRIU:C_TRIU + P] = p[:, None] <= p[None, :]
    c[p[:-1], C_SHIFT + p[1:]] = 1.0
    c[P - 1, C_WRAP] = 1.0
    c[:, C_PAIR:C_PAIR + P] = 0.5 * (p[:, None] // 2 == p[None, :] // 2)
    c[:, C_IOTA:C_IOTA + P] = p[None, :]
    c[:, C_NODE:C_NODE + NT] = p[:, None] + P * np.arange(NT)[None, :]
    sign = [np.where((p >> m) & 1, -1.0, 1.0) for m in range(7)]
    for m in range(8):
        c[:, C_TOGGLE + m] = (sign[m] if m < 7 else 1.0) * (sign[m - 1] if m else 1.0)
    perm = np.zeros((CH, 1 + N_SHIFT, 2, CH), np.float32)
    m = np.arange(CH)
    perm[m, 0, :, m] = 1.0
    n = 1
    for bs in BLOCKS:
        for k in range(bs):
            perm[m // bs * bs + (m % bs - k) % bs, n, :, m] = 1.0
            n += 1
    return c, perm.reshape(CH, (1 + N_SHIFT) * P)


def sort_steps(width):
    log_w = width.bit_length() - 1
    merges, cur = [], 0
    for k in range(1, log_w + 8):
        steps, cross = [], k - log_w
        if cross == 0:
            steps.append((("toggle", cross), cur, 1 - cur))
            cur = 1 - cur
        if cross > 0:
            steps.append((("enter", cross), cur, cur))
            to = (cur + cross + 1) % 2
            steps += [(("group", g, cross), cur, to) for g in range(GROUPS)]
            cur = to
        for s in reversed(range(min(k, log_w))):
            steps.append((("stage", k if k < log_w else None, 1 << s), cur, 1 - cur))
            cur = 1 - cur
        merges.append(steps)
    return merges, cur


GROUPS = 2
A_MERGES, A_LAST = sort_steps(A_W)
G_MERGES, G_LAST = sort_steps(G_W)
FLIP_FROM = A_W.bit_length()

COST = {"stage": lambda *_: 2.3, "toggle": lambda *_: 1.2, "enter": lambda *_: 4.0, "group": lambda g, cross: 1.25 * cross + 0.5}
CHUNK_COST, FIRST_CHUNK, CHUNK_EVERY, TAILS_AFTER, CARRIES_AFTER = 12.0, 60.0, 30.0, 16.0, 26.0


def interleaved():
    order, at, chunk, part, since = [], 0.0, 0, 0, 0.0
    carries = [("tails", TAILS_AFTER), ("carries", CARRIES_AFTER)]
    for step in (s for m in G_MERGES for s in m):
        order.append(("step", step))
        at += COST[step[0][0]](*step[0][1:])
        if chunk < A_CHUNKS:
            if at >= FIRST_CHUNK + CHUNK_EVERY * chunk:
                order.append((("lay", "score", "sum")[part], chunk))
                at += CHUNK_COST / 3
                part = (part + 1) % 3
                chunk += part == 0
        else:
            since += COST[step[0][0]](*step[0][1:])
            if carries and since >= carries[0][1]:
                order.append((carries.pop(0)[0], None))
    while chunk < A_CHUNKS:
        order.append((("lay", "score", "sum")[part], chunk))
        part = (part + 1) % 3
        chunk += part == 0
    return order + [(what, None) for what, _ in carries] + [("sorted", None)]


SORT_AND_ATTEND = interleaved()
A_PIECES = ((0, NT // 8), (NT // 8, NT // 16 * 5), (NT // 16 * 5, NT // 2))
FINISH_ORDER = ((0, 0), (0, 1), (0, 2), (0, 3), (1, 0), (1, 1), (1, 2), (2, 0), (1, 3), (2, 1), (2, 2), (2, 3))
G_PIECES = tuple((NT // 16 * lo, NT // 16 * hi) for lo, hi in ((0, 3), (3, 6), (6, 8)))


def build(nc, io, debug=None):
    with ExitStack() as ctx:
        def sem(name):
            return ctx.enter_context(nc.semaphore(name))

        def dram(name, shape, dt):
            kind = "ExternalOutput" if debug and name in debug else "Internal"
            return nc.dram_tensor(name, shape, dt, kind=kind).ap()

        d_asrc = dram("d_asrc", (P * A_W,), I32)
        d_adst = dram("d_adst", (P * A_W,), I32)
        d_adstq = dram("d_adstq", (P * A_W,), I32)
        d_gsrc = dram("d_gsrc", (G_EDGES,), I32)
        d_gdst = dram("d_gdst", (G_EDGES,), I32)
        d_gdstq = dram("d_gdstq", (G_EDGES,), I32)
        d_q = dram("d_q", (TOKENS, CH), F32)
        d_qseed = dram("d_qseed", (A_USED, CH), F32)
        d_as = dram("d_as", (A_USED, A_F), F32)
        d_acont = dram("d_acont", (P * A_W // A_RUN,), F32)
        d_ac = dram("d_ac", (A_RUNS, A_F), F32)
        d_h = dram("d_h", (TOKENS, G_ROW), F32)
        d_ad = dram("d_ad", (TOKENS, G_HEADS), F32)
        d_adseed = dram("d_adseed", (G_EDGES, G_HEADS), F32)
        d_gs = dram("d_gs", (G_EDGES, G_OUT), F32)
        d_gcont = dram("d_gcont", (G_RUNS,), F32)
        d_gc = dram("d_gc", (G_RUNS, G_OUT), F32)

        LIMIT = 53200
        arena = ctx.enter_context(nc.sbuf_tensor("arena", [P, LIMIT], F32))

        class Region:
            def __init__(self, at):
                self.at = at

            def take(self, n, dt=F32):
                a = self.at
                self.at += n
                assert self.at <= LIMIT, self.at
                v = arena[:, a:a + n]
                return v if dt == F32 else v.bitcast(dt)

        r = Region(0)
        const = r.take(C_COLS)
        ident = const[:, C_IDENT:C_IDENT + P]
        triu = const[:, C_TRIU:C_TRIU + P]
        shift = const[:, C_SHIFT:C_SHIFT + P]
        wrap = const[:, C_WRAP:C_WRAP + P]
        pair = const[:, C_PAIR:C_PAIR + P]
        iota = const[:, C_IOTA:C_IOTA + P]
        node = const[:, C_NODE:C_NODE + NT]
        ones = r.take(P)
        ident16 = r.take(P // 2, F16)
        zeros = r.take(512)
        t_tok = r.take(NT * CH).rearrange("p (i c) -> p i c", c=CH)
        y_tok = r.take(NT * CH).rearrange("p (i c) -> p i c", c=CH)
        t_tile, y_tile = (x.rearrange("p (i h) c -> p h i c", h=2) for x in (t_tok, y_tok))

        def slot(tile):
            return tile % (NT // 2) * 2 + tile // (NT // 2)

        def tiles_of(piece, below=NT):
            return [t for i in range(*piece) for t in (i, i + NT // 2) if t < below]

        g_key_at = r.at
        g_key = [r.take(G_W) for _ in range(2)]
        a_key_at = r.at
        a_key = [r.take(A_W) for _ in range(2)]

        def node_table(dt=F32):
            return r.take(NT, dt)

        class Nodes:
            def __init__(self):
                self.run = node_table()
                self.run_i = node_table(I32)
                self.count = node_table()
                self.end = r.take(NT + 1)
                self.start = node_table()
                self.has = node_table()
                self.pos_f = node_table()
                self.pos = node_table(I32)
                self.prun = node_table(I32)
                self.cidx_f = node_table()
                self.cidx = node_table(I32)
                self.carried = node_table()
                self.seed_f = node_table()
                self.seed = node_table(I32)
                self.tot = node_table()

        a_nodes, g_nodes = Nodes(), Nodes()
        small = r.take(640)
        g_count = small[:, 448:453].bitcast(I32)
        far_count = small[:, 456:457].bitcast(I32)
        piv = [small[:, 0:16].bitcast(I32), small[:, 16:32].bitcast(I32)]
        gn_stat = small[:, 32:32 + HALF * 6].rearrange("p (j s) -> p j s", s=6)
        gn_mv = small[:, 128:160].rearrange("p (j s) -> p j s", s=2)
        gn_mean = small[:, 160:176]
        gn_dev = small[:, 176:192]
        gn_rstd = small[:, 192:208]
        gn_bias = small[:, 208:224]
        alph = small[:, 224:240]
        ln_sum = small[:, 256:320]
        ln_var = small[:, 320:384]
        run_prev = small[:, 384:416]
        run_cont = small[:, 416:448]
        first = r.at

        kv = [r.take(A_RUN * 2 * CH).rearrange("p (j f) -> p j f", f=2 * CH) for _ in range(2)]
        y_at = C_COLS + P + P // 2 + 512 + NT * CH
        rr = Region(y_at)
        list_nodes = rr.take(G_W, I32)
        far_edge = list_nodes[:, A_W:].bitcast(F32)
        hot_lo = rr.take(16 * P // 2, BF16).rearrange("p (n j) -> p n j", j=P)
        hot_hi = rr.take(16 * NT // 2, BF16).rearrange("p (n j) -> p n j", j=NT)
        assert rr.at <= y_at + NT * CH
        a_sidx = [r.take(A_RUN, I32) for _ in range(2)]
        a_didx = [r.take(A_RUN, I32) for _ in range(2)]
        a_fidx = [r.take(4, I32) for _ in range(2)]
        mid = r.at
        c = Region(mid)
        x_ch = c.take(HALF * PIX).rearrange("p (j s) -> p j s", s=PIX)
        y_pad = c.take(HALF * PAD_SIDE ** 2).rearrange("p (j y x) -> p j y x", y=PAD_SIDE, x=PAD_SIDE)
        w_taps = c.take(TAPS * P).rearrange("p (t o) -> p t o", o=P)
        w_dup = c.take(len(BLOCKS) * 2 * CH * TAPS).rearrange("p (b n) -> p b n", b=len(BLOCKS))
        a_below = w_dup.rearrange("p b n -> p (b n)")[:, 0:16 * P].rearrange("p (n j) -> p n j", j=P)
        a_found = Region(c.at).take(NT * P, I32).rearrange("p (n j) -> p n j", j=P)
        w_own = c.take(CH * TAPS)
        square_a = y_pad.rearrange("p j y x -> p (j y x)")[:, 0:NT * CH // 2].rearrange("p (i c) -> p i c", c=CH)
        perm = c.take((1 + N_SHIFT) * P).rearrange("p (n m) -> p n m", m=P)
        a = Region(mid)
        q_seed = [a.take(A_RUN * CH).rearrange("p (j f) -> p j f", f=CH) for _ in range(2)]
        q_first = [a.take(CH) for _ in range(2)]
        q_fm = a.take(CH * A_RUN)
        q_edge = a.take(CH * A_RUN)
        a_nst = a.take(A_RUN)
        a_go = a.take(A_F * A_RUN)
        a_prod = a.take(CH * A_RUN)
        a_score = a.take(A_HEADS * A_RUN)
        a_msg = a.take(A_F * A_RUN)
        a_sum = a.take(A_F * A_RUN)
        a_rows = [a.take(A_RUN * A_F).rearrange("p (j f) -> p j f", f=A_F) for _ in range(2)]
        a2 = Region(first)
        a_tail = a2.take(A_CHUNKS * A_F).rearrange("p (c f) -> p c f", f=A_F)
        a_tailT = a2.take(A_RUNS)
        a_cont = a2.take(A_RUNS)
        a_carT = a2.take(A_RUNS)
        a_car = a2.take(A_CHUNKS * A_F).rearrange("p (c f) -> p c f", f=A_F)
        a_end = a2.take(NT * A_F).rearrange("p (i f) -> p i f", f=A_F)
        a_before = a2.take(NT * A_F).rearrange("p (i f) -> p i f", f=A_F)
        g = Region(first)
        yT = g.take(NT // 2 * P).rearrange("p (i n) -> p i n", n=P)
        w1 = g.take(4 * HID).rearrange("p (e n) -> p e n", e=4)
        w2 = g.take(4 * CH).rearrange("p (e n) -> p e n", e=4)
        b1 = g.take(4)
        b2 = g.take(4 * CH)
        wgat = g.take(G_HF)
        att = g.take(5 * G_HF).rearrange("p (v n) -> p v n", v=5)
        h_tok = g.take(NT * G_ROW).rearrange("p (i f) -> p i f", f=G_ROW)
        ad_tok = g.take(NT * G_HEADS).rearrange("p (i f) -> p i f", f=G_HEADS)
        h_tile, ad_tile = (x.rearrange("p (i h) f -> p h i f", h=2) for x in (h_tok, ad_tok))
        h_prod = Region(y_at).take(NT * G_HF).rearrange("p (i h k) -> p i h k", h=G_HEADS, k=G_EXP)
        hid = [g.take(512) for _ in range(2)]
        exp_out = g.take(4 * NT * CH).rearrange("p (e i c) -> p e i c", e=4, c=CH)
        exp_tile = exp_out.rearrange("p e (i h) c -> p h i e c", h=2)
        g_mid = g.at
        hs = [g.take(G_RUN * G_ROW).rearrange("p (j f) -> p j f", f=G_ROW) for _ in range(2)]
        ad_seed = [g.take(G_RUN * G_HEADS).rearrange("p (j f) -> p j f", f=G_HEADS) for _ in range(2)]
        g_sidx = [g.take(G_RUN, I32) for _ in range(2)]
        g_didx = [g.take(G_RUN, I32) for _ in range(2)]
        g_fidx = [g.take(4, I32) for _ in range(2)]
        ad_first = [g.take(G_HEADS) for _ in range(2)]
        g_rows = [g.take(G_RUN * G_OUT).rearrange("p (j f) -> p j f", f=G_OUT) for _ in range(2)]
        h_split = [g.take(NT * G_HF // 2, BF16) for _ in range(SPLITS)]
        pick_v = g.take(PICKS, I32)
        pick_t = g.take(PICKS, I32)
        pick_key = [g.take(PICKS // 2, F16) for _ in range(2)]
        pick_of = [g.take(PICKS * CANDS) for _ in range(2)]
        pick_all = [g.take(BATCH * P // 2, F16) for _ in range(2)]
        pick_prod = g.take(BATCH * PICK_W)
        assert g.at <= LIMIT
        HJ = G_HEADS * G_RUN
        g = Region(y_at)
        g_nst = g.take(HJ)
        g_cut = g.take(HJ)
        ad_fm = g.take(HJ)
        ad_edge = g.take(HJ)
        g_x = g.take(HJ)
        g_max = g.take(HJ + 1)
        g_dm = g.take(HJ)
        g_em = g.take(HJ)
        g_msg = g.take(G_F * G_RUN)
        g_corr_f = g.take(G_F * G_RUN)
        g_sum = g.take(G_F * G_RUN)
        assert g.at <= g_key_at + 2 * G_W
        pick_hot = [g.take(K_TILES * BATCH * P // 2, BF16).rearrange("p (t n) -> p t n", t=K_TILES) for _ in range(2)]
        assert g.at <= a_key_at + 2 * A_W
        r_a = Region(y_at)
        g_tailT = r_a.take(G_RUNS)
        g_cutT = r_a.take(G_RUNS)
        assert r_a.at <= g_key_at + 2 * G_W
        gs_ = Region(g_mid)
        g_found = gs_.take(NT * P, I32).rearrange("p (n j) -> p n j", j=P)
        g_below = gs_.take(16 * P).rearrange("p (n j) -> p n j", j=P)
        square = g_below.rearrange("p n j -> p (n j)").rearrange("p (i c) -> p i c", c=CH)
        g2 = Region(g_mid)
        g_tmaxT = g2.take(G_RUNS)
        g_cmaxT = g2.take(G_RUNS + 1)
        g3 = Region(first)
        g_dT = g3.take(G_RUNS)
        g_end = g2.take(NT * G_OUT).rearrange("p (i f) -> p i f", f=G_OUT)
        g_tail = Region(a_key_at).take(G_CHUNKS * (G_OUT + G_F)).rearrange("p (c f) -> p c f", f=G_OUT + G_F)
        rest_h = [Region(x).take(NT * G_HF).rearrange("p (i f) -> p i f", f=G_HF) for x in (a_key_at, g_key_at)]
        g4 = Region(y_at)
        n4 = [g4.take(NT * 4).rearrange("p (i h) -> p i h", h=4) for _ in range(12)]
        n16 = [g4.take(NT * G_HF) for _ in range(3)]
        g_before = g4.take(NT * G_OUT).rearrange("p (i f) -> p i f", f=G_OUT)
        assert g4.at <= g_key_at + 2 * G_W
        out_ch = arena[:, g_mid:g_mid + HALF * PIX].rearrange("p (j s) -> p j s", s=PIX)

        ps = [ctx.enter_context(nc.psum_tensor(f"ps{b}", [P, 512], F32)) for b in range(8)]

        const_in, perm_in, x_in, w_in, a_edges_in, g_edges_in = (
            sem(n) for n in ("const_in", "perm_in", "x_in", "w_in", "a_edges_in", "g_edges_in"))
        g_filled, g_count_set, g_stored = sem("g_filled"), sem("g_count_set"), sem("g_stored")
        zeros_set, qseed_zero, adseed_zero = sem("zeros_set"), sem("qseed_zero"), sem("adseed_zero")
        dve_step, dve_far, dve_loop_g = sem("dve_step"), sem("dve_far"), sem("dve_loop_g")
        waits_carried = sem("waits_carried")
        gn_pair_in, gn_pair = sem("gn_pair_in"), sem("gn_pair")
        gn_ready, gn_root, y_ready = sem("gn_ready"), sem("gn_root"), sem("y_ready")
        w_copied = sem("w_copied")
        border_set, perm_scaled, w_mixed, w_ready = sem("border_set"), sem("perm_scaled"), sem("w_mixed"), sem("w_ready")
        alpha_exp_in, alpha_exp = sem("alpha_exp_in"), sem("alpha_exp")
        conv_done, conv_added, t_turned, t_taken = sem("conv_done"), sem("conv_added"), sem("t_turned"), sem("t_taken")
        flip_in, flip_done, flip_taken = sem("flip_in"), sem("flip_done"), sem("flip_taken")
        a_list_set, a_list_out, g_list_set, g_list_out = (sem(n) for n in ("a_list_set", "a_list_out", "g_list_set", "g_list_out"))
        hot_set, hist_done, hist_set, cum_done, run_set, ends_set, starts_done, pos_set = (
            sem(n) for n in ("hot_set", "hist_done", "hist_set", "cum_done", "run_set",
                             "ends_set", "starts_done", "pos_set"))
        found = [[sem(f"found{k}_{n}") for n in range(4)] for k in range(2)]
        last_set, last_shifted, cont_set, cont_out = sem("last_set"), sem("last_shifted"), sem("cont_set"), sem("cont_out")
        root_in, root_out, y_set, q_out, q_scattered = (sem(n) for n in ("root_in", "root_out", "y_set", "q_out", "q_scattered"))
        far_set, far_scattered, far_found, far_ends_in = (sem(n) for n in ("far_set", "far_scattered", "far_found", "far_ends_in"))
        a_before_in = [sem(f"a_before_in{n}") for n in range(len(A_PIECES))]
        g_before_in = [sem(f"g_before_in{n}") for n in range(len(G_PIECES))]
        ad_seed_in = [sem(f"ad_seed_in{b}") for b in range(2)]
        ad_set = sem("ad_set")
        pick_keys_set, pick_spread, pick_all_set, pick_hot_set, picked, pick_taken, dve_pick, dve_keys, h_split_set = (
            sem(n) for n in ("pick_keys_set", "pick_spread", "pick_all_set", "pick_hot_set", "picked", "pick_taken",
                             "dve_pick", "dve_keys", "h_split_set"))
        a_idx_in = [sem(f"a_idx_in{b}") for b in range(2)]
        a_seed_in = [sem(f"a_seed_in{b}") for b in range(2)]
        kv_in = [sem(f"kv_in{b}") for b in range(2)]
        a_used, a_flags, a_laid, a_scored, a_weighed, a_summed, a_rows_set = (
            sem(n) for n in ("a_used", "a_flags", "a_laid", "a_scored", "a_weighed", "a_summed", "a_rows_set"))
        a_rows_out = [sem(f"a_rows_out{b}") for b in range(2)]
        a_tail_in, a_tail_turned, a_tail_taken, a_carried, a_car_turned, a_car_taken, a_car_out, a_ends_in = (
            sem(n) for n in ("a_tail_in", "a_tail_turned", "a_tail_taken", "a_carried", "a_car_turned", "a_car_taken",
                             "a_car_out", "a_ends_in"))
        gw_in, yT_turned, yT_taken, h_done, h_set, h_out, ad_scattered = (
            sem(n) for n in ("gw_in", "yT_turned", "yT_taken", "h_done", "h_set", "h_out", "ad_scattered"))
        hid_done, hid_set, hid_used, exp_taken = (sem(n) for n in ("hid_done", "hid_set", "hid_used", "exp_taken"))
        g_idx_in = [sem(f"g_idx_in{b}") for b in range(2)]
        hs_in = [sem(f"hs_in{b}") for b in range(2)]
        g_used, g_laid, g_max_set, g_exp_done, g_weighed, g_summed, g_rows_set, g_flags = (
            sem(n) for n in ("g_used", "g_laid", "g_max_set", "g_exp_done", "g_weighed", "g_summed", "g_rows_set", "g_flags"))
        g_rows_out = [sem(f"g_rows_out{b}") for b in range(2)]
        g_tail_in, g_rep_set, g_tail_turned, g_tail_taken, g_dT_set, g_dT_exp, g_carried, g_car_turned, g_car_taken, g_car_out, g_ends_in = (
            sem(n) for n in ("g_tail_in", "g_rep_set", "g_tail_turned", "g_tail_taken", "g_dT_set", "g_dT_exp", "g_carried",
                             "g_car_turned", "g_car_taken", "g_car_out", "g_ends_in"))
        node_exp_in, node_exp, gate_root_in, gate_root, gate_exp_in, gate_exp = (
            sem(n) for n in ("node_exp_in", "node_exp", "gate_root_in", "gate_root", "gate_exp_in", "gate_exp"))
        out_set, out_turned, out_laid, out_stored = sem("out_set"), sem("out_turned"), sem("out_laid"), sem("out_stored")

        HS_FIRST, HS_EACH = 16 * (G_RUN + 1), 16 * (G_RUN - PICKS + 1)
        EXPERTS_FIRST, EXPERTS_EARLY = 10, 14

        block = ctx.enter_context(nc.Block())

        def bc(ap, shape):
            return ap.to_broadcast(shape)

        def chunk_count(it, b, per, n):
            return it * (2 * per) + ((b - 2) * per + n)

        def turn_of(b, m):
            return (b * BATCHES + m) % 2

        @block.sync
        def _(sp):
            sp.dma_start(a_key[1][:, 0:A_EDGES // P].bitcast(I32),
                         io["a_edges"][1].rearrange("(p j) -> p j", p=P)).then_inc(a_edges_in, 16)
            sp.dma_start(a_key[0][:, 0:A_EDGES // P].bitcast(I32),
                         io["a_edges"][0].rearrange("(p j) -> p j", p=P)).then_inc(a_edges_in, 16)
            sp.dma_start(const, io["const"]).then_inc(const_in, 16)
            sp.dma_start(alph[0:CH, 0:5], io["alphas"].partition_broadcast(CH)).then_inc(w_in, 16)
            for half in range(2):
                sp.dma_start(x_ch[half * CH:(half + 1) * CH, :, :],
                             io["x"][half * HALF:(half + 1) * HALF].rearrange("j c s -> c j s")).then_inc(x_in, 16)
            sp.dma_start(perm[0:CH, :, :].rearrange("p n m -> p (n m)"), io["perm"]).then_inc(perm_in, 16)
            sp.dma_start(w_own[0:CH, :], io["w_own"]).then_inc(w_in, 16)
            for n, bs in enumerate(BLOCKS):
                view = w_dup[0:CH, n, :].rearrange("p (q s b) -> p q s b", s=2, b=bs * TAPS)
                for copy in range(2):
                    sp.dma_start(view[:, :, copy, :],
                                 io["w_blocks"][n].rearrange("p (q b) -> p q b", b=bs * TAPS)).then_inc(w_in, 16)
            for n in range(2):
                sp.dma_start(g_key[n].bitcast(I32), io["g_edges"][n].rearrange("(p j) -> p j", p=P)).then_inc(g_edges_in, 16)
            sp.wait_ge(zeros_set, 1)
            zq = d_qseed.rearrange("(p n) f -> p (n f)", p=P)
            per = A_USED // P * CH
            for n in range(0, per, 8192):
                sp.dma_start(zq[:, n:n + 8192].rearrange("p (r z) -> p r z", z=512),
                             bc(zeros[:, None, :], [P, 16, 512])).then_inc(qseed_zero, 16)
            sp.dma_start(d_adseed.rearrange("(p n) f -> p (n f)", p=P).rearrange("p (r z) -> p r z", z=512),
                         bc(zeros[:, None, :], [P, 16, 512])).then_inc(adseed_zero, 16)

            sp.wait_ge(a_list_set, 1)
            for out, src in ((d_asrc, a_key[1 - A_LAST]), (d_adst, a_key[A_LAST]), (d_adstq, list_nodes[:, 0:A_W])):
                sp.dma_start(out.rearrange("(p j) -> p j", p=P), src.bitcast(I32)).then_inc(a_list_out, 16)
            sp.wait_ge(cont_set, 1)
            sp.dma_start(d_acont.rearrange("(p j) -> p j", p=P), run_cont[:, 0:A_W // A_RUN]).then_inc(cont_out, 16)
            src_v = d_asrc.rearrange("(c p j) -> c p j", p=P, j=A_RUN)
            dst_v = d_adst.rearrange("(c p j) -> c p j", p=P, j=A_RUN)
            dstq_v = d_adstq.rearrange("(c p j) -> c p j", p=P, j=A_RUN)
            seed_v = d_qseed.rearrange("(c p j) f -> c p j f", p=P, j=A_RUN)
            out_v = d_as.rearrange("(c p j) f -> c p j f", p=P, j=A_RUN)

            sp.wait_ge(a_list_out, 48)
            for b in range(2):
                sp.dma_start(a_sidx[b], src_v[b]).then_inc(a_idx_in[b], 16)
                sp.dma_start(a_didx[b], dst_v[b]).then_inc(a_idx_in[b], 16)
                sp.dma_start(a_fidx[b], dstq_v[b][:, 0:4]).then_inc(a_idx_in[b], 16)
            sp.wait_ge(y_set, 1)
            for half in range(2):
                sp.dma_start(d_q.rearrange("(h i p) c -> h p i c", p=P, h=2)[half], y_tile[:, half]).then_inc(q_out, 16)
            sp.wait_ge(q_scattered, 16 * A_NEAR)
            sp.wait_ge(far_set, 1)
            n_far = sp.value_load(far_count[0:1, 0:1], min_val=0, max_val=P * A_W)
            with sp.If(n_far >= 1):
                sp.wait_ge(far_scattered, 16 * (NT - A_NEAR))
            for b in range(2):
                sp.dma_start(q_seed[b], seed_v[b]).then_inc(a_seed_in[b], 16)

            with sp.Fori(0, A_CHUNKS // 2 - 1) as it:
                for b in range(2):
                    sp.wait_ge(a_used, it * 2 + (b + 1))
                    sp.wait_ge(a_rows_set, it * 2 + (b + 1))
                    sp.dma_start(out_v[bass.ds(it * 2 + b, 1)].rearrange("c p j f -> (c p) j f"), a_rows[b]).then_inc(a_rows_out[b], 16)
                    nxt = it * 2 + (b + 2)
                    sp.dma_start(a_sidx[b], src_v[bass.ds(nxt, 1)].rearrange("c p j -> (c p) j")).then_inc(a_idx_in[b], 16)
                    sp.dma_start(a_didx[b], dst_v[bass.ds(nxt, 1)].rearrange("c p j -> (c p) j")).then_inc(a_idx_in[b], 16)
                    sp.dma_start(a_fidx[b], dstq_v[bass.ds(nxt, 1), :, 0:4].rearrange("c p j -> (c p) j")).then_inc(a_idx_in[b], 16)
                    sp.dma_start(q_seed[b], seed_v[bass.ds(nxt, 1)].rearrange("c p j f -> (c p) j f")).then_inc(a_seed_in[b], 16)
            for b in range(2):
                sp.wait_ge(a_rows_set, A_CHUNKS - 1 + b)
                sp.dma_start(out_v[A_CHUNKS - 2 + b], a_rows[b]).then_inc(a_rows_out[b], 16)
            for b in range(2):
                sp.wait_ge(a_rows_out[b], 16 * (A_CHUNKS // 2))
            sp.wait_ge(cont_out, 16)
            sp.dma_start(a_tail, d_as.rearrange("(c p j) f -> j p c f", p=P, j=A_RUN)[A_RUN - 1]).then_inc(a_tail_in, 16)
            sp.dma_start(a_cont[0:A_F, :], d_acont[0:A_RUNS].partition_broadcast(A_F)).then_inc(a_tail_in, 16)
            sp.wait_ge(a_car_taken, 5)
            sp.dma_start(d_ac.rearrange("(c p) f -> p c f", p=P), a_car).then_inc(a_car_out, 16)

            sp.wait_ge(g_list_set, 1)
            for out, src in ((d_gsrc, g_key[1 - G_LAST]), (d_gdst, g_key[G_LAST]), (d_gdstq, list_nodes)):
                sp.dma_start(out.rearrange("(p j) -> p j", p=P), src.bitcast(I32)).then_inc(g_list_out, 16)
            sp.wait_ge(cont_set, 2)
            sp.dma_start(d_gcont.rearrange("(p j) -> p j", p=P), run_cont[:, 0:G_W // G_RUN]).then_inc(cont_out, 16)

            sp.wait_ge(a_car_out, 16)
            for half in range(2):
                at = slice(half * CH, (half + 1) * CH)
                sp.dma_start(w1[at], io["w1"].rearrange("e c n -> c e n")).then_inc(gw_in, 16)
                sp.dma_start(wgat[at], io["wgat"]).then_inc(gw_in, 16)
            sp.dma_start(w2, io["w2"].rearrange("e n c -> n e c")).then_inc(gw_in, 16)
            sp.dma_start(b1, io["b1"]).then_inc(gw_in, 16)
            sp.dma_start(b2, io["b2"].rearrange("e c -> (e c)").partition_broadcast(P)).then_inc(gw_in, 16)
            for n, name in enumerate(("att_src", "att_dst", "b_gat", "gamma", "beta")):
                sp.dma_start(att[:, n, :], io[name].partition_broadcast(P)).then_inc(gw_in, 16)

            gsrc_v = d_gsrc.rearrange("(c p j) -> c p j", p=P, j=G_RUN)
            gdst_v = d_gdst.rearrange("(c p j) -> c p j", p=P, j=G_RUN)
            gdstq_v = d_gdstq.rearrange("(c p j) -> c p j", p=P, j=G_RUN)
            gseed_v = d_adseed.rearrange("(c p j) f -> c p j f", p=P, j=G_RUN)
            gout_v = d_gs.rearrange("(c p j) f -> c p j f", p=P, j=G_RUN)
            sp.wait_ge(pos_set, 2)
            for b in range(2):
                sp.dma_start(g_sidx[b], gsrc_v[b]).then_inc(g_idx_in[b], 16)
                sp.dma_start(g_didx[b], gdst_v[b]).then_inc(g_idx_in[b], 16)
                sp.dma_start(g_fidx[b], gdstq_v[b][:, 0:4]).then_inc(g_idx_in[b], 16)
            sp.wait_ge(h_set, 1)
            for half in range(2):
                sp.dma_start(d_h.rearrange("(h i p) f -> h p i f", p=P, h=2)[half], h_tile[:, half]).then_inc(h_out, 16)
            sp.wait_ge(ad_set, 1)
            for half in range(2):
                sp.dma_start(d_ad.rearrange("(h i p) f -> h p i f", p=P, h=2)[half], ad_tile[:, half]).then_inc(h_out, 16)
            sp.wait_ge(ad_scattered, 16 * NT)
            for b in range(2):
                sp.dma_start(ad_seed[b], gseed_v[b]).then_inc(ad_seed_in[b], 16)
            for b in range(2):
                sp.sem_inc(g_rows_out[b], 16)
            sp.wait_ge(g_count_set, 1)
            n_all, n_of = sp.value_load(g_count[0:1, 0:1], min_val=2, max_val=G_CHUNKS), [
                sp.value_load(g_count[0:1, 1 + b:2 + b], min_val=1, max_val=G_CHUNKS // 2) for b in range(2)]
            n_fill = sp.value_load(g_count[0:1, 4:5], min_val=0, max_val=16 * G_CHUNKS)
            flat_v = gout_v.rearrange("c p j f -> c p (j f)").rearrange("c p (r z) -> c p r z", z=512)
            with sp.Fori(2, G_CHUNKS) as it:
                with sp.If(it >= n_all):
                    sp.dma_start(flat_v[bass.ds(it, 1)].rearrange("c p r z -> (c p) r z"),
                                 bc(zeros[:, None, :], [P, G_RUN * G_OUT // 512, 512])).then_inc(g_filled, 16)
            with sp.Fori(1, G_CHUNKS // 2) as it:
                for b in range(2):
                    with sp.If(it * 2 + b < n_all):
                        sp.wait_ge(g_used, it * 2 + (b - 1))
                        sp.wait_ge(g_rows_set, it * 2 + (b - 1))
                        sp.sem_inc(waits_carried, 1)
                        sp.dma_start(gout_v[bass.ds(it * 2 + (b - 2), 1)].rearrange("c p j f -> (c p) j f"), g_rows[b]).then_inc(g_rows_out[b], 16)
                        nxt = it * 2 + b
                        sp.dma_start(g_sidx[b], gsrc_v[bass.ds(nxt, 1)].rearrange("c p j -> (c p) j")).then_inc(g_idx_in[b], 16)
                        sp.dma_start(g_didx[b], gdst_v[bass.ds(nxt, 1)].rearrange("c p j -> (c p) j")).then_inc(g_idx_in[b], 16)
                        sp.dma_start(g_fidx[b], gdstq_v[bass.ds(nxt, 1), :, 0:4].rearrange("c p j -> (c p) j")).then_inc(g_idx_in[b], 16)
                        sp.dma_start(ad_seed[b], gseed_v[bass.ds(nxt, 1)].rearrange("c p j f -> (c p) j f")).then_inc(ad_seed_in[b], 16)
            sp.wait_ge(g_rows_set, n_all)
            sp.sem_inc(waits_carried, 1)
            for b in range(2):
                sp.dma_start(gout_v[bass.ds(n_of[b] * 2 + (b - 2), 1)].rearrange("c p j f -> (c p) j f"), g_rows[b]).then_inc(g_rows_out[b], 16)
            for b in range(2):
                sp.wait_ge(g_rows_out[b], n_of[b] * 16 + 16)
                sp.sem_inc(g_stored, 1)
            with sp.If(n_all < G_CHUNKS):
                sp.wait_ge(g_filled, n_fill)
                sp.sem_inc(waits_carried, 1)
            sp.sem_inc(g_stored, 1)
            sp.wait_ge(cont_out, 32)
            sp.dma_start(g_tail[:, :, 0:G_OUT], d_gs.rearrange("(c p j) f -> j p c f", p=P, j=G_RUN)[G_RUN - 1]).then_inc(g_tail_in, 16)
            sp.dma_start(g_cutT[0:G_F, :], d_gcont.partition_broadcast(G_F)).then_inc(g_tail_in, 16)
            sp.wait_ge(g_car_taken, 2 * G_CHUNKS // 4)
            sp.dma_start(d_gc.rearrange("(c p) f -> p c f", p=P), g_tail[:, :, 0:G_OUT]).then_inc(g_car_out, 16)

            out_dram = io["out"]
            for n in range(4):
                sp.wait_ge(out_laid, 2 * (n + 1))
                for half in range(2):
                    sp.dma_start(out_dram[half * HALF + 4 * n:half * HALF + 4 * n + 4].rearrange("j c s -> c j s"),
                                 out_ch[half * CH:(half + 1) * CH, 4 * n:4 * n + 4, :]).then_inc(out_stored, 16)
            sp.wait_ge(out_stored, 16 * 8)

        @block.gpsimd
        def _(pool):
            pool.memset(zeros, 0.0).then_inc(zeros_set, 1)
            pool.memset(y_pad, 0.0).then_inc(border_set, 1)
            pool.memset(w_taps, 0.0).then_inc(border_set, 1)

            def gather_rows(out, table, index, t):
                return pool.indirect_dma_start(out, None, table, bass.IndirectOffsetOnAxis(index[:, t:t + 1], 0))

            pool.wait_ge(run_set, 1)
            pool.wait_ge(a_list_out, 48)
            a_list_rows = d_adst.rearrange("(n j) -> n j", j=P)
            for t in range(A_NEAR):
                gather_rows(a_found[:, t, :], a_list_rows, a_nodes.run_i, t).then_inc(found[0][t // 16], 16)
            pool.wait_ge(far_set, 1)
            n_far = pool.value_load(far_count[0:1, 0:1], min_val=0, max_val=P * A_W)
            with pool.If(n_far >= 1):
                for t in range(A_NEAR, NT):
                    gather_rows(a_found[:, t, :], a_list_rows, a_nodes.run_i, t).then_inc(far_found, 16)

            def a_gather(b):
                for j in range(A_RUN):
                    gather_rows(kv[b][:, j, :], io["kv"], a_sidx[b], j).then_inc(kv_in[b], 16)

            def a_gather_first(b):
                gather_rows(q_first[b], d_q, a_fidx[b], 0).then_inc(kv_in[b], 16)

            def scatter_q(t):
                return pool.indirect_dma_start(d_qseed, bass.IndirectOffsetOnAxis(a_nodes.seed[:, t:t + 1], 0), y_tok[:, slot(t), :], None,
                                               bounds_check=A_USED - 1, oob_is_err=False)

            pool.wait_ge(a_idx_in[0], 48)
            a_gather(0)
            pool.wait_ge(pos_set, 1)
            pool.wait_ge(y_set, 1)
            pool.wait_ge(qseed_zero, 16 * (A_USED // P * CH // 8192))
            for t in range(A_NEAR):
                scatter_q(t).then_inc(q_scattered, 16)
            with pool.If(n_far >= 1):
                for t in range(A_NEAR, NT):
                    scatter_q(t).then_inc(far_scattered, 16)
            pool.wait_ge(q_out, 32)
            a_gather_first(0)
            pool.wait_ge(a_idx_in[1], 48)
            a_gather(1)
            a_gather_first(1)
            with pool.Fori(1, A_CHUNKS // 2) as it:
                for b in range(2):
                    pool.wait_ge(a_idx_in[b], it * 48 + 48)
                    pool.wait_ge(a_used, it * 2 + (b - 1))
                    pool.sem_inc(waits_carried, 1)
                    a_gather(b)
                    a_gather_first(b)

            for b in range(2):
                pool.wait_ge(a_rows_out[b], 16 * (A_CHUNKS // 2))
            pool.wait_ge(a_used, A_CHUNKS)
            pool.wait_ge(a_rows_set, A_CHUNKS)
            for t in range(A_NEAR):
                gather_rows(a_end[:, t, :], d_as, a_nodes.pos, t).then_inc(a_ends_in, 16)
            pool.wait_ge(a_car_out, 16)
            for n, piece in enumerate(A_PIECES):
                for t in tiles_of(piece, A_NEAR):
                    gather_rows(a_before[:, t, :], d_ac, a_nodes.cidx, t).then_inc(a_before_in[n], 16)
            with pool.If(n_far >= 1):
                for t in range(A_NEAR, NT):
                    gather_rows(a_end[:, t, :], d_as, a_nodes.pos, t).then_inc(far_ends_in, 16)
                    gather_rows(a_before[:, t, :], d_ac, a_nodes.cidx, t).then_inc(far_ends_in, 16)

            g_list_rows = d_gdst.rearrange("(n j) -> n j", j=P)

            def g_search(group):
                for t in range(16 * group, 16 * group + 16):
                    gather_rows(g_found[:, t, :], g_list_rows, g_nodes.run_i, t).then_inc(found[1][group], 16)

            pool.wait_ge(run_set, 2)
            pool.wait_ge(g_list_out, 48)
            for group in range(4):
                g_search(group)
            pool.wait_ge(pos_set, 2)
            pool.wait_ge(ad_set, 1)
            pool.wait_ge(adseed_zero, 16)
            for t in range(NT):
                pool.indirect_dma_start(d_adseed, bass.IndirectOffsetOnAxis(g_nodes.seed[:, t:t + 1], 0), ad_tok[:, slot(t), :], None,
                                        bounds_check=G_EDGES - 1, oob_is_err=False).then_inc(ad_scattered, 16)
            pool.wait_ge(h_out, 64)

            def g_gather(b, n_rows):
                gather_rows(ad_first[b], d_ad, g_fidx[b], 0).then_inc(hs_in[b], 16)
                for j in range(n_rows):
                    gather_rows(hs[b][:, j, :], d_h, g_sidx[b], j).then_inc(hs_in[b], 16)

            for b in range(2):
                pool.wait_ge(g_idx_in[b], 48)
                g_gather(b, G_RUN)
            pool.wait_ge(g_count_set, 1)
            n_all = pool.value_load(g_count[0:1, 0:1], min_val=2, max_val=G_CHUNKS)
            with pool.Fori(1, G_CHUNKS // 2) as it:
                for b in range(2):
                    with pool.If(it * 2 + b < n_all):
                        pool.wait_ge(g_idx_in[b], it * 48 + 48)
                        pool.wait_ge(g_used, it * 2 + (b - 1))
                        pool.sem_inc(waits_carried, 1)
                        g_gather(b, G_RUN - PICKS)
            pool.wait_ge(g_stored, 3)
            for t in range(NT):
                gather_rows(g_end[:, slot(t), :], d_gs, g_nodes.pos, t).then_inc(g_ends_in, 16)
            pool.wait_ge(g_car_out, 16)
            for n, piece in enumerate(G_PIECES):
                for t in tiles_of(piece):
                    gather_rows(g_before[:, slot(t), :], d_gc, g_nodes.cidx, t).then_inc(g_before_in[n], 16)

        @block.tensor
        def _(pe):
            def turn(out, in_, n=P):
                return nc.tensor.transpose(out, in_, ident[0:n, 0:n])

            flips = [0]

            def sort_flips(merge, key):
                banks = key[0].shape[1] // 512 // GROUPS
                for what, src, dst in merge:
                    if what[0] not in ("enter", "group"):
                        continue
                    for g in range(GROUPS) if what[0] == "enter" else what[1:2]:
                        flips[0] += 1
                        pe.wait_ge(flip_in, flips[0])
                        for blk in range(4 * banks * g, 4 * banks * (g + 1)):
                            held = key[1 - (src if what[0] == "enter" else dst)]
                            last = turn(ps[blk // 4][:, blk % 4 * P:(blk % 4 + 1) * P], held[:, blk * P:(blk + 1) * P])
                            if blk % 4 == 3:
                                last.then_inc(flip_done, 1)

            def histogram(nb):
                for n in range(nb):
                    last = nc.tensor.matmul(ps[2][:, 0:NT], hot_lo[:, n, :], hot_hi[:, n, :], start=n == 0, stop=n == nb - 1)
                last.then_inc(hist_done, 1)

            def running(k, nodes):
                pe.wait_ge(hist_set, k)
                nc.tensor.matmul(ps[3][:, 0:NT], triu, nodes.tot, start=True, stop=True)
                nc.tensor.matmul(ps[3][:, 128:128 + NT], ones, nodes.tot, start=True, stop=True).then_inc(cum_done, 1)

            def starts(k, nodes):
                pe.wait_ge(ends_set, k)
                nc.tensor.matmul(ps[3][:, 256:256 + NT + 1], wrap, nodes.end, start=True, stop=False)
                nc.tensor.matmul(ps[3][:, 256:256 + NT], shift, nodes.end[:, 1:NT + 1], start=False, stop=True).then_inc(starts_done, 1)

            def last_of_before(k):
                pe.wait_ge(last_set, k)
                if k == 1:
                    nc.tensor.matmul(ps[2][:, 129:130], ones, ln_sum[:, 1:2], start=True, stop=True)
                nc.tensor.matmul(ps[2][:, 128:129], shift, ln_sum[:, 0:1], start=True, stop=True).then_inc(last_shifted, 1)

            def conv(j):
                if j >= 2:
                    pe.wait_ge(conv_added, j - 1)
                for tap in range(TAPS):
                    dy, dx = tap // 3, tap % 3
                    last = nc.tensor.matmul(ps[4 + j % 2][:, :], w_taps[:, tap, :], y_pad[:, 2 * j:2 * j + 2, dy:dy + SIDE, dx:dx + SIDE],
                                            start=tap == 0, stop=tap == TAPS - 1)
                last.then_inc(conv_done, 1)

            def tokens(j):
                pe.wait_ge(conv_added, j + 1)
                if j >= 2:
                    pe.wait_ge(t_taken, j - 1)
                for n in range(4):
                    last = turn(ps[6 + j % 2][:, n * P:(n + 1) * P], x_ch[:, 2 * j + n // 2, n % 2 * P:(n % 2 + 1) * P])
                last.then_inc(t_turned, 1)

            pe.wait_ge(const_in, 16)
            pe.wait_ge(gn_pair_in, 1)
            nc.tensor.matmul(ps[7][:, 0:HALF], pair, gn_mean, start=True, stop=True).then_inc(gn_pair, 1)
            pe.wait_ge(gn_pair_in, 2)
            nc.tensor.matmul(ps[7][:, 32:32 + HALF], pair, gn_dev, start=True, stop=True).then_inc(gn_pair, 1)
            pe.wait_ge(perm_scaled, 1)
            for part in range(2):
                cols = CH * TAPS // 2
                acc = ps[4 + part][:, 0:cols]
                nc.tensor.matmul(acc, perm[0:CH, 0, :], w_own[0:CH, part * cols:(part + 1) * cols], start=True, stop=False)
                n = 1
                for m, bs in enumerate(BLOCKS):
                    view = w_dup[0:CH, m, :].rearrange("p (q b) -> p q b", b=2 * bs * TAPS)
                    q = CH // bs // 2
                    for k in range(bs):
                        lo = (bs - k) % bs * TAPS
                        last = nc.tensor.matmul(acc, perm[0:CH, n, :], view[:, part * q:(part + 1) * q, lo:lo + bs * TAPS],
                                                start=False, stop=n == N_SHIFT)
                        n += 1
                last.then_inc(w_mixed, 1)
            for k, merge in enumerate(A_MERGES, 1):
                if k == FLIP_FROM:
                    pe.wait_ge(w_ready, 1)
                    pe.wait_ge(y_ready, HALF)
                    conv(0)
                sort_flips(merge, a_key)
                if k >= FLIP_FROM:
                    conv(k - FLIP_FROM + 1)
                    tokens(k - FLIP_FROM)
            last_of_before(1)
            pe.wait_ge(hot_set, 1)
            histogram(A_W // P)
            running(1, a_nodes)
            tokens(HALF // 2 - 1)
            starts(1, a_nodes)
            def a_tails():
                pe.wait_ge(a_tail_in, 32)
                for n in range(A_CHUNKS // 4):
                    if n >= 2:
                        pe.wait_ge(a_tail_taken, n - 1)
                    for c_ in range(4):
                        last = turn(ps[4 + n % 2][0:A_F, c_ * P:(c_ + 1) * P], a_tail[:, 4 * n + c_, :])
                    last.then_inc(a_tail_turned, 1)

            def a_carries():
                pe.wait_ge(a_carried, 1)
                for n in range(A_CHUNKS // 4):
                    if n >= 2:
                        pe.wait_ge(a_car_taken, n - 1)
                    for c_ in range(4):
                        last = turn(ps[6 + n % 2][:, c_ * A_F:(c_ + 1) * A_F], a_carT[0:A_F, (4 * n + c_) * P:(4 * n + c_ + 1) * P], A_F)
                    last.then_inc(a_car_turned, 1)

            for what, arg in SORT_AND_ATTEND:
                if what == "step":
                    sort_flips([arg], g_key)
                elif what == "tails":
                    a_tails()
                elif what == "carries":
                    a_carries()
            last_of_before(2)
            pe.wait_ge(hot_set, 2)
            histogram(G_W // P)
            running(2, g_nodes)

            for n in range(8):
                pe.wait_ge(y_set, 2 + sum(4 * n >= hi for lo, hi in A_PIECES))
                if n >= 2:
                    pe.wait_ge(yT_taken, n - 1)
                for k in range(4):
                    i = 4 * n + k
                    last = turn(ps[n % 2][:, k * P:(k + 1) * P],
                                y_tok[:, 2 * i:2 * i + 2, :].rearrange("p a c -> p (a c)"))
                last.then_inc(yT_turned, 1)
                for lo, hi in A_PIECES:
                    if 4 * n + 4 == hi:
                        pe.wait_ge(gw_in, 16 * 12)
                        pe.wait_ge(yT_taken, n + 1)
                        for i in range(lo, hi):
                            for half in range(2):
                                at = slice(half * CH, (half + 1) * CH)
                                last = nc.tensor.matmul(ps[2 + half][:, i * G_HF:(i + 1) * G_HF], yT[at, i, :], wgat[at], start=True, stop=True)
            last.then_inc(h_done, 1)
            def expert_out(n):
                grp, e = n // 4, n % 4
                if n % 4 == 0 and grp >= 1:
                    pe.wait_ge(exp_taken, grp)
                pe.wait_ge(hid_set, n + 1)
                for k in range(4):
                    last = nc.tensor.matmul(ps[6 + k // 2][:, k % 2 * 256 + e * CH:k % 2 * 256 + (e + 1) * CH],
                                            hid[n % 2][:, k * P:(k + 1) * P], w2[:, e, :], start=True, stop=True)
                last.then_inc(hid_used, 1)

            def experts(lo, hi):
                for n in range(lo, hi):
                    grp, e = n // 4, n % 4
                    half, i0 = grp // 8, grp % 8 * 4
                    at = slice(half * CH, (half + 1) * CH)
                    if n >= 2:
                        pe.wait_ge(hid_set, n - 1)
                    nc.tensor.matmul(ps[4 + n % 2][:, :], w1[at, e, :], yT[at, i0:i0 + 4, :].rearrange("p i n -> p (i n)"),
                                     start=True, stop=True).then_inc(hid_done, 1)
                    if n > lo:
                        expert_out(n - 1)
                expert_out(hi - 1)

            experts(0, 4)
            starts(2, g_nodes)
            experts(4, 4 * EXPERTS_EARLY)

            def spread(it, b, m):
                if m == 0:
                    pe.wait_ge(pick_keys_set, it * 2 + (b - 1))
                pe.wait_ge(pick_all_set, chunk_count(it, b, BATCHES, m + 1))
                for k in range(BATCH):
                    last = nc.tensor.matmul(ps[turn_of(b, m)][:, k * P:(k + 1) * P], bc(pick_key[b][:, BATCH * m + k:BATCH * m + k + 1], [P, P]), ident16,
                                            start=True, stop=True)
                last.then_inc(pick_spread, 1)

            def pick(it, b, m):
                pe.wait_ge(pick_hot_set, chunk_count(it, b, BATCHES, m + 3))
                pe.wait_ge(pick_taken, chunk_count(it, b, BATCHES, m + 1))
                for k in range(BATCH):
                    for t in range(K_TILES):
                        for n in range(SPLITS):
                            last = nc.tensor.matmul(ps[2 + turn_of(b, m)][:, k * PICK_W:(k + 1) * PICK_W], pick_hot[turn_of(b, m)][:, t, k * P:(k + 1) * P],
                                                    h_split[n][:, t * PICK_W:(t + 1) * PICK_W],
                                                    start=t == 0 and n == 0, stop=t == K_TILES - 1 and n == SPLITS - 1)
                last.then_inc(picked, 1)

            pe.wait_ge(h_split_set, 2)
            pe.wait_ge(g_count_set, 1)
            pe.sem_inc(picked, 2)
            n_all = pe.value_load(g_count[0:1, 0:1], min_val=2, max_val=G_CHUNKS)
            with pe.If(n_all >= 3):
                for m in range(2):
                    spread(1, 0, m)
            with pe.Fori(1, G_CHUNKS // 2) as it:
                for b in range(2):
                    with pe.If(it * 2 + b < n_all):
                        for m in range(BATCHES - 2):
                            spread(it, b, m + 2)
                            pick(it, b, m)
                        for m in range(2):
                            pick(it, b, BATCHES - 2 + m)
                            with pe.If(it * 2 + (b + 1) < n_all):
                                spread(it + b, 1 - b, m)

            pe.wait_ge(exp_taken, EXPERTS_EARLY)
            pe.wait_ge(g_rep_set, 1)
            for n in range(G_CHUNKS // 4):
                if n >= 2:
                    pe.wait_ge(g_tail_taken, 2 * n - 2)
                for c_ in range(4):
                    nc_ = 4 * n + c_
                    turn(ps[4 + n % 2 * 2][0:G_F, c_ * P:(c_ + 1) * P], g_tail[:, nc_, 0:G_F])
                    last = turn(ps[5 + n % 2 * 2][0:G_F, c_ * P:(c_ + 1) * P], g_tail[:, nc_, G_OUT:G_OUT + G_F])
                last.then_inc(g_tail_turned, 1)
            pe.wait_ge(g_tail_taken, G_CHUNKS // 2)
            experts(4 * EXPERTS_EARLY, 64)
            pe.wait_ge(exp_taken, 16)
            pe.wait_ge(g_carried, 1)
            for n in range(G_CHUNKS // 4):
                if n >= 2:
                    pe.wait_ge(g_car_taken, 2 * n - 2)
                for c_ in range(4):
                    nc_ = 4 * n + c_
                    turn(ps[4 + n % 2 * 2][:, c_ * G_F:(c_ + 1) * G_F], g_cutT[0:G_F, nc_ * P:(nc_ + 1) * P], G_F)
                    last = turn(ps[5 + n % 2 * 2][:, c_ * G_F:(c_ + 1) * G_F], g_cmaxT[0:G_F, 1 + nc_ * P:1 + (nc_ + 1) * P], G_F)
                last.then_inc(g_car_turned, 1)

            for n in range(8):
                for k, (lo, hi) in enumerate(G_PIECES):
                    if 4 * n == lo:
                        pe.wait_ge(out_set, k + 1)
                if n >= 2:
                    pe.wait_ge(out_laid, n - 1)
                for k in range(4):
                    i = 4 * n + k
                    addends = [t_tok[:, 2 * i:2 * i + 2, :]] + [exp_out[:, e, 2 * i:2 * i + 2, :] for e in range(4)]
                    for m, x in enumerate(addends):
                        last = nc.tensor.matmul(ps[n % 2][:, k * P:(k + 1) * P], x.rearrange("p a c -> p (a c)"), ident,
                                                start=m == 0, stop=m == 4)
                last.then_inc(out_turned, 1)

        @block.scalar
        def _(act):
            act.wait_ge(alpha_exp_in, 1)
            nc.scalar.activation(alph[0:CH, 8:13], alph[0:CH, 0:5], ACT.Exp).then_inc(alpha_exp, 1)
            act.wait_ge(gn_ready, 1)
            nc.scalar.activation(gn_rstd, gn_rstd, ACT.Sqrt).then_inc(gn_root, 1)
            act.wait_ge(gn_ready, 2)
            act.wait_ge(border_set, 1)
            act.wait_ge(x_in, 32)
            for j in range(HALF):
                nc.scalar.activation(y_pad[:, j, 1:1 + SIDE, 1:1 + SIDE], x_ch[:, j, :].rearrange("p (y x) -> p y x", x=SIDE),
                                     ACT.Identity, bias=gn_bias[:, j:j + 1], scale=gn_rstd[:, j:j + 1]).then_inc(y_ready, 1)

            act.wait_ge(w_mixed, 2)
            act.wait_ge(border_set, 2)
            for part in range(2):
                for half in range(2):
                    at = slice(half * CH, (half + 1) * CH)
                    o = half * CH + part * CH // 2
                    last = nc.scalar.copy(w_taps[at, :, o:o + CH // 2], ps[4 + part][at, 0:CH * TAPS // 2].rearrange("p (o t) -> p t o", t=TAPS))
                    if half:
                        last.then_inc(w_copied, 1)
            act.wait_ge(w_copied, 2)
            act.sem_inc(w_ready, 1)

            banks = [0]

            def sort_flips(merge, key):
                per = key[0].shape[1] // 512 // GROUPS
                for what, src, dst in merge:
                    if what[0] not in ("enter", "group"):
                        continue
                    for g in range(GROUPS) if what[0] == "enter" else what[1:2]:
                        for bank in range(per * g, per * (g + 1)):
                            banks[0] += 1
                            act.wait_ge(flip_done, banks[0])
                            nc.scalar.copy(key[dst][:, bank * 512:(bank + 1) * 512], ps[bank][:, :]).then_inc(flip_taken, 1)

            def tokens(j):
                act.wait_ge(t_turned, j + 1)
                nc.scalar.copy(t_tok[:, 8 * j:8 * j + 8, :].rearrange("p i c -> p (i c)"), ps[6 + j % 2][:, :]).then_inc(t_taken, 1)

            for k, merge in enumerate(A_MERGES, 1):
                sort_flips(merge, a_key)
                if k >= FLIP_FROM:
                    tokens(k - FLIP_FROM)
            tokens(HALF // 2 - 1)
            act.wait_ge(root_in, 1)
            nc.scalar.activation(ln_var, ln_var, ACT.Sqrt).then_inc(root_out, 1)

            def lay(c):
                b = c % 2
                act.wait_ge(a_seed_in[b], c // 2 * 16 + 16)
                act.wait_ge(a_flags, c + 1)
                by_f = q_fm.rearrange("p (f j) -> p f j", j=A_RUN)
                nc.scalar.copy(by_f[:, :, 1:], q_seed[b].rearrange("p j f -> p f j")[:, :, 1:])
                nc.scalar.copy(a_go.rearrange("p (f j) -> p f j", j=A_RUN), bc(a_nst[:, None, :], [P, A_F, A_RUN]))
                act.wait_ge(kv_in[b], (c // 2 + 1) * 16 * (A_RUN + 1))
                nc.scalar.copy(by_f[:, :, 0], q_first[b]).then_inc(a_laid, 1)

            def weigh(c):
                act.wait_ge(a_scored, c + 1)
                nc.scalar.activation(a_msg[:, CH * A_RUN:], a_score, ACT.Exp).then_inc(a_weighed, 1)

            def rows(c):
                b = c % 2
                act.wait_ge(a_summed, c + 1)
                if c >= 2:
                    act.wait_ge(a_rows_out[b], c // 2 * 16)
                nc.scalar.copy(a_rows[b].rearrange("p j f -> p f j"), a_sum.rearrange("p (f j) -> p f j", j=A_RUN)).then_inc(a_rows_set, 1)

            def a_tails(_):
                for n in range(A_CHUNKS // 4):
                    act.wait_ge(a_tail_turned, n + 1)
                    nc.scalar.copy(a_tailT[0:A_F, n * 512:(n + 1) * 512], ps[4 + n % 2][0:A_F, :]).then_inc(a_tail_taken, 1)

            def a_carries(_):
                for n in range(A_CHUNKS // 4):
                    act.wait_ge(a_car_turned, n + 1)
                    nc.scalar.copy(a_car[:, 4 * n:4 * n + 4, :].rearrange("p c f -> p (c f)"), ps[6 + n % 2][:, 0:4 * A_F]).then_inc(a_car_taken, 1)

            for what, arg in SORT_AND_ATTEND:
                if what == "step":
                    sort_flips([arg], g_key)
                elif what != "sorted":
                    {"lay": lay, "score": weigh, "sum": rows, "tails": a_tails, "carries": a_carries}[what](arg)

            for n in range(8):
                for k, (lo, hi) in enumerate(A_PIECES):
                    if 4 * n == lo:
                        act.wait_ge(root_in, 2 + k)
                        nc.scalar.activation(ln_var[:, 2 * lo:2 * hi], ln_var[:, 2 * lo:2 * hi], ACT.Sqrt).then_inc(root_out, 1)
                act.wait_ge(yT_turned, n + 1)
                nc.scalar.copy(yT[:, 4 * n:4 * n + 4, :].rearrange("p i n -> p (i n)"), ps[n % 2][:, :]).then_inc(yT_taken, 1)
            act.wait_ge(gw_in, 16 * 12)
            def lay(it, b, back):
                act.wait_ge(ad_seed_in[b], it * 16 + (16 - 16 * back * b))
                act.wait_ge(g_flags, it * 2 + (b - 2 * back * b + 1))
                by_f = ad_fm.rearrange("p (f j) -> p f j", j=G_RUN)
                nc.scalar.copy(by_f[:, :, 1:], ad_seed[b].rearrange("p j f -> p f j")[:, :, 1:])
                act.wait_ge(hs_in[b], it * HS_EACH + (HS_FIRST - HS_EACH * back * b))
                nc.scalar.copy(by_f[:, :, 0], ad_first[b]).then_inc(g_laid, 1)

            def weigh(it, b, back):
                act.wait_ge(g_max_set, it * 2 + (b - 2 * back * b + 1))
                nc.scalar.activation(g_msg[:, G_HF * G_RUN:], g_em, ACT.Exp).then_inc(g_exp_done, 1)
                nc.scalar.activation(g_corr_f[:, G_HF * G_RUN:], g_dm, ACT.Exp).then_inc(g_exp_done, 1)
                act.wait_ge(g_exp_done, it * 4 + (2 * (b - 2 * back * b) + 2))
                nc.scalar.copy(g_corr_f[:, 0:G_HF * G_RUN].rearrange("p (h k j) -> p h k j", h=G_HEADS, j=G_RUN),
                               bc(g_corr_f[:, G_HF * G_RUN:].rearrange("p (h j) -> p h j", j=G_RUN)[:, :, None, :],
                                  [P, G_HEADS, G_EXP, G_RUN])).then_inc(g_weighed, 1)

            def rows(it, b, back):
                act.wait_ge(g_summed, it * 2 + (b - 2 * back * b + 1))
                act.wait_ge(g_rows_out[b], it * 16 + (16 - 16 * back * b))
                rows_f = g_rows[b].rearrange("p j f -> p f j")
                nc.scalar.copy(rows_f[:, 0:G_F], g_sum.rearrange("p (f j) -> p f j", j=G_RUN))
                nc.scalar.copy(rows_f[:, G_F:], g_max[:, 1:].rearrange("p (f j) -> p f j", j=G_RUN)).then_inc(g_rows_set, 1)

            def all_keys(it, b, m):
                act.wait_ge(pick_spread, chunk_count(it, b, BATCHES, m + 1))
                act.wait_ge(pick_hot_set, chunk_count(it, b, BATCHES, m + 1))
                nc.scalar.copy(pick_all[turn_of(b, m)], ps[turn_of(b, m)][:, 0:BATCH * P]).then_inc(pick_all_set, 1)

            def gelu(n):
                act.wait_ge(hid_done, n + 1)
                if n >= 2:
                    act.wait_ge(hid_used, n - 1)
                nc.scalar.activation(hid[n % 2], ps[4 + n % 2][:, :], ACT.Gelu, bias=b1[:, n % 4:n % 4 + 1]).then_inc(hid_set, 1)

            for n in range(4 * EXPERTS_EARLY):
                gelu(n)
                if n == 4 * EXPERTS_FIRST - 1:
                    lay(0, 0, 0)
                    weigh(0, 0, 0)
                    rows(0, 0, 0)
            act.wait_ge(g_count_set, 1)
            n_all = act.value_load(g_count[0:1, 0:1], min_val=2, max_val=G_CHUNKS)
            act.sem_inc(pick_all_set, 2)
            with act.If(n_all >= 3):
                for m in range(2):
                    all_keys(1, 0, m)
            with act.Fori(1, G_CHUNKS // 2 + 1) as it:
                for b in range(2):
                    with act.If(it * 2 + b < n_all):
                        all_keys(it, b, 2)
                        all_keys(it, b, 3)
                        lay(it, 1 - b, 1)
                        all_keys(it, b, 4)
                        weigh(it, 1 - b, 1)
                        all_keys(it, b, 5)
                        rows(it, 1 - b, 1)
                        all_keys(it, b, 6)
                        with act.If(it * 2 + (b + 1) < n_all):
                            for m in range(2):
                                all_keys(it + b, 1 - b, m)
                    with act.If(it * 2 + b == n_all):
                        lay(it, 1 - b, 1)
                        weigh(it, 1 - b, 1)
                        rows(it, 1 - b, 1)

            for n in range(G_CHUNKS // 4):
                act.wait_ge(g_tail_turned, n + 1)
                nc.scalar.copy(g_tailT[0:G_F, n * 512:(n + 1) * 512], ps[4 + n % 2 * 2][0:G_F, :]).then_inc(g_tail_taken, 1)
                nc.scalar.copy(g_tmaxT[0:G_F, n * 512:(n + 1) * 512], ps[5 + n % 2 * 2][0:G_F, :]).then_inc(g_tail_taken, 1)
            for n in range(4 * EXPERTS_EARLY, 64):
                gelu(n)
            for k in range(2):
                act.wait_ge(g_dT_set, k + 1)
                tgt = (g_dT, g_tmaxT)[k]
                nc.scalar.activation(tgt[0:G_F, :], tgt[0:G_F, :], ACT.Exp).then_inc(g_dT_exp, 1)
            for n in range(G_CHUNKS // 4):
                act.wait_ge(g_car_turned, n + 1)
                nc.scalar.copy(g_tail[:, 4 * n:4 * n + 4, 0:G_F],
                               ps[4 + n % 2 * 2][:, 0:4 * G_F].rearrange("p (c f) -> p c f", f=G_F)).then_inc(g_car_taken, 1)
                nc.scalar.copy(g_tail[:, 4 * n:4 * n + 4, G_F:G_OUT],
                               ps[5 + n % 2 * 2][:, 0:4 * G_F].rearrange("p (c f) -> p c f", f=G_F)[:, :, G_HF:]).then_inc(g_car_taken, 1)
            def lay_out(n):
                for k in range(G_PIECES[n][0] // 4, G_PIECES[n][1] // 4):
                    act.wait_ge(out_turned, k + 1)
                    nc.scalar.copy(out_ch[:, 2 * k:2 * k + 2, :].rearrange("p j s -> p (j s)"), ps[k % 2][:, :]).then_inc(out_laid, 1)

            for n, part in FINISH_ORDER:
                at = slice(2 * G_PIECES[n][0], 2 * G_PIECES[n][1])
                if part == 0:
                    act.wait_ge(node_exp_in, n + 1)
                    for k in range(3):
                        nc.scalar.activation(n4[4 + k][:, at], n4[4 + k][:, at], ACT.Exp).then_inc(node_exp, 1)
                elif part == 1:
                    act.wait_ge(gate_root_in, n + 1)
                    nc.scalar.activation(ln_var[:, at], ln_var[:, at], ACT.Sqrt).then_inc(gate_root, 1)
                elif part == 2:
                    act.wait_ge(gate_exp_in, n + 1)
                    nc.scalar.activation(n4[8][:, at], n4[8][:, at], ACT.Exp).then_inc(gate_exp, 1)
                elif n >= 1:
                    lay_out(n - 1)
            lay_out(len(G_PIECES) - 1)

        @block.vector
        def _(dve):
            V = nc.vector
            done = [0]

            def step(ins):
                done[0] += 1
                ins.then_inc(dve_step, 1)
                dve.wait_ge(dve_step, done[0])

            far_done = [0]

            def far_step(ins):
                far_done[0] += 1
                ins.then_inc(dve_far, 1)
                dve.wait_ge(dve_far, far_done[0])

            def tt(o, a_, b_, op):
                return V.tensor_tensor(o, a_, b_, op)

            def ts(o, a_, s1, op0, s2=None, op1=None):
                return V.tensor_scalar(o, a_, s1, s2, op0, op1) if op1 is not None else V.tensor_scalar(o, a_, s1, None, op0)

            step(V.memset(ones, 1.0))
            def norm_means():
                dve.wait_ge(x_in, 32)
                for j in range(HALF):
                    ins = V.bn_stats(gn_stat[:, j, :], x_ch[:, j, :])
                step(ins)
                for j in range(HALF):
                    ins = V.bn_aggr(gn_mv[:, j, :], gn_stat[:, j, :])
                step(ins)
                V.tensor_copy(gn_mean, gn_mv[:, :, 0]).then_inc(gn_pair_in, 1)

            def norm_spread():
                dve.wait_ge(gn_pair, 1)
                step(tt(gn_dev, gn_mv[:, :, 0], ps[7][:, 0:HALF], ALU.subtract))
                step(tt(gn_dev, gn_dev, gn_dev, ALU.mult))
                tt(gn_dev, gn_dev, gn_mv[:, :, 1], ALU.add).then_inc(gn_pair_in, 1)

            def norm_variance():
                dve.wait_ge(gn_pair, 2)
                ts(gn_rstd, ps[7][:, 32:32 + HALF], 1e-5, ALU.add).then_inc(gn_ready, 1)

            def norm_scale():
                dve.wait_ge(gn_root, 1)
                step(V.reciprocal(gn_rstd, gn_rstd))
                V.scalar_tensor_tensor(gn_bias, ps[7][:, 0:HALF], -1.0, gn_rstd, ALU.mult, ALU.mult).then_inc(gn_ready, 1)

            def mix_maximum():
                dve.wait_ge(w_in, 16 * 10)
                al = alph[0:CH]
                step(V.tensor_reduce(al[:, 13:14], al[:, 0:5], AX_X, ALU.max))
                ts(al[:, 0:5], al[:, 0:5], al[:, 13:14], ALU.subtract).then_inc(alpha_exp_in, 1)

            def mix_permutations():
                dve.wait_ge(perm_in, 16)
                dve.wait_ge(alpha_exp, 1)
                al = alph[0:CH]
                step(V.tensor_reduce(al[:, 14:15], al[:, 8:13], AX_X, ALU.add))
                step(V.reciprocal(al[:, 15:16], al[:, 14:15]))
                step(ts(al[:, 0:5], al[:, 8:13], al[:, 15:16], ALU.mult))
                ts(perm[0:CH, 0, :], perm[0:CH, 0, :], al[:, 0:1], ALU.mult)
                n = 1
                for m, bs in enumerate(BLOCKS):
                    ins = ts(perm[0:CH, n:n + bs, :], perm[0:CH, n:n + bs, :], al[:, m + 1:m + 2], ALU.mult, 1.0 / bs, ALU.mult)
                    n += bs
                step(ins)
                dve.sem_inc(perm_scaled, 1)

            flipped = [0, 0]

            def compare(s, d, dist):
                sv = s.rearrange("p (a h d) -> p a h d", h=2, d=dist)
                dv = d.rearrange("p (a h d) -> p a h d", h=2, d=dist)
                tt(dv[:, :, 0], sv[:, :, 0], sv[:, :, 1], ALU.min)
                step(tt(dv[:, :, 1], sv[:, :, 0], sv[:, :, 1], ALU.max))

            def sort(merge, key, filled):
                cols = key[0].shape[1]
                per = cols // GROUPS

                def turned(banks):
                    flipped[0] += banks
                    dve.wait_ge(flip_taken, flipped[0])

                def turn(banks):
                    dve.sem_inc(flip_in, 1)
                    flipped[1] += banks

                for what, src, dst in merge:
                    s, d = key[src], key[dst]
                    if what[0] == "toggle":
                        step(ts(d, s, const[:, C_TOGGLE + what[1]:C_TOGGLE + what[1] + 1], ALU.mult))
                    elif what[0] == "enter":
                        for g in range(GROUPS):
                            at = slice(g * per, (g + 1) * per)
                            step(ts(key[1 - src][:, at], s[:, at], const[:, C_TOGGLE + what[1]:C_TOGGLE + what[1] + 1], ALU.mult))
                            turn(per // 512)
                    elif what[0] == "group":
                        g, cross = what[1:]
                        at = slice(g * per, (g + 1) * per)
                        turned(per // 512)
                        for n in range(cross):
                            compare(key[(src + n) % 2][:, at], key[(src + n + 1) % 2][:, at], 1 << (cross - 1 - n))
                        turn(per // 512)
                    else:
                        if flipped[0] < flipped[1]:
                            turned(flipped[1] - flipped[0])
                        k, dist = what[1:]
                        if k is None:
                            compare(s, d, dist)
                        else:
                            block = 2 << k
                            used = -(-filled // block) * block
                            pat = "p (a s b h d) -> p a s b h d"
                            b_ = (1 << k) // (2 * dist)
                            sv = s[:, 0:used].rearrange(pat, s=2, b=b_, h=2, d=dist)
                            dv = d[:, 0:used].rearrange(pat, s=2, b=b_, h=2, d=dist)
                            for way in range(2):
                                lo, hi = sv[:, :, way, :, 0], sv[:, :, way, :, 1]
                                tt(dv[:, :, way, :, 0], lo, hi, (ALU.min, ALU.max)[way])
                                ins_ = tt(dv[:, :, way, :, 1], lo, hi, (ALU.max, ALU.min)[way])
                            step(ins_)

            def pack(key, cols, n_src):
                s, d = key[0][:, 0:cols].bitcast(I32), key[1][:, 0:cols].bitcast(I32)
                step(ts(s, s, float(n_src - 1), ALU.min, 0.0, ALU.max))
                step(ts(d, d, float(NONE), ALU.min, 0.0, ALU.max))
                step(ts(d, d, SRC_BITS, ALU.logical_shift_left, KEY_BASE, ALU.bitwise_or))
                step(tt(s, s, d, ALU.bitwise_or))

            def unpack(key, last, extra):
                k_, o_ = key[last].bitcast(I32), key[1 - last].bitcast(I32)
                step(ts(o_, k_, (1 << SRC_BITS) - 1, ALU.bitwise_and))
                step(ts(k_, k_, SRC_BITS, ALU.logical_shift_right, (1 << 14) - 1, ALU.bitwise_and))
                return ts(extra, k_, float(TOKENS - 1), ALU.min)

            def runs(key, run, k):
                d_ = key.bitcast(I32)
                n_ = key.shape[1] // run
                head = d_.rearrange("p (n j) -> p n j", j=run)[:, :, 0]
                tail = d_.rearrange("p (n j) -> p n j", j=run)[:, :, run - 1]
                V.tensor_copy(run_prev[:, 1:n_], tail[:, 0:n_ - 1])
                if k == 1:
                    step(ts(far_edge, d_, float(TOKENS), ALU.is_lt))
                    step(V.scalar_tensor_tensor(far_edge, d_, float(A_NEAR * P), far_edge, ALU.is_ge, ALU.mult))
                    step(V.tensor_reduce(ln_sum[:, 1:2], far_edge, AX_X, ALU.add))
                V.tensor_copy(ln_sum[:, 0:1], tail[:, n_ - 1:n_]).then_inc(last_set, 1)
                dve.wait_ge(last_shifted, k)
                if k == 1:
                    step(V.tensor_copy(far_count, ps[2][:, 129:130]))
                    dve.sem_inc(far_set, 1)
                step(V.tensor_copy(run_prev[:, 0:1], ps[2][:, 128:129]))
                step(tt(run_cont[:, 0:n_], head, run_prev[:, 0:n_], ALU.is_equal))
                step(tt(run_prev[:, 0:n_], head, tail, ALU.is_equal))
                step(tt(run_cont[:, 0:n_], run_cont[:, 0:n_], run_prev[:, 0:n_], ALU.mult))
                dve.sem_inc(cont_set, 1)

            def search_rows(key, nodes, k):
                nb = key.shape[1] // P
                p_ = key.bitcast(I32).rearrange("p (n j) -> p n j", j=P)[:, :, 0]
                step(ts(piv[0][:, 0:nb], p_, P - 1, ALU.bitwise_and))
                step(ts(piv[1][:, 0:nb], p_, 7, ALU.logical_shift_right))
                tt(hot_lo[:, 0:nb, :], bc(piv[0][:, 0:nb, None], [P, nb, P]), bc(iota[:, None, :], [P, nb, P]), ALU.is_equal)
                step(tt(hot_hi[:, 0:nb, :], bc(piv[1][:, 0:nb, None], [P, nb, NT]), bc(iota[:, None, 0:NT], [P, nb, NT]), ALU.is_equal))
                dve.sem_inc(hot_set, 1)
                dve.wait_ge(hist_done, k)
                step(V.tensor_copy(nodes.tot, ps[2][:, 0:NT]))
                dve.sem_inc(hist_set, 1)
                dve.wait_ge(cum_done, k)
                step(V.tensor_copy(nodes.count, ps[3][:, 128:128 + NT]))
                step(V.tensor_tensor_scan(nodes.start, ones[:, 0:NT], nodes.count, 0.0, ALU.mult, ALU.add))
                step(tt(nodes.run, nodes.start, nodes.count, ALU.subtract))
                step(tt(nodes.run, nodes.run, ps[3][:, 0:NT], ALU.add))
                step(ts(nodes.run, nodes.run, -1.0, ALU.add, 0.0, ALU.max))
                step(V.tensor_copy(nodes.run_i, nodes.run))
                dve.sem_inc(run_set, 1)

            def search_ends(nodes, k, run, rows, below):
                def count(lo, hi):
                    at = slice(lo, hi)
                    yield tt(below[:, 0:hi - lo], rows[:, at, :], bc(node[:, at, None], [P, hi - lo, P]), ALU.is_le)
                    yield V.tensor_reduce(nodes.count[:, at], below[:, 0:hi - lo], AX_X, ALU.add)

                if k == 1:
                    step(V.memset(nodes.count[:, A_NEAR:], 0.0))
                    for lo in range(0, A_NEAR, 16):
                        hi = min(lo + 16, A_NEAR)
                        dve.wait_ge(found[0][lo // 16], 16 * (hi - lo))
                        for ins in count(lo, hi):
                            step(ins)
                    with dve.If(n_far >= 1):
                        dve.wait_ge(far_found, 16 * (NT - A_NEAR))
                        for lo in range(A_NEAR, NT, 16):
                            for ins in count(lo, min(lo + 16, NT)):
                                far_step(ins)
                else:
                    for n_ in range(4):
                        dve.wait_ge(found[1][n_], 256)
                        for ins in count(16 * n_, 16 * n_ + 16):
                            step(ins)
                V.memset(nodes.end[:, 0:1], 0.0)
                step(V.scalar_tensor_tensor(nodes.end[:, 1:], nodes.run, float(P), nodes.count, ALU.mult, ALU.add))
                dve.sem_inc(ends_set, 1)
                dve.wait_ge(starts_done, k)
                end = nodes.end[:, 1:]
                step(V.tensor_copy(nodes.start, ps[3][:, 256:256 + NT]))
                step(tt(nodes.has, end, nodes.start, ALU.is_gt))
                step(ts(nodes.pos, end, -1.0, ALU.add, 0.0, ALU.max))
                step(ts(nodes.prun, nodes.pos, run.bit_length() - 1, ALU.logical_shift_right))
                step(ts(nodes.cidx_f, nodes.prun, float(run), ALU.mult))
                step(tt(nodes.carried, nodes.start, nodes.cidx_f, ALU.is_lt))
                step(tt(nodes.carried, nodes.carried, nodes.has, ALU.mult))
                step(ts(nodes.cidx, nodes.prun, -1.0, ALU.add, 0.0, ALU.max))
                step(ts(nodes.seed_f, nodes.has, -FAR, ALU.mult, FAR, ALU.add))
                step(tt(nodes.seed, nodes.seed_f, nodes.start, ALU.add))
                dve.sem_inc(pos_set, 1)

            def layer_norm(k, eps, square_, lo, hi):
                t_, y_, sum_, var_ = (x[:, lo:hi] for x in (t_tok, y_tok, ln_sum, ln_var))
                step(V.tensor_reduce(sum_, t_, AX_X, ALU.add))
                step(ts(sum_, sum_, 1.0 / CH, ALU.mult))
                step(tt(y_, t_, bc(sum_[:, :, None], [P, hi - lo, CH]), ALU.subtract))
                for at in range(0, hi - lo, NT // 2):
                    n_ = min(NT // 2, hi - lo - at)
                    step(tt(square_[:, 0:n_], y_[:, at:at + n_], y_[:, at:at + n_], ALU.mult))
                    step(V.tensor_reduce(var_[:, at:at + n_], square_[:, 0:n_], AX_X, ALU.add))
                step(ts(var_, var_, 1.0 / CH, ALU.mult, eps, ALU.add))
                dve.sem_inc(root_in, 1)
                dve.wait_ge(root_out, k)
                step(V.reciprocal(var_, var_))
                step(tt(y_, y_, bc(var_[:, :, None], [P, hi - lo, CH]), ALU.mult))
                dve.sem_inc(y_set, 1)

            def conv_add(j):
                dve.wait_ge(conv_done, j + 1)
                xs = x_ch[:, 2 * j:2 * j + 2, :].rearrange("p j s -> p (j s)")
                tt(xs, xs, ps[4 + j % 2][:, :], ALU.add).then_inc(conv_added, 1)

            dve.wait_ge(a_edges_in, 32)
            pack(a_key, A_EDGES // P, A_NODES)
            for key in a_key:
                ins = V.memset(key[:, A_EDGES // P:].bitcast(I32), PAD_KEY)
            step(ins)
            dve.wait_ge(const_in, 16)
            between = {3: (norm_means, mix_maximum), 4: (norm_spread, mix_permutations), 5: (norm_variance,), 6: (norm_scale,)}
            for k, merge in enumerate(A_MERGES, 1):
                if k >= FLIP_FROM:
                    conv_add(k - FLIP_FROM)
                sort(merge, a_key, A_EDGES // P)
                for part in between.get(k, ()):
                    part()
            step(unpack(a_key, A_LAST, list_nodes[:, 0:A_W]))
            dve.sem_inc(a_list_set, 1)
            runs(a_key[A_LAST], A_RUN, 1)
            search_rows(a_key[A_LAST], a_nodes, 1)
            conv_add(HALF // 2 - 1)
            n_far = dve.value_load(far_count[0:1, 0:1], min_val=0, max_val=P * A_W)
            dve.wait_ge(t_taken, HALF // 2)
            dve.wait_ge(a_list_out, 48)
            layer_norm(1, 1e-5, square_a, 0, NT)
            dve.wait_ge(g_edges_in, 32)
            pack(g_key, G_W, TOKENS)
            search_ends(a_nodes, 1, A_RUN, a_found, a_below)

            def lay(c):
                dve.wait_ge(a_idx_in[c % 2], c // 2 * 48 + 48)
                d_ = a_didx[c % 2]
                tt(a_nst[:, 1:], d_[:, 1:], d_[:, :-1], ALU.is_equal).then_inc(a_flags, 1)

            def score(c):
                dve.wait_ge(a_laid, c + 1)
                step(V.tensor_tensor_scan(q_edge, a_go[:, 0:CH * A_RUN], q_fm, 0.0, ALU.mult, ALU.add))
                k_f = kv[c % 2][:, :, 0:CH].rearrange("p j f -> p f j")
                step(tt(a_prod.rearrange("p (f j) -> p f j", j=A_RUN), q_edge.rearrange("p (f j) -> p f j", j=A_RUN), k_f, ALU.mult))
                step(V.tensor_reduce(a_score.rearrange("p (h j) -> p h j", j=A_RUN),
                                     a_prod.rearrange("p (h d j) -> p h j d", d=A_DIM, j=A_RUN), AX_X, ALU.add))
                step(ts(a_score, a_score, A_DIM ** -0.5, ALU.mult, -5.0, ALU.max))
                ts(a_score, a_score, 5.0, ALU.min).then_inc(a_scored, 1)

            def weighted_sum(c):
                dve.wait_ge(a_weighed, c + 1)
                w = a_msg[:, CH * A_RUN:].rearrange("p (h j) -> p h j", j=A_RUN)
                step(tt(a_msg[:, 0:CH * A_RUN].rearrange("p (h d j) -> p h d j", d=A_DIM, j=A_RUN),
                        kv[c % 2][:, :, CH:].rearrange("p j (h d) -> p h d j", d=A_DIM),
                        bc(w[:, :, None, :], [P, A_HEADS, A_DIM, A_RUN]), ALU.mult))
                dve.sem_inc(a_used, 1)
                if c >= 1:
                    dve.wait_ge(a_rows_set, c)
                step(V.tensor_tensor_scan(a_sum, a_go, a_msg, 0.0, ALU.mult, ALU.add))
                dve.sem_inc(a_summed, 1)

            def a_carries():
                dve.wait_ge(a_tail_taken, A_CHUNKS // 4)
                dve.wait_ge(a_tail_in, 32)
                step(V.tensor_tensor_scan(a_carT[0:A_F], a_cont[0:A_F], a_tailT[0:A_F], 0.0, ALU.mult, ALU.add))
                dve.sem_inc(a_carried, 1)

            step(V.memset(a_nst[:, 0:1], 0.0))
            for what, arg in SORT_AND_ATTEND:
                if what == "step":
                    sort([arg], g_key, G_W)
                elif what == "sorted":
                    step(unpack(g_key, G_LAST, list_nodes))
                    dve.sem_inc(g_list_set, 1)
                    dve.wait_ge(cont_out, 16)
                    runs(g_key[G_LAST], G_RUN, 2)
                    search_rows(g_key[G_LAST], g_nodes, 2)
                elif what == "carries":
                    a_carries()
                elif what != "tails":
                    {"lay": lay, "score": score, "sum": weighted_sum}[what](arg)
            def normalized(lo, hi, step):
                end_, before_ = a_end[:, lo:hi], a_before[:, lo:hi]
                n_ = hi - lo
                tt(before_, before_, bc(a_nodes.carried[:, lo:hi, None], [P, n_, A_F]), ALU.mult)
                step(tt(end_, end_, bc(a_nodes.has[:, lo:hi, None], [P, n_, A_F]), ALU.mult))
                step(tt(end_, end_, before_, ALU.add))
                z = end_[:, :, CH:]
                step(ts(z, z, 1e-6, ALU.add))
                step(V.reciprocal(z, z))
                wv = end_[:, :, 0:CH].rearrange("p i (h d) -> p i h d", d=A_DIM)
                step(tt(wv, wv, bc(z[:, :, :, None], [P, n_, A_HEADS, A_DIM]), ALU.mult))
                half = lo // (NT // 2)
                at = t_tile[:, half, lo - half * NT // 2:hi - half * NT // 2]
                step(tt(at, at, end_[:, :, 0:CH], ALU.add))

            dve.wait_ge(g_list_out, 48)
            dve.wait_ge(a_ends_in, 16 * A_NEAR)
            with dve.If(n_far >= 1):
                dve.wait_ge(far_ends_in, 16 * 2 * (NT - A_NEAR))
                normalized(A_NEAR, NT, far_step)
            for n, (lo, hi) in enumerate(A_PIECES):
                dve.wait_ge(a_before_in[n], 16 * len(tiles_of((lo, hi), A_NEAR)))
                normalized(lo, hi, step)
                if NT // 2 + lo < A_NEAR:
                    normalized(NT // 2 + lo, min(NT // 2 + hi, A_NEAR), step)
                layer_norm(2 + n, 1e-5, square, 2 * lo, 2 * hi)

            dve.wait_ge(gw_in, 16 * 12)
            dve.wait_ge(h_done, 1)
            for half in range(2):
                V_last = V.tensor_copy(h_tile[:, half, :, 0:G_HF], ps[2 + half][:, :].rearrange("p (i f) -> p i f", f=G_HF))
            step(V_last)
            hh = h_tok[:, :, 0:G_HF]
            prod = h_prod.rearrange("p i h k -> p i (h k)")
            step(tt(prod, hh, bc(att[:, 0:1, :], [P, NT, G_HF]), ALU.mult))
            step(V.tensor_reduce(h_tok[:, :, G_HF:], h_prod, AX_X, ALU.add))
            dve.sem_inc(h_set, 1)
            step(tt(prod, hh, bc(att[:, 1:2, :], [P, NT, G_HF]), ALU.mult))
            step(V.tensor_reduce(ad_tok, h_prod, AX_X, ALU.add))
            dve.sem_inc(ad_set, 1)
            search_ends(g_nodes, 2, G_RUN, g_found, g_below)
            cnt = g_count[0:1]
            step(V.tensor_copy(cnt[:, 3:4], ps[3][0:1, 256 + NT:257 + NT]))
            step(ts(cnt[:, 3:4], cnt[:, 3:4], float(P * G_RUN - 1), ALU.add))
            step(ts(cnt[:, 3:4], cnt[:, 3:4], (P * G_RUN).bit_length() - 1, ALU.logical_shift_right))
            step(ts(cnt[:, 0:1], cnt[:, 3:4], 2.0, ALU.max))
            step(ts(cnt[:, 3:4], cnt[:, 0:1], 1.0, ALU.add))
            step(ts(cnt[:, 1:2], cnt[:, 3:4], 1, ALU.logical_shift_right))
            step(ts(cnt[:, 2:3], cnt[:, 0:1], 1, ALU.logical_shift_right))
            step(ts(cnt[:, 4:5], cnt[:, 0:1], -16.0, ALU.mult, 16.0 * G_CHUNKS, ALU.add))
            dve.sem_inc(g_count_set, 1)
            h_all, (r_1, r_2) = h_tok[:, :, 0:G_HF], rest_h
            part_1, part_2, part_3 = (x.rearrange("p (i f) -> p i f", f=G_HF) for x in h_split)
            step(V.tensor_copy(part_1, h_all))
            step(tt(r_1, h_all, part_1, ALU.subtract))
            step(V.tensor_copy(part_2, r_1))
            step(tt(r_2, r_1, part_2, ALU.subtract))
            step(V.tensor_copy(part_3, r_2))
            dve.sem_inc(h_split_set, 1)
            step(V.tensor_copy(ident16, ident))
            dve.sem_inc(h_split_set, 1)

            def expert_group(grp):
                dve.wait_ge(hid_used, 4 * grp + 4)
                i0 = grp % 8 * 4
                for k in range(2):
                    ins = tt(exp_tile[:, grp // 8, i0 + 2 * k:i0 + 2 * k + 2], ps[6 + k][:, :].rearrange("p (i e c) -> p i e c", e=4, c=CH),
                             bc(b2.rearrange("p (e c) -> p e c", c=CH)[:, None], [P, 2, 4, CH]), ALU.add)
                ins.then_inc(exp_taken, 1)

            for grp in range(EXPERTS_FIRST):
                expert_group(grp)

            G_STEPS_DVE, PICK_STEPS, KEY_STEPS = 9, 2 * BATCHES + 2, 8
            V.memset(g_max[:, 0:1], 0.0)
            step(V.memset(g_nst.rearrange("p (h j) -> p h j", j=G_RUN)[:, :, 0:1], 0.0))
            g_done, p_done = [0], [0]

            def link(it, b, back, ins):
                g_done[0] += 1
                ins.then_inc(dve_loop_g, 1)
                dve.wait_ge(dve_loop_g, it * (2 * G_STEPS_DVE) + ((b - 2 * back * b) * G_STEPS_DVE + g_done[0]))

            def flags(it, b, back):
                g_done[0] = 0
                dve.wait_ge(g_idx_in[b], it * 48 + (48 - 48 * back * b))
                n_ = G_RUN - 1
                link(it, b, back, tt(g_nst.rearrange("p (h j) -> p h j", j=G_RUN)[:, :, 1:], bc(g_didx[b][:, None, 1:], [P, G_HEADS, n_]),
                                     bc(g_didx[b][:, None, :-1], [P, G_HEADS, n_]), ALU.is_equal))
                ts(g_cut, g_nst, BIG, ALU.mult, -BIG, ALU.add).then_inc(g_flags, 1)

            def maximum(it, b, back, first=False):
                c1 = it * 2 + (b - 2 * back * b + 1)
                dve.wait_ge(g_laid, c1)
                link(it, b, back, V.tensor_tensor_scan(ad_edge, g_nst, ad_fm, 0.0, ALU.mult, ALU.add))
                hs_f = hs[b].rearrange("p j f -> p f j")
                link(it, b, back, tt(g_x.rearrange("p (h j) -> p h j", j=G_RUN), ad_edge.rearrange("p (h j) -> p h j", j=G_RUN), hs_f[:, G_HF:], ALU.add))
                link(it, b, back, V.scalar_tensor_tensor(g_x, g_x, 0.2, g_x, ALU.mult, ALU.max))
                if not first:
                    dve.wait_ge(g_rows_set, it * 2 + (b - 2 * back * b))
                link(it, b, back, V.tensor_tensor_scan(g_max[:, 1:], g_cut, g_x, 0.0, ALU.add, ALU.max))
                tt(g_em, g_x, g_max[:, 1:], ALU.subtract)
                link(it, b, back, tt(g_dm, g_max[:, :-1], g_max[:, 1:], ALU.subtract))
                link(it, b, back, tt(g_dm, g_dm, g_cut, ALU.add))
                dve.sem_inc(g_max_set, 1)

            def weighted_sums(it, b, back):
                dve.wait_ge(g_weighed, it * 2 + (b - 2 * back * b + 1))
                w = g_msg[:, G_HF * G_RUN:].rearrange("p (h j) -> p h j", j=G_RUN)
                link(it, b, back, tt(g_msg[:, 0:G_HF * G_RUN].rearrange("p (h k j) -> p h k j", k=G_EXP, j=G_RUN),
                                     hs[b][:, :, 0:G_HF].rearrange("p j (h k) -> p h k j", k=G_EXP),
                                     bc(w[:, :, None, :], [P, G_HEADS, G_EXP, G_RUN]), ALU.mult))
                dve.sem_inc(g_used, 1)
                link(it, b, back, V.tensor_tensor_scan(g_sum, g_corr_f, g_msg, 0.0, ALU.mult, ALU.add))
                dve.sem_inc(g_summed, 1)
                assert g_done[0] == G_STEPS_DVE

            def pick_link(it, b, ins):
                p_done[0] += 1
                ins.then_inc(dve_pick, 1)
                dve.wait_ge(dve_pick, chunk_count(it, b, PICK_STEPS, p_done[0]))

            def pick_keys(it, b):
                n_done = [0]

                def key_link(ins):
                    n_done[0] += 1
                    ins.then_inc(dve_keys, 1)
                    dve.wait_ge(dve_keys, chunk_count(it, b, KEY_STEPS, n_done[0]))

                dve.wait_ge(g_idx_in[b], it * 48 + 48)
                src = g_sidx[b][:, G_RUN - PICKS:]
                of_ = pick_of[b].rearrange("p (j k) -> p j k", k=CANDS)
                key_link(ts(pick_t, src, 2, ALU.logical_shift_right, (K_TILES - 1) * P, ALU.bitwise_and))
                key_link(ts(pick_v, src, P - 1, ALU.bitwise_and))
                key_link(tt(pick_v, pick_v, pick_t, ALU.bitwise_or))
                key_link(V.tensor_copy(pick_key[b], pick_v))
                dve.sem_inc(pick_keys_set, 1)
                key_link(ts(pick_t, src, 6, ALU.logical_shift_right, CANDS - 2, ALU.bitwise_and))
                key_link(ts(pick_v, src, SRC_BITS - 1, ALU.logical_shift_right))
                key_link(tt(pick_v, pick_v, pick_t, ALU.bitwise_or))
                key_link(tt(of_, bc(pick_v[:, :, None], [P, PICKS, CANDS]), bc(iota[:, None, 0:CANDS], [P, PICKS, CANDS]), ALU.is_equal))
                assert n_done[0] == KEY_STEPS

            def one_hot(it, b, m):
                dve.wait_ge(pick_all_set, chunk_count(it, b, BATCHES, m + 3))
                dve.wait_ge(picked, chunk_count(it, b, BATCHES, m + 1))
                for t in range(K_TILES):
                    ins = ts(pick_hot[turn_of(b, m)][:, t], pick_all[turn_of(b, m)], node[:, t:t + 1], ALU.is_equal)
                ins.then_inc(pick_hot_set, 1)

            def take_picked(it, b, m):
                dve.wait_ge(picked, chunk_count(it, b, BATCHES, m + 3))
                at = slice(m * BATCH, (m + 1) * BATCH)
                prod_ = pick_prod.rearrange("p (j k f) -> p j k f", k=CANDS, f=G_HF)
                pick_link(it, b, tt(prod_, ps[2 + turn_of(b, m)][:, 0:BATCH * PICK_W].rearrange("p (j k f) -> p j k f", k=CANDS, f=G_HF),
                                    bc(pick_of[b].rearrange("p (j k) -> p j k", k=CANDS)[:, at, :, None], [P, BATCH, CANDS, G_HF]), ALU.mult))
                dve.sem_inc(pick_taken, 1)
                lo = G_RUN - PICKS + m * BATCH
                pick_link(it, b, V.tensor_reduce(hs[b][:, lo:lo + BATCH, 0:G_HF], prod_.rearrange("p j k f -> p j f k"), AX_X, ALU.add))

            def picked_a_src(it, b):
                rows_ = hs[b][:, G_RUN - PICKS:]
                prod_ = pick_prod[:, 0:PICKS * G_HF]
                pick_link(it, b, tt(prod_.rearrange("p (j f) -> p j f", f=G_HF), rows_[:, :, 0:G_HF], bc(att[:, 0:1, :], [P, PICKS, G_HF]), ALU.mult))
                pick_link(it, b, V.tensor_reduce(rows_[:, :, G_HF:], prod_.rearrange("p (j h k) -> p j h k", h=G_HEADS, k=G_EXP), AX_X, ALU.add))

            flags(0, 0, 0)
            maximum(0, 0, 0, True)
            weighted_sums(0, 0, 0)
            for grp in range(EXPERTS_FIRST, EXPERTS_EARLY):
                expert_group(grp)
            n_all = dve.value_load(g_count[0:1, 0:1], min_val=2, max_val=G_CHUNKS)
            dve.sem_inc(pick_hot_set, 2)
            dve.sem_inc(pick_taken, 2)
            with dve.If(n_all >= 3):
                pick_keys(1, 0)
                one_hot(1, 0, 0)
                one_hot(1, 0, 1)
            with dve.Fori(1, G_CHUNKS // 2 + 1) as it:
                for b in range(2):
                    with dve.If(it * 2 + b < n_all):
                        p_done[0] = 0
                        flags(it, 1 - b, 1)
                        for m in range(BATCHES - 2):
                            one_hot(it, b, m + 2)
                            take_picked(it, b, m)
                            if m == 1:
                                maximum(it, 1 - b, 1)
                            if m == 2:
                                weighted_sums(it, 1 - b, 1)
                        for m in range(2):
                            dve.sem_inc(waits_carried, 1)
                            with dve.If(it * 2 + (b + 1) < n_all):
                                if m == 0:
                                    pick_keys(it + b, 1 - b)
                                one_hot(it + b, 1 - b, m)
                            take_picked(it, b, BATCHES - 2 + m)
                        picked_a_src(it, b)
                        dve.sem_inc(waits_carried, 1)
                        assert p_done[0] == PICK_STEPS
                    with dve.If(it * 2 + b == n_all):
                        flags(it, 1 - b, 1)
                        maximum(it, 1 - b, 1)
                        weighted_sums(it, 1 - b, 1)

            dve.wait_ge(g_tail_in, 32)
            m_tail = g_tail[:, :, G_F:G_OUT]
            V.tensor_copy(g_tail[:, :, G_OUT:G_OUT + G_HF].rearrange("p c (h k) -> p c h k", k=G_EXP),
                          bc(m_tail[:, :, :, None], [P, G_CHUNKS, G_HEADS, G_EXP]))
            step(V.tensor_copy(g_tail[:, :, G_OUT + G_HF:], m_tail))
            dve.sem_inc(g_rep_set, 1)
            cut, tmax, cmax, d_t, tail = (x[0:G_F] for x in (g_cutT, g_tmaxT, g_cmaxT, g_dT, g_tailT))
            step(ts(cut, cut, BIG, ALU.mult, -BIG, ALU.add))
            dve.wait_ge(g_tail_taken, G_CHUNKS // 2)
            V.memset(cmax[:, 0:1], -BIG)
            step(V.tensor_tensor_scan(cmax[:, 1:], cut, tmax, -BIG, ALU.add, ALU.max))
            step(tt(d_t, cmax[:, :-1], cmax[:, 1:], ALU.subtract))
            step(tt(d_t, d_t, cut, ALU.add))
            dve.sem_inc(g_dT_set, 1)
            step(tt(tmax, tmax, cmax[:, 1:], ALU.subtract))
            dve.sem_inc(g_dT_set, 1)
            for grp in range(EXPERTS_EARLY, 16):
                expert_group(grp)
            dve.wait_ge(g_dT_exp, 2)
            step(tt(tail, tail, tmax, ALU.mult))
            step(V.tensor_tensor_scan(cut, d_t, tail, 0.0, ALU.mult, ALU.add))
            dve.sem_inc(g_carried, 1)

            def finish(n, lo, hi):
                N = hi - lo
                m_end, m_before, e_own, m_all, w_end, w_before, w_own_, sc, ex, rank, cmp_, den = (x[:, lo:hi] for x in n4)
                end_, before_, h_, ad_ = (x[:, lo:hi] for x in (g_end, g_before, h_tok, ad_tok))
                sum_, var_ = ln_sum[:, lo:hi], ln_var[:, lo:hi]
                flat, sq = (x.rearrange("p (i f) -> p i f", f=G_HF)[:, lo:hi] for x in n16[0:2])
                agg, part = (x.rearrange("p i (h k) -> p i h k", k=4) for x in (flat, sq))

                def of_slots(table):
                    return bc(table.rearrange("p (h i) -> p i h", h=2)[:, lo // 2:hi // 2, :, None], [P, N // 2, 2, 4])

                def pairs(x):
                    return x.rearrange("p (i h) f -> p i h f", h=2)

                step(tt(den, h_[:, :, G_HF:], ad_, ALU.add))
                step(V.scalar_tensor_tensor(e_own, den, 0.2, den, ALU.mult, ALU.max))
                dve.wait_ge(g_ends_in, 16 * NT)
                dve.wait_ge(g_before_in[n], 16 * N)
                for m_, rows_, on, off in ((m_end, end_, g_nodes.has, g_nodes.tot), (m_before, before_, g_nodes.carried, g_nodes.seed_f)):
                    step(tt(pairs(m_), pairs(rows_[:, :, G_F:]), of_slots(on), ALU.mult))
                    step(tt(pairs(m_), pairs(m_), of_slots(off), ALU.add))
                step(tt(m_all, m_end, m_before, ALU.max))
                step(tt(m_all, m_all, e_own, ALU.max))
                for w_, m_ in ((w_end, m_end), (w_before, m_before), (w_own_, e_own)):
                    ins = tt(w_, m_, m_all, ALU.subtract)
                step(ins)
                dve.sem_inc(node_exp_in, 1)
                yield
                dve.wait_ge(node_exp, 3 * n + 3)

                def heads(x):
                    return x.rearrange("p i (h k) -> p i h k", k=4)

                def per_head(x):
                    return bc(x[:, :, :, None], [P, N, 4, 4])

                step(tt(agg, heads(end_[:, :, 0:G_HF]), per_head(w_end), ALU.mult))
                step(tt(part, heads(before_[:, :, 0:G_HF]), per_head(w_before), ALU.mult))
                step(tt(flat, flat, sq, ALU.add))
                step(tt(part, heads(h_[:, :, 0:G_HF]), per_head(w_own_), ALU.mult))
                step(tt(flat, flat, sq, ALU.add))
                step(tt(den, end_[:, :, G_HF:G_F], w_end, ALU.mult))
                step(tt(cmp_, before_[:, :, G_HF:G_F], w_before, ALU.mult))
                step(tt(den, den, cmp_, ALU.add))
                step(V.scalar_tensor_tensor(den, w_own_, 1e-16, den, ALU.add, ALU.add))
                step(V.reciprocal(den, den))
                step(tt(agg, agg, per_head(den), ALU.mult))

                def all_nodes(v):
                    return bc(att[:, v:v + 1, :], [P, N, G_HF])

                step(tt(flat, flat, all_nodes(2), ALU.add))
                step(V.tensor_reduce(sum_, flat, AX_X, ALU.add))
                step(ts(sum_, sum_, 1.0 / G_HF, ALU.mult))
                step(tt(flat, flat, bc(sum_[:, :, None], [P, N, G_HF]), ALU.subtract))
                step(tt(sq, flat, flat, ALU.mult))
                step(V.tensor_reduce(var_, sq, AX_X, ALU.add))
                step(ts(var_, var_, 1.0 / G_HF, ALU.mult, 1e-5, ALU.add))
                dve.sem_inc(gate_root_in, 1)
                yield
                dve.wait_ge(gate_root, n + 1)
                step(V.reciprocal(var_, var_))
                step(tt(flat, flat, bc(var_[:, :, None], [P, N, G_HF]), ALU.mult))
                step(tt(flat, flat, all_nodes(3), ALU.mult))
                step(tt(flat, flat, all_nodes(4), ALU.add))
                step(V.tensor_reduce(sc, flat.rearrange("p i (h k) -> p i k h", k=4), AX_X, ALU.add))
                step(ts(sc, sc, 1.0 / G_HEADS, ALU.mult))
                step(V.memset(rank, 0.0))
                for j in range(4):
                    if j < 3:
                        tt(cmp_[:, :, j + 1:], bc(sc[:, :, j:j + 1], [P, N, 3 - j]), sc[:, :, j + 1:], ALU.is_ge)
                    step(tt(cmp_[:, :, 0:j + 1], bc(sc[:, :, j:j + 1], [P, N, j + 1]), sc[:, :, 0:j + 1], ALU.is_gt))
                    step(tt(rank, rank, cmp_, ALU.add))
                step(V.tensor_reduce(sum_, sc, AX_X, ALU.max))
                step(tt(ex, sc, bc(sum_[:, :, None], [P, N, 4]), ALU.subtract))
                dve.sem_inc(gate_exp_in, 1)
                yield
                dve.wait_ge(gate_exp, n + 1)
                step(V.scalar_tensor_tensor(ex, rank, 2.0, ex, ALU.is_lt, ALU.mult))
                step(V.tensor_reduce(sum_, ex, AX_X, ALU.add))
                step(V.reciprocal(sum_, sum_))
                step(tt(ex, ex, bc(sum_[:, :, None], [P, N, 4]), ALU.mult))
                eo = exp_out[:, :, lo:hi]
                step(tt(eo, eo, bc(ex.rearrange("p i e -> p e i")[:, :, :, None], [P, 4, N, CH]), ALU.mult))
                dve.sem_inc(out_set, 1)
                yield

            step(ts(g_nodes.tot, g_nodes.has, BIG, ALU.mult, -BIG, ALU.add))
            step(ts(g_nodes.seed_f, g_nodes.carried, BIG, ALU.mult, -BIG, ALU.add))
            parts = [finish(n, 2 * lo, 2 * hi) for n, (lo, hi) in enumerate(G_PIECES)]
            for n, _ in FINISH_ORDER:
                next(parts[n])


OUT_SHAPE = (IMAGES, CH, SIDE, SIDE)


def kernel(debug=None, **inputs):
    import concourse.bacc as bacc
    from concourse.bass_utils import run_bass_kernel_spmd

    def given(name, shape=None):
        a = np.ascontiguousarray(inputs[name])
        return a.reshape(shape) if shape else a

    w = given("L0_conv_weight", (CH, CH, TAPS))
    const, perm = shape_constants()
    arrays = {
        "x": given("x", (IMAGES, CH, PIX)),
        "alphas": given("L0_conv_alphas"),
        "w_own": np.ascontiguousarray(w.transpose(1, 0, 2)).reshape(CH, CH * TAPS),
        "w_blocks": np.stack([np.ascontiguousarray(
            w.reshape(CH // bs, bs, CH // bs, bs, TAPS).transpose(2, 1, 0, 3, 4)).reshape(CH, CH * TAPS) for bs in BLOCKS]),
        "kv": np.concatenate([given("L1_attn_k", (A_NODES, CH)), given("L1_attn_v", (A_NODES, CH))], axis=1),
        "a_edges": given("L1_attn_edge_index"),
        "g_edges": given("L1_ffn_edge_index"),
        "wgat": given("L1_ffn_W_gat"), "att_src": given("L1_ffn_att_src", (G_HF,)), "att_dst": given("L1_ffn_att_dst", (G_HF,)),
        "b_gat": given("L1_ffn_b_gat"), "gamma": given("L1_ffn_ln_gamma"), "beta": given("L1_ffn_ln_beta"),
        "w1": given("L1_ffn_W1"), "b1": np.ascontiguousarray(given("L1_ffn_b1").T), "w2": given("L1_ffn_W2"), "b2": given("L1_ffn_b2"),
        "const": const, "perm": perm,
    }
    nc = bacc.Bacc("TRN2", target_bir_lowering=False, num_devices=1)
    io = {n: nc.dram_tensor(f"in_{n}", a.shape, mybir.dt.from_np(a.dtype), kind="ExternalInput").ap() for n, a in arrays.items()}
    io["out"] = nc.dram_tensor("out", (IMAGES, CH, PIX), F32, kind="ExternalOutput").ap()
    build(nc, io, debug)
    r = run_bass_kernel_spmd(nc, [{f"in_{n}": a for n, a in arrays.items()}], core_ids=[0])
    return r.results[0]["out"].reshape(OUT_SHAPE)
```
